# Optimizing a Trainium2 kernel written in Bass

```python
import numpy as np
import jax
import jax.numpy as jnp

def _softmax(x, axis=-1):
    return jax.nn.softmax(x, axis=axis)

def _gelu(x):
    return jax.nn.gelu(x, approximate=True)

def _silu(x):
    return jax.nn.silu(x)

def _sigmoid(x):
    return jax.nn.sigmoid(x)

def _layernorm(x, axis=-1, eps=1e-05):
    m = jnp.mean(x, axis=axis, keepdims=True)
    v = jnp.var(x, axis=axis, keepdims=True)
    return (x - m) / jnp.sqrt(v + eps)

def _scatter_add(tgt, idx, src, axis=0):
    return tgt.at[idx].add(src)

def _segment_sum(src, seg, n):
    return jax.ops.segment_sum(src, seg, n)
kernel_name = 'mk_decoder_preln_d1_seqx_r8_69b54c'

def setup_inputs(seed: int=0):
    np.random.seed(seed)
    _w = jnp.asarray

    def _rec_inputs():
        import jax
        import jax.numpy as jnp
        _rk = jax.random.key(seed)
        x = -0.0002928 + 1 * jax.random.normal(jax.random.fold_in(_rk, 1), (16, 128, 128), jnp.float32)
        _lenS = 128 - jax.random.randint(jax.random.fold_in(_rk, 7), (16,), 0, max(1, 128 // 4) + 1, jnp.int32)
        _lenS2 = 120 - jax.random.randint(jax.random.fold_in(_rk, 8), (16,), 0, max(1, 120 // 4) + 1, jnp.int32)
        _ctx_1024P = jax.random.normal(jax.random.fold_in(_rk, 11), (16, 16, 128), jnp.float32)
        _ctx_1024c = jax.random.dirichlet(jax.random.fold_in(_rk, 511), 0.3 * jnp.ones((16,), jnp.float32), (16, 120))
        _ctx_1024t = jnp.einsum('bsk,bkd->bsd', _ctx_1024c, _ctx_1024P)
        _ctx_1024t = _ctx_1024t * jax.lax.rsqrt(jnp.mean(jnp.square(_ctx_1024t)) + 1e-12) * 0.953939
        ctx_1024 = -1.39393e-06 + 0.999914 * (_ctx_1024t + 0.3 * jax.random.normal(jax.random.fold_in(_rk, 611), (16, 120, 128), jnp.float32))
        return (x, ctx_1024)
    x, ctx_1024 = _rec_inputs()

    def _L0_attn_setup():
        import jax, jax.numpy as jnp
        import numpy as np
        NUM_HEADS = 4
        CHUNK = 64
        GATE_NORM = 16.0
        EPS = 1e-05

        def _xavier(key, fan_in, fan_out):
            gain = 2.0 ** (-2.5)
            limit = gain * np.sqrt(6.0 / (fan_in + fan_out))
            return jax.random.uniform(key, (fan_in, fan_out), jnp.float32, -limit, limit)

        def _to_chunks(t, B, H, NC, C):
            d = t.shape[-1]
            return t.reshape(B, H, NC, C, d).transpose(2, 0, 1, 3, 4)

        def _gla_forward(x, Wq, Wk, Wv, Wg, gk_w1, gk_w2, gk_b2, g_norm_w, Wo):
            B, L, D = x.shape
            H = NUM_HEADS
            C = CHUNK
            NC = L // C
            q = x @ Wq
            k = x @ Wk
            v = x @ Wv
            gk = jax.nn.log_sigmoid(x @ gk_w1 @ gk_w2 + gk_b2) / GATE_NORM

            def split_heads(t):
                return t.reshape(B, L, H, -1).transpose(0, 2, 1, 3)
            q, k, v, gk = map(split_heads, (q, k, v, gk))
            dk = q.shape[-1]
            scale = dk ** (-0.5)
            qc = _to_chunks(q, B, H, NC, C)
            kc = _to_chunks(k, B, H, NC, C)
            vc = _to_chunks(v, B, H, NC, C)
            gc = _to_chunks(gk, B, H, NC, C)
            Bcum = jnp.cumsum(gc, axis=3)
            causal = jnp.tril(jnp.ones((C, C), jnp.float32))

            def step(Hst, inp):
                qi, ki, vi, bi = inp
                qg = qi * jnp.exp(bi) * scale
                kg = ki * jnp.exp(-bi)
                o_inter = jnp.einsum('bhcd,bhde->bhce', qg, Hst)
                A = jnp.einsum('bhtd,bhsd->bhts', qg, kg) * causal
                o_intra = jnp.einsum('bhts,bhse->bhte', A, vi)
                b_last = bi[:, :, -1:, :]
                kH = ki * jnp.exp(b_last - bi)
                H_new = jnp.exp(b_last).transpose(0, 1, 3, 2) * Hst + jnp.einsum('bhcd,bhce->bhde', kH, vi)
                return (H_new, o_inter + o_intra)
            dv = v.shape[-1]
            H0 = jnp.zeros((B, H, dk, dv), jnp.float32)
            _, oc = jax.lax.scan(step, H0, (qc, kc, vc, Bcum))
            o = oc.transpose(1, 2, 0, 3, 4).reshape(B, H, L, dv)
            o = o.transpose(0, 2, 1, 3)
            rms = jnp.sqrt(jnp.mean(o * o, axis=-1, keepdims=True) + EPS)
            o_n = o / rms * g_norm_w
            g = (x @ Wg).reshape(B, L, H, dv)
            o = o_n * g * jax.nn.sigmoid(g)
            return o.reshape(B, L, H * dv) @ Wo
        key = jax.random.key(seed)
        ks = jax.random.split(key, 8)
        B, L, D = (4, 256, 128)
        Dk, Dv, R = (128, 256, 16)
        x = jax.random.normal(ks[0], (B, L, D), jnp.float32)
        return {'x': x, 'Wq': _xavier(ks[1], D, Dk), 'Wk': _xavier(ks[2], D, Dk), 'Wv': _xavier(ks[3], D, Dv), 'Wg': _xavier(ks[4], D, Dv), 'gk_w1': _xavier(ks[5], D, R), 'gk_w2': _xavier(ks[6], R, Dk), 'gk_b2': jnp.zeros((Dk,), jnp.float32), 'g_norm_w': jnp.ones((Dv // NUM_HEADS,), jnp.float32), 'Wo': _xavier(ks[7], Dv, D)}
    _L0_attn_all = _L0_attn_setup()
    _L0_attn_in = {k: v for k, v in _L0_attn_all.items() if k in ('Wq', 'Wk', 'Wv', 'Wg', 'gk_w1', 'gk_w2', 'gk_b2', 'g_norm_w', 'Wo')}
    del _L0_attn_all

    def _L0_xattn_setup():
        import jax, jax.numpy as jnp
        import numpy as np
        D_MODEL = 128
        NUM_HEADS = 16
        DEPTH = D_MODEL // NUM_HEADS

        def _split_heads(x, B):
            return x.reshape(B, -1, NUM_HEADS, DEPTH).transpose(0, 2, 1, 3)
        key = jax.random.key(seed)
        ks = jax.random.split(key, 11)
        B, S = (2, 256)
        s = 1.0 / np.sqrt(D_MODEL)
        return {'q': jax.random.normal(ks[0], (B, S, D_MODEL), jnp.float32), 'k': jax.random.normal(ks[1], (B, S, D_MODEL), jnp.float32), 'v': jax.random.normal(ks[2], (B, S, D_MODEL), jnp.float32), 'wq': jax.random.normal(ks[3], (D_MODEL, D_MODEL), jnp.float32) * s, 'bq': jax.random.normal(ks[4], (D_MODEL,), jnp.float32) * s, 'wk': jax.random.normal(ks[5], (D_MODEL, D_MODEL), jnp.float32) * s, 'bk': jax.random.normal(ks[6], (D_MODEL,), jnp.float32) * s, 'wv': jax.random.normal(ks[7], (D_MODEL, D_MODEL), jnp.float32) * s, 'bv': jax.random.normal(ks[8], (D_MODEL,), jnp.float32) * s, 'wo': jax.random.normal(ks[9], (D_MODEL, D_MODEL), jnp.float32) * s, 'bo': jax.random.normal(ks[10], (D_MODEL,), jnp.float32) * s}
    _L0_xattn_all = _L0_xattn_setup()
    _L0_xattn_in = {k: v for k, v in _L0_xattn_all.items() if k in ('wq', 'bq', 'wk', 'bk', 'wv', 'bv', 'wo', 'bo')}
    del _L0_xattn_all

    def _L0_ffn_setup():
        import jax, jax.numpy as jnp
        import numpy as np
        B, L, H, E, I = (4, 256, 128, 8, 512)
        S = B * L
        CAP_FACTOR_EVAL = 2.0
        MIN_CAP = 4
        _cap = int(np.floor(CAP_FACTOR_EVAL * S / E))
        _cap += _cap % 2
        CAPACITY = max(_cap, MIN_CAP)

        def _layer_norm(x, g, b, eps=1e-05):
            mu = x.mean(-1, keepdims=True)
            var = ((x - mu) ** 2).mean(-1, keepdims=True)
            return (x - mu) * jax.lax.rsqrt(var + eps) * g + b
        key = jax.random.key(seed)
        ks = jax.random.split(key, 8)
        gate_std = float(np.sqrt(0.1 / H))
        return {'inputs': jax.random.normal(ks[0], (B, L, H), jnp.float32), 'gate_weight': jax.random.normal(ks[1], (E, H), jnp.float32) * gate_std, 'ln_gamma': jnp.ones((H,), jnp.float32), 'ln_beta': jnp.zeros((H,), jnp.float32), 'wi': jax.random.normal(ks[2], (E, H, I), jnp.float32) * float(1.0 / np.sqrt(H)), 'wo': jax.random.normal(ks[3], (E, I, H), jnp.float32) * float(1.0 / np.sqrt(I)), 'conf_w1': jax.random.normal(ks[4], (H // 2, H), jnp.float32) * float(np.sqrt(2.0 / (H + H // 2))), 'conf_b1': -jnp.ones((H // 2,), jnp.float32), 'conf_w2': jax.random.normal(ks[5], (1, H // 2), jnp.float32) * float(np.sqrt(2.0 / (1 + H // 2))), 'conf_b2': -jnp.ones((1,), jnp.float32), 'comp_w': jax.random.normal(ks[6], (1, H), jnp.float32) * float(1.0 / np.sqrt(H)), 'comp_b': jnp.zeros((1,), jnp.float32)}
    _L0_ffn_all = _L0_ffn_setup()
    _L0_ffn_in = {k: v for k, v in _L0_ffn_all.items() if k in ('gate_weight', 'ln_gamma', 'ln_beta', 'wi', 'wo', 'conf_w1', 'conf_b1', 'conf_w2', 'conf_b2', 'comp_w', 'comp_b')}
    del _L0_ffn_all
    return {'x': x, 'ctx_1024': ctx_1024, 'L0_attn_Wq': _L0_attn_in['Wq'], 'L0_attn_Wk': _L0_attn_in['Wk'], 'L0_attn_Wv': _L0_attn_in['Wv'], 'L0_attn_Wg': _L0_attn_in['Wg'], 'L0_attn_gk_w1': _L0_attn_in['gk_w1'], 'L0_attn_gk_w2': _L0_attn_in['gk_w2'], 'L0_attn_gk_b2': _L0_attn_in['gk_b2'], 'L0_attn_g_norm_w': _L0_attn_in['g_norm_w'], 'L0_attn_Wo': _L0_attn_in['Wo'], 'L0_xattn_wq': _L0_xattn_in['wq'], 'L0_xattn_bq': _L0_xattn_in['bq'], 'L0_xattn_wk': _L0_xattn_in['wk'], 'L0_xattn_bk': _L0_xattn_in['bk'], 'L0_xattn_wv': _L0_xattn_in['wv'], 'L0_xattn_bv': _L0_xattn_in['bv'], 'L0_xattn_wo': _L0_xattn_in['wo'], 'L0_xattn_bo': _L0_xattn_in['bo'], 'L0_ffn_gate_weight': _L0_ffn_in['gate_weight'], 'L0_ffn_ln_gamma': _L0_ffn_in['ln_gamma'], 'L0_ffn_ln_beta': _L0_ffn_in['ln_beta'], 'L0_ffn_wi': _L0_ffn_in['wi'], 'L0_ffn_wo': _L0_ffn_in['wo'], 'L0_ffn_conf_w1': _L0_ffn_in['conf_w1'], 'L0_ffn_conf_b1': _L0_ffn_in['conf_b1'], 'L0_ffn_conf_w2': _L0_ffn_in['conf_w2'], 'L0_ffn_conf_b2': _L0_ffn_in['conf_b2'], 'L0_ffn_comp_w': _L0_ffn_in['comp_w'], 'L0_ffn_comp_b': _L0_ffn_in['comp_b']}

def reference(x, ctx_1024, L0_attn_Wq, L0_attn_Wk, L0_attn_Wv, L0_attn_Wg, L0_attn_gk_w1, L0_attn_gk_w2, L0_attn_gk_b2, L0_attn_g_norm_w, L0_attn_Wo, L0_xattn_wq, L0_xattn_bq, L0_xattn_wk, L0_xattn_bk, L0_xattn_wv, L0_xattn_bv, L0_xattn_wo, L0_xattn_bo, L0_ffn_gate_weight, L0_ffn_ln_gamma, L0_ffn_ln_beta, L0_ffn_wi, L0_ffn_wo, L0_ffn_conf_w1, L0_ffn_conf_b1, L0_ffn_conf_w2, L0_ffn_conf_b2, L0_ffn_comp_w, L0_ffn_comp_b):
    import jax
    import jax.numpy as jnp

    def _L0_attn_ref(x, Wq, Wk, Wv, Wg, gk_w1, gk_w2, gk_b2, g_norm_w, Wo):
        import jax, jax.numpy as jnp
        import numpy as np
        NUM_HEADS = 4
        CHUNK = 64
        GATE_NORM = 16.0
        EPS = 1e-05

        def _xavier(key, fan_in, fan_out):
            gain = 2.0 ** (-2.5)
            limit = gain * np.sqrt(6.0 / (fan_in + fan_out))
            return jax.random.uniform(key, (fan_in, fan_out), jnp.float32, -limit, limit)

        def _to_chunks(t, B, H, NC, C):
            d = t.shape[-1]
            return t.reshape(B, H, NC, C, d).transpose(2, 0, 1, 3, 4)

        def _gla_forward(x, Wq, Wk, Wv, Wg, gk_w1, gk_w2, gk_b2, g_norm_w, Wo):
            B, L, D = x.shape
            H = NUM_HEADS
            C = CHUNK
            NC = L // C
            q = x @ Wq
            k = x @ Wk
            v = x @ Wv
            gk = jax.nn.log_sigmoid(x @ gk_w1 @ gk_w2 + gk_b2) / GATE_NORM

            def split_heads(t):
                return t.reshape(B, L, H, -1).transpose(0, 2, 1, 3)
            q, k, v, gk = map(split_heads, (q, k, v, gk))
            dk = q.shape[-1]
            scale = dk ** (-0.5)
            qc = _to_chunks(q, B, H, NC, C)
            kc = _to_chunks(k, B, H, NC, C)
            vc = _to_chunks(v, B, H, NC, C)
            gc = _to_chunks(gk, B, H, NC, C)
            Bcum = jnp.cumsum(gc, axis=3)
            causal = jnp.tril(jnp.ones((C, C), jnp.float32))

            def step(Hst, inp):
                qi, ki, vi, bi = inp
                qg = qi * jnp.exp(bi) * scale
                kg = ki * jnp.exp(-bi)
                o_inter = jnp.einsum('bhcd,bhde->bhce', qg, Hst)
                A = jnp.einsum('bhtd,bhsd->bhts', qg, kg) * causal
                o_intra = jnp.einsum('bhts,bhse->bhte', A, vi)
                b_last = bi[:, :, -1:, :]
                kH = ki * jnp.exp(b_last - bi)
                H_new = jnp.exp(b_last).transpose(0, 1, 3, 2) * Hst + jnp.einsum('bhcd,bhce->bhde', kH, vi)
                return (H_new, o_inter + o_intra)
            dv = v.shape[-1]
            H0 = jnp.zeros((B, H, dk, dv), jnp.float32)
            _, oc = jax.lax.scan(step, H0, (qc, kc, vc, Bcum))
            o = oc.transpose(1, 2, 0, 3, 4).reshape(B, H, L, dv)
            o = o.transpose(0, 2, 1, 3)
            rms = jnp.sqrt(jnp.mean(o * o, axis=-1, keepdims=True) + EPS)
            o_n = o / rms * g_norm_w
            g = (x @ Wg).reshape(B, L, H, dv)
            o = o_n * g * jax.nn.sigmoid(g)
            return o.reshape(B, L, H * dv) @ Wo
        return _gla_forward(x, Wq, Wk, Wv, Wg, gk_w1, gk_w2, gk_b2, g_norm_w, Wo)

    def _L0_xattn_ref(q, k, v, wq, bq, wk, bk, wv, bv, wo, bo):
        import jax, jax.numpy as jnp
        import numpy as np
        D_MODEL = 128
        NUM_HEADS = 16
        DEPTH = D_MODEL // NUM_HEADS

        def _split_heads(x, B):
            return x.reshape(B, -1, NUM_HEADS, DEPTH).transpose(0, 2, 1, 3)
        B, S, _ = q.shape
        qh = _split_heads(q @ wq.T + bq, B)
        kh = _split_heads(k @ wk.T + bk, B)
        vh = _split_heads(v @ wv.T + bv, B)
        scale = jnp.sqrt(jnp.asarray(DEPTH, jnp.float32))
        scores = jnp.einsum('bhqd,bhkd->bhqk', qh, kh) / scale
        attn = jax.nn.softmax(scores, axis=-1)
        out = jnp.einsum('bhqk,bhkd->bhqd', attn, vh)
        out = out.transpose(0, 2, 1, 3).reshape(B, S, D_MODEL)
        return out @ wo.T + bo

    def _L0_ffn_ref(inputs, gate_weight, ln_gamma, ln_beta, wi, wo, conf_w1, conf_b1, conf_w2, conf_b2, comp_w, comp_b):
        import jax, jax.numpy as jnp
        import numpy as np
        B, L, H, E, I = (4, 256, 128, 8, 512)
        S = B * L
        CAP_FACTOR_EVAL = 2.0
        MIN_CAP = 4
        _cap = int(np.floor(CAP_FACTOR_EVAL * S / E))
        _cap += _cap % 2
        CAPACITY = max(_cap, MIN_CAP)

        def _layer_norm(x, g, b, eps=1e-05):
            mu = x.mean(-1, keepdims=True)
            var = ((x - mu) ** 2).mean(-1, keepdims=True)
            return (x - mu) * jax.lax.rsqrt(var + eps) * g + b
        tokens = inputs.reshape(-1, H)
        residual = tokens
        tokens = _layer_norm(tokens, ln_gamma, ln_beta)
        complexity_score = jax.nn.sigmoid(tokens @ comp_w.T + comp_b).mean()
        hdn = jax.nn.relu(tokens @ conf_w1.T + conf_b1)
        confidence_score = jax.nn.sigmoid(hdn @ conf_w2.T + conf_b2).mean()
        logits = tokens.astype(jnp.float32) @ gate_weight.astype(jnp.float32).T
        probs = jax.nn.softmax(logits, axis=-1)
        top1 = jnp.argmax(logits, axis=-1)
        onehot = jax.nn.one_hot(top1, E, dtype=jnp.int32)
        rank_e = jnp.cumsum(onehot, axis=0) - onehot
        rank = jnp.sum(rank_e * onehot, axis=-1)
        keep = rank < CAPACITY
        weight = jnp.take_along_axis(probs, top1[:, None], axis=-1)[:, 0]
        weight = (weight * keep).astype(tokens.dtype)
        slot = jnp.where(keep, rank, 0)
        dispatch = jnp.zeros((E, CAPACITY, H), tokens.dtype)
        dispatch = dispatch.at[top1, slot].add(tokens * keep[:, None])
        h = jax.nn.gelu(jnp.einsum('ech,ehi->eci', dispatch, wi), approximate=False)
        expert_out = jnp.einsum('eci,eih->ech', h, wo)
        combined = weight[:, None] * expert_out[top1, slot]
        out = (residual + combined).reshape(inputs.shape)
        return out
    x = x + _L0_attn_ref(_layernorm(x, axis=-1), L0_attn_Wq, L0_attn_Wk, L0_attn_Wv, L0_attn_Wg, L0_attn_gk_w1, L0_attn_gk_w2, L0_attn_gk_b2, L0_attn_g_norm_w, L0_attn_Wo)
    x = x + _L0_xattn_ref(_layernorm(x, axis=-1), ctx_1024, ctx_1024, L0_xattn_wq, L0_xattn_bq, L0_xattn_wk, L0_xattn_bk, L0_xattn_wv, L0_xattn_bv, L0_xattn_wo, L0_xattn_bo)
    x = x + _L0_ffn_ref(_layernorm(x, axis=-1), L0_ffn_gate_weight, L0_ffn_ln_gamma, L0_ffn_ln_beta, L0_ffn_wi, L0_ffn_wo, L0_ffn_conf_w1, L0_ffn_conf_b1, L0_ffn_conf_w2, L0_ffn_conf_b2, L0_ffn_comp_w, L0_ffn_comp_b)
    return x

_drawn_inputs = setup_inputs


def setup_inputs(seed=0):
    import zlib

    import numpy as np

    out = dict(_drawn_inputs(seed))
    spreads = {'L0_attn_gk_b2': (0.0, 0.8),
     'L0_attn_g_norm_w': (1.0, 0.6),
     'L0_ffn_ln_gamma': (1.0, 0.2),
     'L0_ffn_ln_beta': (0.0, 0.316),
     'L0_ffn_conf_b1': (-1.0, 0.2)}
    factors = {'L0_attn_Wq': 3.739,
     'L0_attn_Wk': 3.82,
     'L0_attn_Wv': 3.781,
     'L0_attn_Wg': 3.794,
     'L0_attn_gk_w1': 8.0,
     'L0_attn_gk_w2': 8.0,
     'L0_attn_Wo': 3.792,
     'L0_xattn_bq': 2.749,
     'L0_xattn_bk': 8.0}
    for name, (base, spread) in spreads.items():
        noise = np.random.default_rng([zlib.crc32(name.encode()), seed]).standard_normal(out[name].shape)
        drawn = base * np.exp(spread * noise) if base else spread * noise
        out[name] = jnp.asarray(drawn.astype(out[name].dtype))
    for name, factor in factors.items():
        out[name] = (out[name] * factor).astype(out[name].dtype)
    return out
```

```python
from contextlib import ExitStack

import numpy as np

import concourse.bass as bass
from concourse import mybir

F32 = mybir.dt.float32
BF16 = mybir.dt.bfloat16
U32 = mybir.dt.uint32
ALU = mybir.AluOpType
ACT = mybir.ActivationFunctionType
AX = mybir.AxisListType

P = 128
SEQS, L, D = 16, 128, 128
KEYS = 120
GROUP = 2
GROUPS = SEQS // GROUP
T = GROUP * L
GLA_HEADS, DK, DV, CHUNK = 4, 32, 64, 64
RANK = 16
HEADS, DEPTH = 16, 8
PAIRS = HEADS // 2
PARTS = 3
Q_PART = (0, 0, 0, 1, 1, 1, 2, 2)
K_PART = (0, 1, 2, 0, 1, 2, 0, 1)
EXPERTS, HIDDEN = 8, 512
CAPACITY = 256
SLOTS = EXPERTS * CAPACITY
TILES = SEQS
HT = HIDDEN // P
EPS = 1e-5
GATE_NORM = 16.0
LN_EXP = "natural_log_exp_and_others"


def layout(parts):
    at, out = 0, {}
    for name, width in parts:
        out[name] = (at, at + width)
        at += width
    return out, at


EARLY, EARLY_W = layout([("ident", P), ("w1", RANK), ("w2", D), ("b2", 1), ("bq", 1), ("bk", 1), ("bv", 1),
                         ("gamma", 1), ("beta", 1), ("vg", 512), ("q", D), ("k", D)])
LATE, LATE_W = layout([("wo", 2 * D), ("xk", D), ("xv", D), ("xq", D), ("xo", D), ("gate", EXPERTS),
                       ("gnorm", GLA_HEADS * DV), ("bo", D)])
SHAPE, SHAPE_W = layout([("reset", T), ("causal", P), ("mhalf", 8), ("ebase", EXPERTS * TILES),
                         ("order", EXPERTS * TILES), ("treset", EXPERTS * TILES)])
SHAPE16, SHAPE16_W = layout([("ident", P), ("pick", PAIRS * KEYS), ("before", P), ("ones", P)])


def build(nc, x, ctx_t, early_d, late_d, shape_d, shape16_d, wi_d, wo_d, out, slots_in, slots_out):
    with ExitStack() as stack:
        def sb(name, shape, dt=F32):
            return stack.enter_context(nc.sbuf_tensor(name, shape, dt))

        def bank(name):
            return stack.enter_context(nc.psum_tensor(name, [P, 512], F32))

        def sem(name):
            return stack.enter_context(nc.semaphore(name))

        early = sb("early", [P, EARLY_W])
        late = sb("late", [P, LATE_W])
        shapes = sb("shapes", [P, SHAPE_W])
        shapes_w = sb("shapes_w", [P, SHAPE16_W])
        shapes16 = sb("shapes16", [P, SHAPE16_W], BF16)

        def E(name):
            return early[:, EARLY[name][0]:EARLY[name][1]]

        def Lt(name):
            return late[:, LATE[name][0]:LATE[name][1]]

        def S(name):
            return shapes[:, SHAPE[name][0]:SHAPE[name][1]]

        def S16(name):
            return shapes16[:, SHAPE16[name][0]:SHAPE16[name][1]]

        pick = S16("pick").rearrange("p (a k) -> p a k", a=PAIRS)
        half_gnorm = sb("half_gnorm", [P, GLA_HEADS * DV])

        xy_all = sb("xy_all", [P, SEQS, D])
        z_all = sb("z_all", [P, SEQS, D])
        logits = sb("logits", [P, EXPERTS, TILES])

        x_g = [sb(f"x_g{i}", [P, GROUP, D]) for i in range(2)]
        ctx_g = [sb(f"ctx_g{i}", [P, GROUP, KEYS]) for i in range(2)]
        st1 = sb("st1", [P, GROUP, 6])
        pause = sb("pause", [P, 1])
        mv1 = sb("mv1", [P, GROUP, 2])
        ve1 = sb("ve1", [P, GROUP])
        rs1 = sb("rs1", [P, GROUP])
        xn1 = sb("xn1", [P, GROUP, D])
        xn1_t = sb("xn1_t", [P, T])
        low = sb("low", [RANK, T])
        z_abs = sb("z_abs", [P, T])
        z_exp = sb("z_exp", [P, T])
        z_ln = sb("z_ln", [P, T])
        z_min = sb("z_min", [P, T])
        gk = sb("gk", [P, T])
        bcum = sb("bcum", [P, T])
        e_pos = sb("e_pos", [P, T])
        e_neg = sb("e_neg", [P, T])
        qg = sb("qg", [P, GROUP, L])
        k_first = sb("k_first", [P, GROUP, L])
        k_second = sb("k_second", [P, GROUP, L])
        v_sb = sb("v_sb", [P, GROUP, GLA_HEADS * DV])
        th = sb("th", [P, GROUP, GLA_HEADS * DV])
        silu2 = sb("silu2", [P, GROUP, GLA_HEADS * DV])
        silu_n = sb("silu_n", [P, GROUP, GLA_HEADS * DV])
        att = [sb(f"att{h}", [P, GROUP, L]) for h in range(GLA_HEADS)]
        o_sq = sb("o_sq", [P, GROUP * GLA_HEADS, DV])
        o_ss = sb("o_ss", [P, GROUP * GLA_HEADS])
        o_ms = sb("o_ms", [P, GROUP * GLA_HEADS])
        o_rs = sb("o_rs", [P, GROUP * GLA_HEADS])
        o_gate = sb("o_gate", [P, GROUP, GLA_HEADS * DV])
        og = sb("og", [P, GROUP, GLA_HEADS * DV])
        og_t = sb("og_t", [P, GROUP, 2, L])
        x1 = sb("x1", [P, GROUP, D])
        x1b = [sb(f"x1b{i}", [P, GROUP, D]) for i in range(2)]
        st2 = sb("st2", [P, GROUP, 6])
        mv2 = sb("mv2", [P, GROUP, 2])
        ve2 = sb("ve2", [P, GROUP])
        rs2 = sb("rs2", [P, GROUP])
        xn2 = sb("xn2", [P, GROUP, D])
        xn2_t = sb("xn2_t", [P, T])
        k_part = [sb(f"k_part{i}", [P, GROUP * KEYS], BF16) for i in range(PARTS)]
        q_part = [sb(f"q_part{i}", [P, T], BF16) for i in range(PARTS)]
        k_rest = sb("k_rest", [P, GROUP * KEYS])
        q_rest = sb("q_rest", [P, T])
        ks = [sb(f"ks{i}", [P, PAIRS, GROUP * KEYS], BF16) for i in range(2)]
        qs = [sb(f"qs{i}", [P, PAIRS, T], BF16) for i in range(2)]
        v_aug = [sb(f"v_aug{i}", [KEYS, GROUP, HEADS, DEPTH + 1]) for i in range(2)]

        max_neg = sb("max_neg", [P, 2, PAIRS])
        max_part = sb("max_part", [P, 2, 8, PAIRS], BF16)
        max_t = sb("max_t", [P, P], BF16)
        prob = sb("prob", [KEYS, 2, PAIRS, L])
        den = sb("den", [P, HEADS])
        o2 = sb("o2", [P, HEADS, DEPTH])
        o2_t = sb("o2_t", [P, L])
        x2 = sb("x2", [P, GROUP, D])
        st3 = sb("st3", [P, GROUP, 6])
        mv3 = sb("mv3", [P, GROUP, 2])
        ve3 = sb("ve3", [P, GROUP])
        rs3 = sb("rs3", [P, GROUP])
        rr3 = sb("rr3", [P, GROUP])
        ve4 = sb("ve4", [P, GROUP])
        rs4 = sb("rs4", [P, GROUP])
        y = sb("y", [P, GROUP, D])
        z_g = sb("z_g", [P, GROUP, D])
        z_t = sb("z_t", [P, T])

        def rt(name, dt=F32):
            return sb(name, [P, EXPERTS, TILES], dt)

        def tt_(name, dt=F32):
            return sb(name, [P, TILES], dt)

        r_max, r_val, r_sum, r_inv, r_slot, r_keep, r_off, r_tmp, weight = [
            tt_(n) for n in ("r_max", "r_val", "r_sum", "r_inv", "r_slot", "r_keep", "r_off", "r_tmp", "weight")]
        r_eq, r_cand, one_hot, r_diff, r_exp, r_incl, r_rank, r_a, r_b = [
            rt(n) for n in ("r_eq", "r_cand", "one_hot", "r_diff", "r_exp", "r_incl", "r_rank", "r_a", "r_b")]
        hot16 = rt("hot16", BF16)
        tiles_before = rt("tiles_before", BF16)
        to_slot = tt_("to_slot", U32)
        from_slot = tt_("from_slot", U32)

        wi_e = [sb(f"wi_e{i}", [P, HIDDEN]) for i in range(2)]
        wo_e = [sb(f"wo_e{i}", [P, HT, D]) for i in range(2)]
        tok = [sb(f"tok{i}", [P, 2, D]) for i in range(2)]
        tok_t = [sb(f"tok_t{i}", [P, CAPACITY]) for i in range(2)]
        hid = [sb(f"hid{i}", [P, HT, CAPACITY]) for i in range(2)]
        e_out = [sb(f"e_out{i}", [P, 2, D]) for i in range(2)]
        back = sb("back", [P, SEQS, D])
        result = sb("result", [P, SEQS, D])

        A, B, C, M = bank("bank_a"), bank("bank_b"), bank("bank_c"), bank("bank_m")
        SB = [bank("bank_s0"), bank("bank_s1")]
        TB = [bank("bank_t0"), bank("bank_t1")]

        names = """early_in late_in shapes_in shapes16_in shapes16_set zeroed cleared half_gnorm_set v_ones
            stats1 aggr1 veps1 rstd1 xn1_set xt1 xt1_out low_done low_out z_done abs_set exp_set ln_set min_set
            gk_set scan_set decay_set vg_done v_set tanh_set silu_set silu_n_set qk_done qg_set kf_set gated
            at_done att_set o_done sq_set ss_set ms_set rs_set gate_set og_set ogt_done ogt_out wo_done x1_set
            x1b_set stats2 aggr2 veps2 rstd2 xn2_set xt2 xt2_out q_done kv_done k1_set krest_set k2_set k3_set
            vaug_set q1_set qrest_set q2_set q3_set
            s_done max_set m1_set m2_set mt_done mt_out t_done exp2_set pv_done den_set o2_set o2t_done o2t_out
            xo_done x2_set stats3 aggr3 veps3 rstd3 rr3_set veps4 rstd4 y_set xy_set z_set zall_set zt_done
            zt_out lg_done lg_set
            r_chain r_sub r_expd hot_set before_set rank_done idx_set scattered gathered
            tt_done tok_out h_done gelu_set eo_done eo_set res_set stored""".split()
        N = {n: sem(n) for n in names}
        x_in = [sem("x_in0"), sem("x_in1")]
        ctx_in = [sem("ctx_in0"), sem("ctx_in1")]
        ks_in = [sem("ks_in0"), sem("ks_in1")]
        qs_in = [sem("qs_in0"), sem("qs_in1")]
        we_in = [sem("we_in0"), sem("we_in1")]
        tok_in = [sem("tok_in0"), sem("tok_in1")]
        eo_stored = [sem("eo_stored0"), sem("eo_stored1")]

        def upto(g, n, k=None):
            j, par = g
            return (2 * j + par) * n + (n if k is None else k)

        def before(g, n):
            j, par = g
            return (2 * j + par) * n

        def schedule(step_a, step_b, step_c, step_s, step_t, step_o, step_e, Fori):
            def beside(done, ahead):
                step_s(done, 0)
                step_a(ahead)
                step_t(done, 0)
                step_b(ahead)
                step_s(done, 1)
                step_o(done, 0)
                step_c(ahead)
                step_t(done, 1)
                step_o(done, 1)
                step_e(done)

            def alone(done):
                for b in range(GROUP):
                    step_s(done, b)
                    step_t(done, b)
                    step_o(done, b)
                step_e(done)

            step_a((0, 0))
            step_b((0, 0))
            step_c((0, 0))
            beside((0, 0), (0, 1))
            with Fori(0, GROUPS // 2 - 1) as j:
                beside((j, 1), (j + 1, 0))
                beside((j + 1, 0), (j + 1, 1))
            alone((GROUPS // 2 - 1, 1))

        def nothing(*_):
            pass

        block = stack.enter_context(nc.Block())

        @block.sync
        def _(sp):
            def load_x(j, par):
                G = 2 * j + par
                sp.dma_start(x_g[par][:, :, :], x[:, bass.ds(G * GROUP, GROUP), :]).then_inc(x_in[par], 16)
                sp.dma_start(ctx_g[par][:, :, :], ctx_t[:, bass.ds(G * GROUP, GROUP), :]).then_inc(ctx_in[par], 16)

            load_x(0, 0)
            sp.dma_start(early[:, :], early_d).then_inc(N["early_in"], 16)
            sp.dma_start(shapes[:, :], shape_d).then_inc(N["shapes_in"], 16)
            sp.dma_start(late[:, :], late_d).then_inc(N["late_in"], 16)
            sp.dma_start(shapes_w[:, :], shape16_d).then_inc(N["shapes16_in"], 16)
            load_x(0, 1)
            sp.wait_ge(N["cleared"], 1)
            sp.dma_start(slots_in.rearrange("(t p) d -> p t d", p=P), back[:, :, :]).then_inc(N["zeroed"], 16)

            def load_more(g):
                used = sp.snap(before(g, 1) - 1) if not isinstance(g[0], int) else before(g, 1) - 1
                sp.wait_ge(N["x1_set"], used)
                sp.wait_ge(N["kv_done"], used)
                load_x(*g)

            def stack(g, count, free):
                par = g[1]
                ready = upto(g, 1)
                sp.wait_ge(N["k3_set"], ready)
                sp.wait_ge(N[count], free)
                for c in range(8):
                    sp.dma_start(ks[par][c::8, :, :], k_part[K_PART[c]][:, :]).then_inc(ks_in[par], 16)
                sp.wait_ge(N["q3_set"], ready)
                for c in range(8):
                    sp.dma_start(qs[par][c::8, :, :], q_part[Q_PART[c]][:, :]).then_inc(qs_in[par], 16)

            stack((0, 0), "lg_done", 0)
            stack((0, 1), "lg_done", 0)
            with sp.Fori(0, GROUPS // 2 - 1) as j:
                load_more((j + 1, 0))
                stack((j + 1, 0), "pv_done", before((j, 1), GROUP))
                load_more((j + 1, 1))
                stack((j + 1, 1), "lg_done", before((j + 1, 0), 1))

            def weights(j, par):
                e = 2 * j + par
                sp.dma_start(wi_e[par][:, :], wi_d[:, bass.ds(e, 1), :].rearrange("p o n -> p (o n)")
                             ).then_inc(we_in[par], 16)
                sp.dma_start(wo_e[par][:, :, :], wo_d[:, bass.ds(e * HT, HT), :]).then_inc(we_in[par], 16)

            def tokens(j, par):
                e = 2 * j + par
                sp.dma_start(tok[par][:, :, :],
                             slots_in.rearrange("(t p) d -> p t d", p=P)[:, bass.ds(e * 2, 2), :]
                             ).then_inc(tok_in[par], 16)

            def store(j, par):
                e = 2 * j + par
                sp.wait_ge(N["eo_set"], e + 1)
                sp.dma_start(slots_out.rearrange("(t p) d -> p t d", p=P)[:, bass.ds(e * 2, 2), :],
                             e_out[par][:, :, :]).then_inc(eo_stored[par], 16)

            weights(0, 0)
            weights(0, 1)
            sp.wait_ge(N["scattered"], 16 * TILES)
            tokens(0, 0)
            tokens(0, 1)
            with sp.Fori(0, EXPERTS // 2 - 1) as j:
                for par in range(2):
                    e = sp.snap(2 * j + par)
                    made = sp.snap(e + 1)
                    sp.wait_ge(N["tt_done"], made)
                    tokens(j + 1, par)
                    sp.wait_ge(N["eo_done"], made)
                    weights(j + 1, par)
                    store(j, par)
            for par in range(2):
                store(EXPERTS // 2 - 1, par)
            sp.wait_ge(eo_stored[0], 16 * (EXPERTS // 2))
            sp.wait_ge(eo_stored[1], 16 * (EXPERTS // 2))
            for i in range(4):
                sp.wait_ge(N["res_set"], 4 * (i + 1))
                sp.dma_start(out[:, 4 * i:4 * i + 4, :], result[:, 4 * i:4 * i + 4, :]).then_inc(N["stored"], 16)
            sp.wait_ge(N["stored"], 64)

        @block.gpsimd
        def _(pool):
            pool.wait_ge(N["shapes_in"], 16)
            pool.wait_ge(N["late_in"], 16)
            mh = S("mhalf")

            def step_a(g):
                pool.wait_ge(N["veps1"], upto(g, 1))
                pool.tensor_tensor(rs1[:, :], ve1[:, :], mh[:, 0:GROUP], ALU.pow).then_inc(N["rstd1"], 1)

            def step_b(g):
                pool.wait_ge(N["half_gnorm_set"], 1)
                for b in range(GROUP):
                    pool.wait_ge(N["silu_set"], upto(g, GROUP, b + 1))
                    pool.tensor_tensor(silu_n[:, b, :], silu2[:, b, :], half_gnorm[:, :], ALU.mult
                                       ).then_inc(N["silu_n_set"], 1)
                pool.wait_ge(N["ms_set"], upto(g, 1))
                pool.tensor_tensor(o_rs[:, :], o_ms[:, :], mh[:, 0:GROUP * GLA_HEADS], ALU.pow
                                   ).then_inc(N["rs_set"], 1)
                pool.wait_ge(N["rs_set"], upto(g, 1))
                pool.wait_ge(N["silu_n_set"], upto(g, GROUP))
                pool.tensor_tensor(o_gate[:, :, :].rearrange("p b (h e) -> p (b h) e", h=GLA_HEADS),
                                   silu_n[:, :, :].rearrange("p b (h e) -> p (b h) e", h=GLA_HEADS),
                                   o_rs[:, :].unsqueeze(2).to_broadcast([P, GROUP * GLA_HEADS, DV]),
                                   ALU.mult).then_inc(N["gate_set"], 1)

            def step_c(g):
                j, par = g
                pool.wait_ge(N["veps2"], upto(g, 1))
                pool.tensor_tensor(rs2[:, :], ve2[:, :], mh[:, 0:GROUP], ALU.pow).then_inc(N["rstd2"], 1)
                pool.tensor_tensor(x1b[par][:, :, :], x1[:, :, :],
                                   Lt("bo").unsqueeze(1).to_broadcast([P, GROUP, D]), ALU.add
                                   ).then_inc(N["x1b_set"], 1)

            def step_e(g):
                pool.wait_ge(N["veps3"], upto(g, 1))
                pool.tensor_tensor(rs3[:, :], ve3[:, :], mh[:, 0:GROUP], ALU.pow).then_inc(N["rstd3"], 1)
                pool.wait_ge(N["veps4"], upto(g, 1))
                pool.tensor_tensor(rs4[:, :], ve4[:, :], mh[:, 0:GROUP], ALU.pow).then_inc(N["rstd4"], 1)

            schedule(step_a, step_b, step_c, nothing, nothing, nothing, step_e, pool.Fori)

            pool.wait_ge(N["idx_set"], 2)
            pool.wait_ge(N["zeroed"], 16)
            for i in range(TILES):
                pool.indirect_dma_start(out=slots_in, out_offset=bass.IndirectOffsetOnAxis(ap=to_slot[:, i:i + 1], axis=0),
                                        in_=z_all[:, i, :], in_offset=None, bounds_check=SLOTS - 1,
                                        oob_is_err=False).then_inc(N["scattered"], 16)
            pool.wait_ge(eo_stored[0], 16 * (EXPERTS // 2))
            pool.wait_ge(eo_stored[1], 16 * (EXPERTS // 2))
            for i in range(TILES):
                pool.indirect_dma_start(out=back[:, i, :], out_offset=None, in_=slots_out,
                                        in_offset=bass.IndirectOffsetOnAxis(ap=from_slot[:, i:i + 1], axis=0)
                                        ).then_inc(N["gathered"], 16)

        @block.tensor
        def _(pe):
            pe.wait_ge(N["early_in"], 16)
            ident = E("ident")

            def step_a(g):
                j, par = g
                pe.wait_ge(N["xt2_out"], before(g, 1))
                pe.wait_ge(N["xn1_set"], upto(g, 1))
                for b in range(GROUP):
                    mm = pe.transpose(A[:, b * L:(b + 1) * L], xn1[:, b, :], ident)
                mm.then_inc(N["xt1"], 1)
                pe.wait_ge(N["vaug_set"], before(g, 1))
                pe.wait_ge(N["krest_set"], before(g, 1))
                pe.wait_ge(N["xt1_out"], upto(g, 1))
                pe.matmul(B[0:RANK, 0:T], E("w1"), xn1_t[:, :], start=True, stop=True).then_inc(N["low_done"], 1)
                pe.matmul(A[:, :], xn1_t[:, 0:L], E("vg"), start=True, stop=True).then_inc(N["vg_done"], 1)
                pe.wait_ge(N["qrest_set"], before(g, 1))
                pe.wait_ge(N["low_out"], upto(g, 1))
                pe.matmul(C[:, 0:T], E("w2")[0:RANK, :], low[:, :], start=True, stop=True).then_inc(N["z_done"], 1)
                pe.matmul(B[:, :], xn1_t[:, L:T], E("vg"), start=True, stop=True).then_inc(N["vg_done"], 1)
                pe.wait_ge(N["abs_set"], upto(g, 1))
                pe.wait_ge(N["min_set"], upto(g, 1))
                pe.matmul(C[:, 0:T], E("q"), xn1_t[:, :], start=True, stop=True)
                pe.matmul(C[:, T:2 * T], E("k"), xn1_t[:, :], start=True, stop=True).then_inc(N["qk_done"], 1)

            def step_b(g):
                pe.wait_ge(N["gated"], upto(g, 1))
                for h in range(GLA_HEADS):
                    rows = slice(DK * h, DK * (h + 1))
                    if h < 2:
                        pe.wait_ge(N["v_set"], upto(g, GROUP, h + 1))
                        pe.wait_ge(N["silu_set"], upto(g, GROUP, h + 1))
                    else:
                        pe.wait_ge(N["att_set"], upto(g, GLA_HEADS, h - 1))
                    bank_h = (A, B)[h % 2]
                    for b in range(GROUP):
                        pe.matmul(bank_h[:, b * L:b * L + CHUNK], k_first[rows, b, :], qg[rows, b, 0:CHUNK],
                                  start=True, stop=True)
                        mm = pe.matmul(bank_h[:, b * L + CHUNK:(b + 1) * L], k_second[rows, b, :],
                                       qg[rows, b, CHUNK:L], start=True, stop=True)
                    mm.then_inc(N["at_done"], 1)
                pe.wait_ge(N["att_set"], upto(g, GLA_HEADS))
                for b in range(GROUP):
                    for h in range(GLA_HEADS):
                        at = (b * GLA_HEADS + h) * DV
                        mm = pe.matmul(C[:, at:at + DV], att[h][:, b, :], v_sb[:, b, h * DV:(h + 1) * DV],
                                       start=True, stop=True)
                mm.then_inc(N["o_done"], 1)

            def step_c(g):
                j, par = g
                pe.wait_ge(N["late_in"], 16)
                pe.wait_ge(N["og_set"], upto(g, 1))
                for b in range(GROUP):
                    for c in range(2):
                        at = (2 * b + c) * L
                        mm = pe.transpose(A[:, at:at + L], og[:, b, c * P:(c + 1) * P], ident)
                mm.then_inc(N["ogt_done"], 1)
                pe.wait_ge(N["ogt_out"], upto(g, 1))
                for b in range(GROUP):
                    for c in range(2):
                        mm = pe.matmul(B[:, b * D:(b + 1) * D], og_t[:, b, c, :],
                                       Lt("wo")[:, c * D:(c + 1) * D], start=(c == 0), stop=(c == 1))
                mm.then_inc(N["wo_done"], 1)
                pe.wait_ge(N["x1_set"], upto(g, 1))
                pe.wait_ge(ctx_in[par], 16 * (j + 1))
                pe.matmul(B[:, 0:GROUP * KEYS], Lt("xk"), ctx_g[par][:, :, :].rearrange("p b k -> p (b k)"),
                          start=True, stop=True)
                for b in range(GROUP):
                    mm = pe.matmul(B[0:KEYS, T + b * D:T + (b + 1) * D], ctx_g[par][:, b, :], Lt("xv"),
                                   start=True, stop=True)
                mm.then_inc(N["kv_done"], 1)
                pe.wait_ge(N["xn2_set"], upto(g, 1))
                for b in range(GROUP):
                    mm = pe.transpose(A[:, b * L:(b + 1) * L], xn2[:, b, :], ident)
                mm.then_inc(N["xt2"], 1)
                pe.wait_ge(N["xt2_out"], upto(g, 1))
                pe.matmul(C[:, 0:T], Lt("xq"), xn2_t[:, :], start=True, stop=True).then_inc(N["q_done"], 1)

            def unit(u):
                return u % 2, range(4 * (u // 2), 4 * (u // 2) + 4)

            def step_s(g, b):
                j, par = g
                if b == 0:
                    pe.wait_ge(ks_in[par], 128 * (j + 1))
                    pe.wait_ge(qs_in[par], 128 * (j + 1))
                for u in range(4):
                    two, pairs = unit(u)
                    rows = slice(64 * two, 64 * two + 64)
                    if u < 2:
                        pe.wait_ge(N["max_set"], before(g, 8) + 4 * b)
                    else:
                        pe.wait_ge(N["max_set"], before(g, 8) + 4 * b + u - 1)
                    for i, pair in enumerate(pairs):
                        mm = pe.matmul(SB[two][:, i * KEYS:(i + 1) * KEYS], qs[par][rows, pair, b * L:(b + 1) * L],
                                       ks[par][rows, pair, b * KEYS:(b + 1) * KEYS], start=True, stop=True)
                    mm.then_inc(N["s_done"], 1)

            def step_t(g, b):
                j, par = g
                n = before(g, GROUP) + b
                pe.wait_ge(N["x2_set"], n)
                pe.wait_ge(N["lg_set"], before(g, 1))
                pe.wait_ge(N["m2_set"], n + 1)
                pe.transpose(M[:, 0:P // 2].bitcast(BF16), max_part[:, :, :, :].rearrange("p w c a -> p (w c a)"),
                             S16("ident")).then_inc(N["mt_done"], 1)
                pe.wait_ge(N["mt_out"], n + 1)
                for u in range(4):
                    two, pairs = unit(u)
                    rows = slice(64 * two, 64 * two + 64)
                    if u < 2:
                        pe.wait_ge(N["exp2_set"], before(g, 8) + 4 * b)
                    else:
                        pe.wait_ge(N["exp2_set"], before(g, 8) + 4 * b + u - 1)
                    for i, pair in enumerate(pairs):
                        pe.matmul(TB[two][0:KEYS, i * L:(i + 1) * L], ks[par][rows, pair, b * KEYS:(b + 1) * KEYS],
                                  qs[par][rows, pair, b * L:(b + 1) * L], start=True, stop=False)
                        mm = pe.matmul(TB[two][0:KEYS, i * L:(i + 1) * L], pick[rows, pair, :], max_t[rows, :],
                                       start=False, stop=True)
                    mm.then_inc(N["t_done"], 1)

            def step_o(g, b):
                j, par = g
                n = before(g, GROUP) + b
                if b == 0:
                    pe.wait_ge(N["vaug_set"], upto(g, 1))
                for u in range(4):
                    two, pairs = unit(u)
                    pe.wait_ge(N["exp2_set"], before(g, 8) + 4 * b + u + 1)
                    for pair in pairs:
                        h = 2 * pair + two
                        mm = pe.matmul(M[:, h * (DEPTH + 1):(h + 1) * (DEPTH + 1)], prob[:, two, pair, :],
                                       v_aug[par][:, b, h, :], start=True, stop=True)
                mm.then_inc(N["pv_done"], 1)
                pe.wait_ge(N["o2_set"], n + 1)
                pe.transpose(M[:, 0:L], o2[:, :, :].rearrange("p h e -> p (h e)"), ident).then_inc(N["o2t_done"], 1)
                pe.wait_ge(N["o2t_out"], n + 1)
                pe.matmul(M[:, 0:D], o2_t[:, :], Lt("xo"), start=True, stop=True).then_inc(N["xo_done"], 1)

            def step_e(g):
                pe.wait_ge(N["x2_set"], upto(g, GROUP))
                pe.wait_ge(N["z_set"], upto(g, 1))
                for b in range(GROUP):
                    mm = pe.transpose(M[:, b * L:(b + 1) * L], z_g[:, b, :], ident)
                mm.then_inc(N["zt_done"], 1)
                pe.wait_ge(N["zt_out"], upto(g, 1))
                for b in range(GROUP):
                    mm = pe.matmul(M[:, b * EXPERTS:(b + 1) * EXPERTS], z_t[:, b * L:(b + 1) * L], Lt("gate"),
                                   start=True, stop=True)
                mm.then_inc(N["lg_done"], 1)

            pe.wait_ge(N["shapes16_set"], 1)
            schedule(step_a, step_b, step_c, step_s, step_t, step_o, step_e, pe.Fori)

            pe.wait_ge(N["hot_set"], 1)
            pe.wait_ge(N["before_set"], 1)
            flat = EXPERTS * TILES
            pe.matmul(M[:, 0:flat], S16("before"), hot16[:, :, :].rearrange("p e i -> p (e i)"),
                      start=True, stop=False)
            pe.matmul(M[:, 0:flat], S16("ones"), tiles_before[:, :, :].rearrange("p e i -> p (e i)"),
                      start=False, stop=True).then_inc(N["rank_done"], 1)

            def expert(j, par, first=False):
                e = 2 * j + par
                t_bank = (A, B)[par]
                h_banks = (SB, TB)[par]
                o_bank = (C, M)[par]
                pe.wait_ge(tok_in[par], 16 * (j + 1))
                for c in range(2):
                    mm = pe.transpose(t_bank[:, c * P:(c + 1) * P], tok[par][:, c, :], ident)
                mm.then_inc(N["tt_done"], 1)
                pe.wait_ge(N["tok_out"], e + 1)
                pe.wait_ge(we_in[par], 32 * (j + 1))
                pe.wait_ge(N["eo_set"], 2 * j)
                for i in range(HT):
                    mm = pe.matmul(h_banks[i // 2][:, (i % 2) * CAPACITY:(i % 2 + 1) * CAPACITY],
                                   wi_e[par][:, i * P:(i + 1) * P], tok_t[par][:, :], start=True, stop=True)
                    if i % 2:
                        mm.then_inc(N["h_done"], 1)
                for c in range(2):
                    for i in range(HT):
                        if c == 0 and i % 2 == 0:
                            pe.wait_ge(N["gelu_set"], 2 * e + i // 2 + 1)
                        mm = pe.matmul(o_bank[:, c * D:(c + 1) * D], hid[par][:, i, c * P:(c + 1) * P],
                                       wo_e[par][:, i, :], start=(i == 0), stop=(i == HT - 1))
                mm.then_inc(N["eo_done"], 1)

            expert(0, 0)
            expert(0, 1)
            with pe.Fori(1, EXPERTS // 2) as j:
                expert(j, 0)
                expert(j, 1)

        @block.scalar
        def _(act):
            act.wait_ge(N["early_in"], 16)
            act.preload_act_table_set(LN_EXP)

            def step_a(g):
                act.wait_ge(N["qk_done"], before(g, 1))
                act.wait_ge(N["xt1"], upto(g, 1))
                act.activation(xn1_t[:, :], A[:, 0:T], ACT.Identity).then_inc(N["xt1_out"], 1)
                act.wait_ge(N["z_done"], upto(g, 1))
                act.wait_ge(N["exp_set"], before(g, 1))
                act.activation(z_abs[:, :], C[:, 0:T], ACT.Abs, bias=E("b2")).then_inc(N["abs_set"], 1)
                act.wait_ge(N["abs_set"], upto(g, 1))
                act.activation(z_exp[:, :], z_abs[:, :], ACT.Exp, scale=-1.0).then_inc(N["exp_set"], 1)
                act.wait_ge(N["exp_set"], upto(g, 1))
                act.wait_ge(N["gk_set"], before(g, 1))
                act.activation(z_ln[:, :], z_exp[:, :], ACT.Ln, bias=1.0).then_inc(N["ln_set"], 1)
                for b in range(GROUP):
                    act.wait_ge(N["vg_done"], upto(g, GROUP, b + 1))
                    act.wait_ge(N["o_done"], before(g, 1))
                    act.activation(v_sb[:, b, :], (A, B)[b][:, 0:256], ACT.Identity).then_inc(N["v_set"], 1)
                act.wait_ge(N["scan_set"], upto(g, 1))
                act.wait_ge(N["gated"], before(g, 1))
                act.activation(e_pos[:, :], bcum[:, :], ACT.Exp, scale=1.0 / GATE_NORM)
                act.activation(e_neg[:, :], bcum[:, :], ACT.Exp, scale=-1.0 / GATE_NORM).then_inc(N["decay_set"], 1)
                for b in range(GROUP):
                    act.wait_ge(N["silu_set"], before(g, GROUP) + b)
                    act.activation(th[:, b, :], (A, B)[b][:, 256:512], ACT.Tanh, scale=0.5
                                   ).then_inc(N["tanh_set"], 1)
                act.preload_act_table_set(LN_EXP)

            def step_b(g):
                act.wait_ge(N["o_done"], upto(g, 1))
                act.wait_ge(N["ss_set"], before(g, 1))
                act.activation(o_sq[:, :, :].rearrange("p h e -> p (h e)"), C[:, :], ACT.Square
                               ).then_inc(N["sq_set"], 1)

            def step_c(g):
                j, par = g
                act.wait_ge(N["ogt_done"], upto(g, 1))
                act.wait_ge(N["wo_done"], before(g, 1))
                act.activation(og_t[:, :, :, :].rearrange("p b c t -> p (b c t)"), A[:, :], ACT.Identity
                               ).then_inc(N["ogt_out"], 1)
                last_par = 1 - par
                act.wait_ge(N["kv_done"], upto(g, 1))
                if par:
                    act.wait_ge(ks_in[last_par], 128 * (j + 1))
                    act.wait_ge(qs_in[last_par], 128 * (j + 1))
                else:
                    act.wait_ge(ks_in[last_par], 128 * j)
                    act.wait_ge(qs_in[last_par], 128 * j)
                act.activation(k_part[0][:, :], B[:, 0:GROUP * KEYS], ACT.Identity, bias=E("bk")
                               ).then_inc(N["k1_set"], 1)
                act.wait_ge(N["xt2"], upto(g, 1))
                act.wait_ge(N["q_done"], before(g, 1))
                act.activation(xn2_t[:, :], A[:, 0:T], ACT.Identity).then_inc(N["xt2_out"], 1)
                act.wait_ge(N["q_done"], upto(g, 1))
                act.activation(q_part[0][:, :], C[:, 0:T], ACT.Identity, bias=E("bq")).then_inc(N["q1_set"], 1)

            def step_t(g, b):
                n = before(g, GROUP) + b
                act.wait_ge(N["mt_done"], n + 1)
                act.wait_ge(N["t_done"], before(g, 8) + 4 * b)
                act.activation(max_t[:, :], M[:, 0:P // 2].bitcast(BF16), ACT.Identity).then_inc(N["mt_out"], 1)
                act.wait_ge(N["pv_done"], n)
                for u in range(4):
                    two, lo = u % 2, 4 * (u // 2)
                    act.wait_ge(N["t_done"], before(g, 8) + 4 * b + u + 1)
                    act.activation(prob[:, two, lo:lo + 4, :].rearrange("p a t -> p (a t)"), TB[two][0:KEYS, :],
                                   ACT.Exp, scale=float(DEPTH) ** -0.5).then_inc(N["exp2_set"], 1)

            def step_o(g, b):
                n = before(g, GROUP) + b
                act.wait_ge(N["o2t_done"], n + 1)
                act.activation(o2_t[:, :], M[:, 0:L], ACT.Identity, bias=E("bv")).then_inc(N["o2t_out"], 1)

            def step_e(g):
                act.wait_ge(N["zt_done"], upto(g, 1))
                act.activation(z_t[:, :], M[:, 0:T], ACT.Identity, bias=E("beta"), scale=E("gamma")
                               ).then_inc(N["zt_out"], 1)
                act.wait_ge(N["lg_done"], upto(g, 1))
                j, par = g
                at = (2 * j + par) * GROUP
                act.activation(logits[:, :, bass.ds(at, GROUP)],
                               M[:, 0:GROUP * EXPERTS].rearrange("p (b e) -> p e b", b=GROUP),
                               ACT.Identity).then_inc(N["lg_set"], 1)

            schedule(step_a, step_b, step_c, nothing, step_t, step_o, step_e, act.Fori)

            act.wait_ge(N["r_sub"], 1)
            act.activation(r_exp[:, :, :], r_diff[:, :, :], ACT.Exp).then_inc(N["r_expd"], 1)

            with act.Fori(0, EXPERTS // 2) as j:
                for par in range(2):
                    e = 2 * j + par
                    act.wait_ge(N["tt_done"], e + 1)
                    act.activation(tok_t[par][:, :], (A, B)[par][:, 0:CAPACITY], ACT.Identity, bias=E("beta"),
                                   scale=E("gamma")).then_inc(N["tok_out"], 1)
                    for i in range(2):
                        act.wait_ge(N["h_done"], 2 * e + i + 1)
                        act.activation(hid[par][:, 2 * i:2 * i + 2, :].rearrange("p a t -> p (a t)"),
                                       (SB, TB)[par][i][:, :], ACT.Gelu).then_inc(N["gelu_set"], 1)

        @block.vector
        def _(dve):
            dve.memset(back[:, :, :], 0.0).then_inc(N["cleared"], 1)
            dve.memset(k_first[:, :, :], 0.0)
            dve.memset(max_part[:, :, :, :], 0.0)
            for i in range(2):
                dve.memset(v_aug[i][:, :, :, :], 1.0).then_inc(N["v_ones"], 1)
            dve.wait_ge(N["v_ones"], 2)

            def norm_stats(src, st, mv, ve, s_stats, s_aggr, s_veps, g):
                for b in range(GROUP):
                    dve.bn_stats(st[:, b, :], src[:, b, :]).then_inc(s_stats, 1)
                dve.wait_ge(s_stats, upto(g, GROUP))
                dve.memset(pause[:, :], 0.0)
                for b in range(GROUP):
                    dve.bn_aggr(mv[:, b, :], st[:, b, :]).then_inc(s_aggr, 1)
                dve.wait_ge(s_aggr, upto(g, GROUP))
                dve.tensor_scalar(ve[:, :], mv[:, :, 1], EPS, None, ALU.add).then_inc(s_veps, 1)

            def step_a(g):
                j, par = g
                dve.wait_ge(x_in[par], 16 * (j + 1))
                norm_stats(x_g[par], st1, mv1, ve1, N["stats1"], N["aggr1"], N["veps1"], g)
                dve.wait_ge(N["rstd1"], upto(g, 1))
                for b in range(GROUP):
                    op = dve.tensor_scalar(xn1[:, b, :], x_g[par][:, b, :], mv1[:, b, 0:1], rs1[:, b:b + 1],
                                           ALU.subtract, ALU.mult)
                op.then_inc(N["xn1_set"], 1)
                dve.wait_ge(N["low_done"], upto(g, 1))
                dve.tensor_copy(low[:, :], B[0:RANK, 0:T]).then_inc(N["low_out"], 1)
                dve.wait_ge(N["abs_set"], upto(g, 1))
                dve.tensor_scalar(z_min[:, :], C[:, 0:T], E("b2"), 0.0, ALU.add, ALU.min).then_inc(N["min_set"], 1)
                dve.wait_ge(N["ln_set"], upto(g, 1))
                dve.wait_ge(N["min_set"], upto(g, 1))
                dve.tensor_tensor(gk[:, :], z_min[:, :], z_ln[:, :], ALU.subtract).then_inc(N["gk_set"], 1)
                dve.wait_ge(N["gk_set"], upto(g, 1))
                dve.tensor_tensor_scan(bcum[:, :], S("reset"), gk[:, :], 0.0, ALU.mult, ALU.add
                                       ).then_inc(N["scan_set"], 1)
                for b in range(GROUP):
                    dve.wait_ge(N["tanh_set"], upto(g, GROUP, b + 1))
                    dve.wait_ge(N["silu_n_set"], before(g, GROUP))
                    dve.scalar_tensor_tensor(silu2[:, b, :], th[:, b, :], 1.0, (A, B)[b][:, 256:512],
                                             ALU.add, ALU.mult).then_inc(N["silu_set"], 1)
                dve.wait_ge(N["decay_set"], upto(g, 1))
                dve.wait_ge(N["qk_done"], upto(g, 1))
                tk = lambda a: a.rearrange("p (b t) -> p b t", b=GROUP)
                dve.scalar_tensor_tensor(qg[:, :, :], tk(C[:, 0:T]), float(DK) ** -0.5, tk(e_pos[:, :]),
                                         ALU.mult, ALU.mult)
                dve.tensor_tensor(k_second[:, :, CHUNK:L], tk(C[:, T:2 * T])[:, :, CHUNK:L],
                                  tk(e_neg[:, :])[:, :, CHUNK:L], ALU.mult)
                dve.tensor_tensor(k_first[:, :, 0:CHUNK], tk(C[:, T:2 * T])[:, :, 0:CHUNK],
                                  tk(e_neg[:, :])[:, :, 0:CHUNK], ALU.mult).then_inc(N["kf_set"], 1)
                dve.wait_ge(N["kf_set"], upto(g, 1))
                dve.tensor_tensor(k_second[:, :, 0:CHUNK], k_first[:, :, 0:CHUNK],
                                  tk(e_pos[:, :])[:, :, CHUNK - 1:CHUNK].to_broadcast([P, GROUP, CHUNK]),
                                  ALU.mult).then_inc(N["gated"], 1)

            def step_b(g):
                for h in range(GLA_HEADS):
                    dve.wait_ge(N["at_done"], upto(g, GLA_HEADS, h + 1))
                    dve.tensor_tensor(att[h][:, :, :], (A, B)[h % 2][:, 0:T].rearrange("p (b t) -> p b t", b=GROUP),
                                      S("causal").unsqueeze(1).to_broadcast([P, GROUP, L]), ALU.mult
                                      ).then_inc(N["att_set"], 1)
                dve.wait_ge(N["sq_set"], upto(g, 1))
                dve.tensor_reduce(o_ss[:, :], o_sq[:, :, :], AX.X, ALU.add).then_inc(N["ss_set"], 1)
                dve.wait_ge(N["ss_set"], upto(g, 1))
                dve.tensor_scalar(o_ms[:, :], o_ss[:, :], 1.0 / DV, EPS, ALU.mult, ALU.add).then_inc(N["ms_set"], 1)
                dve.wait_ge(N["gate_set"], upto(g, 1))
                dve.tensor_tensor(og[:, :, :].rearrange("p b c -> p (b c)"), C[:, :],
                                  o_gate[:, :, :].rearrange("p b c -> p (b c)"), ALU.mult).then_inc(N["og_set"], 1)

            def step_c(g):
                j, par = g
                dve.wait_ge(N["wo_done"], upto(g, 1))
                dve.wait_ge(N["x1b_set"], before(g, 1))
                dve.tensor_tensor(x1[:, :, :].rearrange("p b d -> p (b d)"), B[:, 0:GROUP * D],
                                  x_g[par][:, :, :].rearrange("p b d -> p (b d)"), ALU.add
                                  ).then_inc(N["x1_set"], 1)
                dve.wait_ge(N["x1_set"], upto(g, 1))
                norm_stats(x1, st2, mv2, ve2, N["stats2"], N["aggr2"], N["veps2"], g)
                dve.wait_ge(N["rstd2"], upto(g, 1))
                for b in range(GROUP):
                    op = dve.tensor_scalar(xn2[:, b, :], x1[:, b, :], mv2[:, b, 0:1], rs2[:, b:b + 1],
                                           ALU.subtract, ALU.mult)
                op.then_inc(N["xn2_set"], 1)
                dve.wait_ge(N["k1_set"], upto(g, 1))
                dve.scalar_tensor_tensor(k_rest[:, :], B[:, 0:GROUP * KEYS], E("bk"), k_part[0][:, :],
                                         ALU.add, ALU.subtract).then_inc(N["krest_set"], 1)
                dve.tensor_copy(v_aug[par][:, :, :, 0:DEPTH],
                                B[0:KEYS, T:2 * T].rearrange("p (b h e) -> p b h e", b=GROUP, h=HEADS)
                                ).then_inc(N["vaug_set"], 1)
                dve.wait_ge(N["krest_set"], upto(g, 1))
                dve.tensor_copy(k_part[1][:, :], k_rest[:, :]).then_inc(N["k2_set"], 1)
                dve.wait_ge(N["k2_set"], upto(g, 1))
                dve.tensor_tensor(k_part[2][:, :], k_rest[:, :], k_part[1][:, :], ALU.subtract
                                  ).then_inc(N["k3_set"], 1)
                dve.wait_ge(N["q1_set"], upto(g, 1))
                dve.scalar_tensor_tensor(q_rest[:, :], C[:, 0:T], E("bq"), q_part[0][:, :],
                                         ALU.add, ALU.subtract).then_inc(N["qrest_set"], 1)
                dve.wait_ge(N["qrest_set"], upto(g, 1))
                dve.tensor_copy(q_part[1][:, :], q_rest[:, :]).then_inc(N["q2_set"], 1)
                dve.wait_ge(N["q2_set"], upto(g, 1))
                dve.tensor_tensor(q_part[2][:, :], q_rest[:, :], q_part[1][:, :], ALU.subtract
                                  ).then_inc(N["q3_set"], 1)

            def step_s(g, b):
                n = before(g, GROUP) + b
                dve.wait_ge(N["m2_set"], n)
                for u in range(4):
                    two, lo = u % 2, 4 * (u // 2)
                    dve.wait_ge(N["s_done"], before(g, 8) + 4 * b + u + 1)
                    dve.tensor_reduce(max_neg[:, two, lo:lo + 4],
                                      SB[two][:, 0:4 * KEYS].rearrange("p (a k) -> p a k", a=4),
                                      AX.X, ALU.max, negate=True).then_inc(N["max_set"], 1)
                dve.wait_ge(N["max_set"], before(g, 8) + 4 * b + 4)
                dve.wait_ge(N["mt_done"], n)
                dve.tensor_copy(max_part[:, :, 0, :], max_neg[:, :, :]).then_inc(N["m1_set"], 1)
                dve.wait_ge(N["m1_set"], n + 1)
                dve.tensor_tensor(max_part[:, :, 1, :], max_neg[:, :, :], max_part[:, :, 0, :], ALU.subtract
                                  ).then_inc(N["m2_set"], 1)

            def step_o(g, b):
                j, par = g
                n = before(g, GROUP) + b
                sums = M[:, 0:HEADS * (DEPTH + 1)].rearrange("p (h e) -> p h e", h=HEADS)
                dve.wait_ge(N["pv_done"], n + 1)
                dve.reciprocal(den[:, :], sums[:, :, DEPTH]).then_inc(N["den_set"], 1)
                dve.wait_ge(N["den_set"], n + 1)
                dve.tensor_tensor(o2[:, :, :], sums[:, :, 0:DEPTH],
                                  den[:, :].unsqueeze(2).to_broadcast([P, HEADS, DEPTH]), ALU.mult
                                  ).then_inc(N["o2_set"], 1)
                dve.wait_ge(N["xo_done"], n + 1)
                dve.wait_ge(N["x1b_set"], upto(g, 1))
                dve.tensor_tensor(x2[:, b, :], M[:, 0:D], x1b[par][:, b, :], ALU.add).then_inc(N["x2_set"], 1)

            def step_e(g):
                j, par = g
                at = (2 * j + par) * GROUP
                dve.wait_ge(N["x2_set"], upto(g, GROUP))
                norm_stats(x2, st3, mv3, ve3, N["stats3"], N["aggr3"], N["veps3"], g)
                dve.wait_ge(N["rstd3"], upto(g, 1))
                for b in range(GROUP):
                    op = dve.tensor_scalar(y[:, b, :], x2[:, b, :], mv3[:, b, 0:1], rs3[:, b:b + 1],
                                           ALU.subtract, ALU.mult)
                op.then_inc(N["y_set"], 1)
                dve.tensor_tensor(rr3[:, :], rs3[:, :], rs3[:, :], ALU.mult).then_inc(N["rr3_set"], 1)
                dve.wait_ge(N["rr3_set"], 2 * before(g, 1) + 1)
                dve.tensor_tensor(rr3[:, :], rr3[:, :], mv3[:, :, 1], ALU.mult).then_inc(N["rr3_set"], 1)
                dve.wait_ge(N["rr3_set"], 2 * before(g, 1) + 2)
                dve.tensor_scalar(ve4[:, :], rr3[:, :], EPS, None, ALU.add).then_inc(N["veps4"], 1)
                dve.wait_ge(N["y_set"], upto(g, 1))
                dve.tensor_tensor(xy_all[:, bass.ds(at, GROUP), :], x2[:, :, :], y[:, :, :], ALU.add
                                  ).then_inc(N["xy_set"], 1)
                dve.wait_ge(N["rstd4"], upto(g, 1))
                for b in range(GROUP):
                    op = dve.tensor_scalar(z_g[:, b, :], y[:, b, :], rs4[:, b:b + 1], None, ALU.mult)
                op.then_inc(N["z_set"], 1)
                dve.wait_ge(N["z_set"], upto(g, 1))
                dve.tensor_copy(z_all[:, bass.ds(at, GROUP), :], z_g[:, :, :]).then_inc(N["zall_set"], 1)

            dve.wait_ge(N["early_in"], 16)
            dve.wait_ge(N["shapes_in"], 16)
            dve.wait_ge(N["shapes16_in"], 16)
            dve.tensor_copy(shapes16[:, :], shapes_w[:, :]).then_inc(N["shapes16_set"], 1)
            dve.wait_ge(N["late_in"], 16)
            dve.tensor_scalar(half_gnorm[:, :], Lt("gnorm"), 0.5, None, ALU.mult).then_inc(N["half_gnorm_set"], 1)
            schedule(step_a, step_b, step_c, step_s, nothing, step_o, step_e, dve.Fori)

            chain = [0]

            def then(op):
                chain[0] += 1
                op.then_inc(N["r_chain"], 1)
                dve.wait_ge(N["r_chain"], chain[0])

            def each(a):
                return a[:, :].unsqueeze(1).to_broadcast([P, EXPERTS, TILES])

            def by_token(a):
                return a[:, :, :].rearrange("p e i -> p i e")

            cst = lambda n: S(n).rearrange("p (e i) -> p e i", e=EXPERTS)
            dve.wait_ge(N["lg_set"], GROUPS)
            then(dve.tensor_reduce(r_max[:, :], by_token(logits), AX.X, ALU.max))
            dve.tensor_tensor(r_diff[:, :, :], logits[:, :, :], each(r_max), ALU.subtract).then_inc(N["r_sub"], 1)
            then(dve.tensor_tensor(r_eq[:, :, :], logits[:, :, :], each(r_max), ALU.is_equal))
            then(dve.tensor_tensor(r_cand[:, :, :], r_eq[:, :, :], cst("order"), ALU.mult))
            then(dve.tensor_reduce(r_val[:, :], by_token(r_cand), AX.X, ALU.max))
            then(dve.tensor_tensor(one_hot[:, :, :], r_cand[:, :, :], each(r_val), ALU.is_equal))
            dve.tensor_copy(hot16[:, :, :], one_hot[:, :, :]).then_inc(N["hot_set"], 1)
            flat = lambda a: a[:, :, :].rearrange("p e i -> p (e i)")
            then(dve.tensor_tensor_scan(flat(r_incl), S("treset"), flat(one_hot), 0.0, ALU.mult, ALU.add))
            dve.tensor_tensor(tiles_before[:, :, :], r_incl[:, :, :], one_hot[:, :, :], ALU.subtract
                              ).then_inc(N["before_set"], 1)
            dve.wait_ge(N["r_expd"], 1)
            then(dve.tensor_reduce(r_sum[:, :], by_token(r_exp), AX.X, ALU.add))
            then(dve.reciprocal(r_inv[:, :], r_sum[:, :]))
            dve.wait_ge(N["rank_done"], 1)
            m_rank = M[:, 0:EXPERTS * TILES].rearrange("p (e i) -> p e i", e=EXPERTS)
            then(dve.tensor_tensor(r_a[:, :, :], m_rank, cst("ebase"), ALU.add))
            then(dve.tensor_tensor(r_b[:, :, :], r_a[:, :, :], one_hot[:, :, :], ALU.mult))
            then(dve.tensor_reduce(r_slot[:, :], by_token(r_b), AX.X, ALU.add))
            then(dve.scalar_tensor_tensor(flat(r_rank), M[:, 0:EXPERTS * TILES], float(CAPACITY), flat(one_hot),
                                          ALU.is_lt, ALU.mult))
            then(dve.tensor_reduce(r_keep[:, :], by_token(r_rank), AX.X, ALU.add))
            then(dve.tensor_tensor(weight[:, :], r_inv[:, :], r_keep[:, :], ALU.mult))
            then(dve.tensor_tensor(r_tmp[:, :], r_slot[:, :], r_keep[:, :], ALU.mult))
            dve.tensor_copy(from_slot[:, :], r_tmp[:, :]).then_inc(N["idx_set"], 1)
            then(dve.tensor_scalar(r_off[:, :], r_keep[:, :], -2.0 * SLOTS, 2.0 * SLOTS, ALU.mult, ALU.add))
            dve.tensor_tensor(to_slot[:, :], r_tmp[:, :], r_off[:, :], ALU.add).then_inc(N["idx_set"], 1)

            def expert_rows(j, par):
                dve.wait_ge(N["eo_done"], 2 * j + par + 1)
                dve.wait_ge(eo_stored[par], 16 * j)
                dve.tensor_copy(e_out[par][:, :, :].rearrange("p c d -> p (c d)"), (C, M)[par][:, 0:2 * D]
                                ).then_inc(N["eo_set"], 1)

            expert_rows(0, 0)
            expert_rows(0, 1)
            with dve.Fori(1, EXPERTS // 2) as j:
                expert_rows(j, 0)
                expert_rows(j, 1)

            dve.wait_ge(N["gathered"], 16 * TILES)
            for i in range(TILES):
                dve.scalar_tensor_tensor(result[:, i, :], back[:, i, :], weight[:, i:i + 1], xy_all[:, i, :],
                                         ALU.mult, ALU.add).then_inc(N["res_set"], 1)


def host_constants():
    s = np.arange(P)
    shape = np.zeros((P, SHAPE_W), np.float32)

    def put(name, value):
        a, b = SHAPE[name]
        shape[:, a:b] = value
    put("reset", (np.arange(T) % CHUNK != 0)[None, :])
    put("causal", s[:, None] <= s[None, :])
    put("mhalf", -0.5)
    e = np.repeat(np.arange(EXPERTS), TILES)
    put("ebase", (e * CAPACITY)[None, :])
    put("order", (EXPERTS - e)[None, :])
    put("treset", (np.arange(EXPERTS * TILES) % TILES != 0)[None, :])
    shape16 = np.zeros((P, SHAPE16_W), np.float32)

    def put16(name, value):
        a, b = SHAPE16[name]
        shape16[:, a:b] = value
    put16("ident", np.eye(P))
    pick = np.zeros((2, 8, PAIRS, PAIRS, KEYS), np.float32)
    for pair in range(PAIRS):
        pick[:, 0:2, pair, pair, :] = 1.0
    put16("pick", pick.reshape(P, PAIRS * KEYS))
    put16("before", s[:, None] < s[None, :])
    put16("ones", 1.0)
    return shape, shape16


def kernel(**inputs):
    import concourse.bacc as bacc
    from concourse.bass_utils import run_bass_kernel_spmd as run

    a = {k: np.asarray(v) for k, v in inputs.items()}
    order = np.arange(D).reshape(PAIRS, 2, DEPTH).transpose(1, 2, 0).reshape(-1)
    col = lambda v: v[:, None]
    early = np.zeros((P, EARLY_W), np.float32)
    late = np.zeros((P, LATE_W), np.float32)

    def put(dst, where, name, value):
        dst[:value.shape[0], where[name][0]:where[name][1]] = value
    put(early, EARLY, "ident", np.eye(P, dtype=np.float32))
    put(early, EARLY, "w1", a["L0_attn_gk_w1"])
    put(early, EARLY, "w2", a["L0_attn_gk_w2"])
    put(early, EARLY, "b2", col(a["L0_attn_gk_b2"]))
    put(early, EARLY, "bq", col(a["L0_xattn_bq"][order]))
    put(early, EARLY, "bk", col(a["L0_xattn_bk"][order]))
    put(early, EARLY, "bv", col(a["L0_xattn_bv"]))
    put(early, EARLY, "gamma", col(a["L0_ffn_ln_gamma"]))
    put(early, EARLY, "beta", col(a["L0_ffn_ln_beta"]))
    put(early, EARLY, "vg", np.concatenate([a["L0_attn_Wv"], a["L0_attn_Wg"]], axis=1))
    put(early, EARLY, "q", a["L0_attn_Wq"])
    put(early, EARLY, "k", a["L0_attn_Wk"])
    put(late, LATE, "wo", a["L0_attn_Wo"].reshape(2, P, D).transpose(1, 0, 2).reshape(P, 2 * D))
    put(late, LATE, "xk", a["L0_xattn_wk"].T[:, order])
    put(late, LATE, "xv", a["L0_xattn_wv"].T)
    put(late, LATE, "xq", a["L0_xattn_wq"].T[:, order])
    put(late, LATE, "xo", a["L0_xattn_wo"].T)
    put(late, LATE, "gate", a["L0_ffn_gate_weight"].T)
    put(late, LATE, "gnorm", np.tile(a["L0_attn_g_norm_w"], (P, GLA_HEADS)))
    put(late, LATE, "bo", np.tile(a["L0_xattn_bo"], (P, 1)))
    shape, shape16 = host_constants()
    arrays = {
        "x": a["x"].transpose(1, 0, 2),
        "ctx_t": a["ctx_1024"].transpose(2, 0, 1),
        "early": early, "late": late, "shape": shape, "shape16": shape16,
        "wi": a["L0_ffn_wi"].transpose(1, 0, 2),
        "wo": a["L0_ffn_wo"].reshape(EXPERTS * HT, P, D).transpose(1, 0, 2),
    }
    arrays = {k: np.ascontiguousarray(v) for k, v in arrays.items()}
    nc = bacc.Bacc("TRN2", target_bir_lowering=False, num_devices=1)
    ins = {k: nc.dram_tensor(f"in_{k}", v.shape, mybir.dt.from_np(v.dtype), kind="ExternalInput").ap()
           for k, v in arrays.items()}
    out = nc.dram_tensor("out", (P, SEQS, D), F32, kind="ExternalOutput").ap()
    slots_in = nc.dram_tensor("slots_in", (SLOTS, D), F32, kind="Internal").ap()
    slots_out = nc.dram_tensor("slots_out", (SLOTS, D), F32, kind="Internal").ap()
    build(nc, ins["x"], ins["ctx_t"], ins["early"], ins["late"], ins["shape"], ins["shape16"], ins["wi"], ins["wo"],
          out, slots_in, slots_out)
    r = run(nc, [{f"in_{k}": v for k, v in arrays.items()}], core_ids=[0])
    return np.ascontiguousarray(r.results[0]["out"].transpose(1, 0, 2))
```

```python
from contextlib import ExitStack

import numpy as np

import concourse.bass as bass
from concourse import mybir

F32 = mybir.dt.float32
BF16 = mybir.dt.bfloat16
U32 = mybir.dt.uint32
ALU = mybir.AluOpType
ACT = mybir.ActivationFunctionType
AX = mybir.AxisListType

P = 128
SEQS, L, D = 16, 128, 128
KEYS = 120
GROUP = 2
GROUPS = SEQS // GROUP
assert GROUPS == 8
T = GROUP * L
GLA_HEADS, DK, DV, CHUNK = 4, 32, 64, 64
RANK = 16
HEADS, DEPTH = 16, 8
PAIRS = HEADS // 2
TILE = 32
PARTS = 3
Q_PART = (0, 0, 0, 1, 1, 1, 2, 2)
K_PART = (0, 1, 2, 0, 1, 2, 0, 1)
EXPERTS, HIDDEN = 8, 512
CAPACITY = 256
SLOTS = EXPERTS * CAPACITY
TILES = SEQS
HT = HIDDEN // P
ORDER = """r0 s0 a0 b0 c0 r1 m0 a1 b1 r2 t00 c1 s1 x a2 r3 t01 b2 e0 c2 t02 a3 b3 e1 t03 m1 c3 a4 t10 e2 b4
    t11 e3 c4 a45 t12 e4 a5 o0 b5 t13 o1 o2 o3""".split()
AHEAD = {"a": 3, "b": 2, "x": 2, "c": 1, "s": 0, "m": 0, "t": 0, "o": 0, "r": -1, "e": -1}
EPS = 1e-5
GATE_NORM = 16.0
LN_EXP = "natural_log_exp_and_others"


def layout(parts):
    at, out = 0, {}
    for name, width in parts:
        out[name] = (at, at + width)
        at += width
    return out, at


EARLY, EARLY_W = layout([("ident", P), ("w1", RANK), ("w2", D), ("b2", 1), ("bq", 1), ("bk", 1), ("bv", 1),
                         ("gamma", 1), ("beta", 1), ("vg", 512), ("q", D), ("k", D)])
LATE, LATE_W = layout([("wo", 2 * D), ("xk", D), ("xv", D), ("xq", D), ("xo", D), ("gate", EXPERTS),
                       ("gnorm", GLA_HEADS * DV), ("bo", D)])
SHAPE, SHAPE_W = layout([("reset", T), ("causal", P), ("mhalf", 8), ("ebase", EXPERTS * TILES),
                         ("order", EXPERTS * TILES), ("treset", EXPERTS * TILES)])
SHAPE16, SHAPE16_W = layout([("ident", P), ("pick", PAIRS * KEYS), ("before", P), ("ones", P)])


def build(nc, x, ctx_t, early_d, late_d, shape_d, shape16_d, wi_d, wo_d, out, slots_in, slots_out):
    with ExitStack() as stack:
        def sb(name, shape, dt=F32):
            return stack.enter_context(nc.sbuf_tensor(name, shape, dt))

        def bank(name):
            return stack.enter_context(nc.psum_tensor(name, [P, 512], F32))

        def sem(name):
            return stack.enter_context(nc.semaphore(name))

        early = sb("early", [P, EARLY_W])
        late = sb("late", [P, LATE_W])
        shapes = sb("shapes", [P, SHAPE_W])
        shapes_w = sb("shapes_w", [P, SHAPE16_W])
        shapes16 = sb("shapes16", [P, SHAPE16_W], BF16)

        def E(name):
            return early[:, EARLY[name][0]:EARLY[name][1]]

        def Lt(name):
            return late[:, LATE[name][0]:LATE[name][1]]

        def S(name):
            return shapes[:, SHAPE[name][0]:SHAPE[name][1]]

        def S16(name):
            return shapes16[:, SHAPE16[name][0]:SHAPE16[name][1]]

        pick = S16("pick").rearrange("p (a k) -> p a k", a=PAIRS)
        half_gnorm = sb("half_gnorm", [P, GLA_HEADS * DV])

        x_all = sb("x_all", [P, SEQS, D])
        xy_all = sb("xy_all", [P, SEQS, D])
        z_all = sb("z_all", [P, SEQS, D])
        logits = sb("logits", [P, EXPERTS, TILES])

        ctx_g = [sb(f"ctx_g{i}", [P, GROUP, KEYS]) for i in range(2)]
        st1 = sb("st1", [P, GROUP, 6])
        pause = sb("pause", [P, 1])
        mv1 = sb("mv1", [P, GROUP, 2])
        ve1 = sb("ve1", [P, GROUP])
        rs1 = sb("rs1", [P, GROUP])
        xn1 = sb("xn1", [P, GROUP, D])
        xn1_t = sb("xn1_t", [P, T])
        low = sb("low", [RANK, T])
        z_abs = sb("z_abs", [P, T])
        z_exp = sb("z_exp", [P, T])
        z_ln = sb("z_ln", [P, T])
        z_min = sb("z_min", [P, T])
        gk = sb("gk", [P, T])
        bcum = sb("bcum", [P, T])
        e_pos = sb("e_pos", [P, T])
        e_neg = sb("e_neg", [P, T])
        qg = [sb(f"qg{i}", [P, GROUP, L]) for i in range(2)]
        k_first = [sb(f"k_first{i}", [P, GROUP, L]) for i in range(2)]
        k_second = [sb(f"k_second{i}", [P, GROUP, L]) for i in range(2)]
        v_sb = [sb(f"v_sb{i}", [P, GROUP, GLA_HEADS * DV]) for i in range(2)]
        th = sb("th", [P, GROUP, GLA_HEADS * DV])
        silu2 = sb("silu2", [P, GROUP, GLA_HEADS * DV])
        silu_n = [sb(f"silu_n{i}", [P, GROUP, GLA_HEADS * DV]) for i in range(2)]
        att = [sb(f"att{h}", [P, GROUP, L]) for h in range(GLA_HEADS)]
        o_sq = sb("o_sq", [P, GROUP * GLA_HEADS, DV])
        o_ss = sb("o_ss", [P, GROUP * GLA_HEADS])
        o_ms = sb("o_ms", [P, GROUP * GLA_HEADS])
        o_rs = sb("o_rs", [P, GROUP * GLA_HEADS])
        o_gate = sb("o_gate", [P, GROUP, GLA_HEADS * DV])
        og = [sb(f"og{i}", [P, GROUP, GLA_HEADS * DV]) for i in range(2)]
        og_t = sb("og_t", [P, GROUP, 2, L])
        x1 = sb("x1", [P, GROUP, D])
        x1b = [sb(f"x1b{i}", [P, GROUP, D]) for i in range(2)]
        st2 = sb("st2", [P, GROUP, 6])
        mv2 = sb("mv2", [P, GROUP, 2])
        ve2 = sb("ve2", [P, GROUP])
        rs2 = sb("rs2", [P, GROUP])
        xn2 = sb("xn2", [P, GROUP, D])
        xn2_t = sb("xn2_t", [P, T])
        k_part = [sb(f"k_part{i}", [P, GROUP * KEYS], BF16) for i in range(PARTS)]
        q_part = [sb(f"q_part{i}", [P, T], BF16) for i in range(PARTS)]
        k_rest = sb("k_rest", [P, GROUP * KEYS])
        q_rest = sb("q_rest", [P, T])
        ks = [sb(f"ks{i}", [P, PAIRS, GROUP * KEYS], BF16) for i in range(2)]
        qs = [sb(f"qs{i}", [P, PAIRS, T], BF16) for i in range(2)]
        v_aug = [sb(f"v_aug{i}", [KEYS, GROUP, HEADS, TILE]) for i in range(2)]

        max_neg = sb("max_neg", [P, 2, PAIRS])
        max_part = sb("max_part", [P, 2, 8, PAIRS], BF16)
        max_t = sb("max_t", [P, P], BF16)
        prob = [sb(f"prob{i}", [KEYS, 4, 4, L]) for i in range(GROUP)]
        pv = sb("pv", [P, 4 * L])
        den = sb("den", [P, HEADS])
        o2 = sb("o2", [P, HEADS, DEPTH])
        o2_t = sb("o2_t", [P, L])
        x2 = [sb(f"x2_{i}", [P, GROUP, D]) for i in range(2)]
        st3 = sb("st3", [P, GROUP, 6])
        mv3 = sb("mv3", [P, GROUP, 2])
        ve3 = sb("ve3", [P, GROUP])
        rs3 = sb("rs3", [P, GROUP])
        rr3 = sb("rr3", [P, GROUP])
        ve4 = sb("ve4", [P, GROUP])
        rs4 = sb("rs4", [P, GROUP])
        y = sb("y", [P, GROUP, D])
        z_g = sb("z_g", [P, GROUP, D])
        z_t = sb("z_t", [P, T])

        def rt(name, dt=F32):
            return sb(name, [P, EXPERTS, TILES], dt)

        def tt_(name, dt=F32):
            return sb(name, [P, TILES], dt)

        r_max, r_val, r_sum, r_inv, r_slot, r_keep, r_off, r_tmp, weight = [
            tt_(n) for n in ("r_max", "r_val", "r_sum", "r_inv", "r_slot", "r_keep", "r_off", "r_tmp", "weight")]
        r_eq, r_cand, one_hot, r_diff, r_exp, r_incl, r_rank, r_a, r_b = [
            rt(n) for n in ("r_eq", "r_cand", "one_hot", "r_diff", "r_exp", "r_incl", "r_rank", "r_a", "r_b")]
        hot16 = rt("hot16", BF16)
        tiles_before = rt("tiles_before", BF16)
        to_slot = tt_("to_slot", U32)
        from_slot = tt_("from_slot", U32)

        wi_e = [sb(f"wi_e{i}", [P, HIDDEN]) for i in range(2)]
        wo_e = [sb(f"wo_e{i}", [P, HT, D]) for i in range(2)]
        tok = [sb(f"tok{i}", [P, 2, D]) for i in range(2)]
        tok_t = [sb(f"tok_t{i}", [P, CAPACITY]) for i in range(2)]
        hid = [sb(f"hid{i}", [P, HT, CAPACITY]) for i in range(2)]
        e_out = [sb(f"e_out{i}", [P, 2, D]) for i in range(2)]
        back = sb("back", [P, SEQS, D])
        result = sb("result", [P, SEQS, D])

        A, B, C, K, M = [bank(f"bank_{n}") for n in "abckm"]
        SB = [bank("bank_s0"), bank("bank_s1")]
        TB = bank("bank_t")

        names = """early_in late_in shapes_in shapes16_in shapes16_set zeroed cleared half_gnorm_set v_ones
            stats1 aggr1 veps1 rstd1 xn1_set xt1 xt1_out low_done low_out z_done abs_set exp_set ln_set min_set
            gk_set scan_set decay_set vg_done v_set tanh_set silu_set silu_n_set qk_done qg_set kf_set gated
            at_done att_set o_done sq_set ss_set ms_set rs_set gate_set og_set ogt_done ogt_out wo_done x1_set
            x1b_set stats2 aggr2 veps2 rstd2 xn2_set xt2 xt2_out q_done kv_done k1_set krest_set k2_set k3_set
            vaug_set q1_set qrest_set q2_set q3_set
            s_done max_set m1_set m2_set mt_done mt_out t_done exp2_set pv_done pv_out pvt_done den_set o2_set o2t_done o2t_out
            xo_done x2_set stats3 aggr3 veps3 rstd3 rr3_set veps4 rstd4 y_set xy_set z_set zall_set zt_done
            zt_out lg_done lg_set
            r_chain r_sub r_expd hot_set before_set rank_done idx_set scattered gathered
            tt_done tok_out h_done gelu_set eo_done eo_set res_set stored""".split()
        N = {n: sem(n) for n in names}
        x_in = [sem(f"x_in{i}") for i in range(3)]
        ctx_in = [sem("ctx_in0"), sem("ctx_in1")]
        ks_in = [sem("ks_in0"), sem("ks_in1")]
        qs_in = [sem("qs_in0"), sem("qs_in1")]
        we_in = [sem("we_in0"), sem("we_in1")]
        tok_in = [sem("tok_in0"), sem("tok_in1")]
        eo_stored = [sem("eo_stored0"), sem("eo_stored1")]

        def upto(g, n, k=None):
            j, par = g
            return (2 * j + par) * n + (n if k is None else k)

        def before(g, n):
            j, par = g
            return (2 * j + par) * n

        def is_first(g):
            return isinstance(g[0], int) and g == (0, 0)

        def wait_after(eng, signal, g, n, less):
            count = before(g, n) - less
            if not isinstance(count, int) or count > 0:
                eng.wait_ge(signal, count)

        def schedule(steps, Fori):
            def stage(group_of):
                for name in ORDER:
                    g = group_of(AHEAD[name[0]])
                    if g is not None and name in steps:
                        steps[name](g)

            def fixed(n):
                stage(lambda ahead: divmod(n + ahead, 2) if 0 <= n + ahead < GROUPS else None)

            for n in range(-4, 1):
                fixed(n)
            with Fori(0, 2) as j:
                for n in (1, 2):
                    stage(lambda ahead: (j + (n + ahead) // 2, (n + ahead) % 2) if n + ahead < GROUPS else None)
            for n in range(5, GROUPS + 1):
                fixed(n)

        block = stack.enter_context(nc.Block())

        @block.sync
        def _(sp):
            def x_ctx(g):
                j, par = g
                wait_after(sp, N["kv_done"], g, 1, 1)
                sp.dma_start(ctx_g[par][:, :, :], ctx_t[:, bass.ds((2 * j + par) * GROUP, GROUP), :]
                             ).then_inc(ctx_in[par], 16)

            def load_x(i, first, last):
                sp.dma_start(x_all[:, first:last, :], x[:, first:last, :]).then_inc(x_in[i], 16)

            def c2(g):
                par = g[1]
                sp.wait_ge(N["k3_set"], upto(g, 1))
                wait_after(sp, N["t_done"], g, 8, 8)
                for c in range(8):
                    sp.dma_start(ks[par][c::8, :, :], k_part[K_PART[c]][:, :]).then_inc(ks_in[par], 16)

            def c4(g):
                par = g[1]
                sp.wait_ge(N["q3_set"], upto(g, 1))
                for c in range(8):
                    sp.dma_start(qs[par][c::8, :, :], q_part[Q_PART[c]][:, :]).then_inc(qs_in[par], 16)

            load_x(0, 0, GROUP)
            sp.dma_start(early[:, :], early_d).then_inc(N["early_in"], 16)
            load_x(1, GROUP, 2 * GROUP)
            sp.dma_start(shapes[:, :], shape_d).then_inc(N["shapes_in"], 16)
            sp.dma_start(late[:, :], late_d).then_inc(N["late_in"], 16)
            sp.dma_start(shapes_w[:, :], shape16_d).then_inc(N["shapes16_in"], 16)
            load_x(2, 2 * GROUP, SEQS)
            sp.wait_ge(N["cleared"], 1)
            sp.dma_start(slots_in.rearrange("(t p) d -> p t d", p=P), back[:, :, :]).then_inc(N["zeroed"], 16)
            schedule({"x": x_ctx, "c2": c2, "c4": c4}, sp.Fori)

            def weights(j, par):
                e = 2 * j + par
                sp.dma_start(wi_e[par][:, :], wi_d[:, bass.ds(e, 1), :].rearrange("p o n -> p (o n)")
                             ).then_inc(we_in[par], 16)
                sp.dma_start(wo_e[par][:, :, :], wo_d[:, bass.ds(e * HT, HT), :]).then_inc(we_in[par], 16)

            def tokens(j, par):
                e = 2 * j + par
                sp.dma_start(tok[par][:, :, :],
                             slots_in.rearrange("(t p) d -> p t d", p=P)[:, bass.ds(e * 2, 2), :]
                             ).then_inc(tok_in[par], 16)

            def store(j, par):
                e = 2 * j + par
                sp.wait_ge(N["eo_set"], e + 1)
                sp.dma_start(slots_out.rearrange("(t p) d -> p t d", p=P)[:, bass.ds(e * 2, 2), :],
                             e_out[par][:, :, :]).then_inc(eo_stored[par], 16)

            weights(0, 0)
            weights(0, 1)
            sp.wait_ge(N["scattered"], 16 * TILES)
            tokens(0, 0)
            tokens(0, 1)
            with sp.Fori(0, EXPERTS // 2 - 1) as j:
                for par in range(2):
                    e = sp.snap(2 * j + par)
                    made = sp.snap(e + 1)
                    sp.wait_ge(N["tt_done"], made)
                    tokens(j + 1, par)
                    sp.wait_ge(N["eo_done"], made)
                    weights(j + 1, par)
                    store(j, par)
            for par in range(2):
                store(EXPERTS // 2 - 1, par)
            sp.wait_ge(eo_stored[0], 16 * (EXPERTS // 2))
            sp.wait_ge(eo_stored[1], 16 * (EXPERTS // 2))
            for i in range(4):
                sp.wait_ge(N["res_set"], 4 * (i + 1))
                sp.dma_start(out[:, 4 * i:4 * i + 4, :], result[:, 4 * i:4 * i + 4, :]).then_inc(N["stored"], 16)
            sp.wait_ge(N["stored"], 64)

        @block.gpsimd
        def _(pool):
            pool.wait_ge(N["shapes_in"], 16)
            pool.wait_ge(N["late_in"], 16)
            mh = S("mhalf")

            def a0(g):
                pool.wait_ge(N["veps1"], upto(g, 1))
                pool.tensor_tensor(rs1[:, :], ve1[:, :], mh[:, 0:GROUP], ALU.pow).then_inc(N["rstd1"], 1)

            def a3(g):
                pool.wait_ge(N["ln_set"], upto(g, 1))
                pool.wait_ge(N["min_set"], upto(g, 1))
                pool.tensor_tensor(gk[:, :], z_min[:, :], z_ln[:, :], ALU.subtract).then_inc(N["gk_set"], 1)

            def a5(g):
                par = g[1]
                if is_first(g):
                    pool.wait_ge(N["half_gnorm_set"], 1)
                for b in range(GROUP):
                    pool.wait_ge(N["silu_set"], upto(g, GROUP, b + 1))
                    pool.tensor_tensor(silu_n[par][:, b, :], silu2[:, b, :], half_gnorm[:, :], ALU.mult
                                       ).then_inc(N["silu_n_set"], 1)

            def b4(g):
                pool.wait_ge(N["ms_set"], upto(g, 1))
                pool.tensor_tensor(o_rs[:, :], o_ms[:, :], mh[:, 0:GROUP * GLA_HEADS], ALU.pow
                                   ).then_inc(N["rs_set"], 1)

            def b5(g):
                par = g[1]
                pool.wait_ge(N["rs_set"], upto(g, 1))
                pool.wait_ge(N["silu_n_set"], upto(g, GROUP))
                pool.tensor_tensor(o_gate[:, :, :].rearrange("p b (h e) -> p (b h) e", h=GLA_HEADS),
                                   silu_n[par][:, :, :].rearrange("p b (h e) -> p (b h) e", h=GLA_HEADS),
                                   o_rs[:, :].unsqueeze(2).to_broadcast([P, GROUP * GLA_HEADS, DV]),
                                   ALU.mult).then_inc(N["gate_set"], 1)

            def c1(g):
                par = g[1]
                pool.wait_ge(N["veps2"], upto(g, 1))
                pool.tensor_tensor(rs2[:, :], ve2[:, :], mh[:, 0:GROUP], ALU.pow).then_inc(N["rstd2"], 1)
                wait_after(pool, N["x2_set"], g, GROUP, GROUP)
                pool.tensor_tensor(x1b[par][:, :, :], x1[:, :, :],
                                   Lt("bo").unsqueeze(1).to_broadcast([P, GROUP, D]), ALU.add
                                   ).then_inc(N["x1b_set"], 1)

            def c2(g):
                pool.wait_ge(N["k2_set"], upto(g, 1))
                pool.tensor_tensor(k_part[2][:, :], k_rest[:, :], k_part[1][:, :], ALU.subtract
                                   ).then_inc(N["k3_set"], 1)

            def e0(g):
                pool.wait_ge(N["veps3"], upto(g, 1))
                pool.tensor_tensor(rs3[:, :], ve3[:, :], mh[:, 0:GROUP], ALU.pow).then_inc(N["rstd3"], 1)

            def e1(g):
                j, par = g
                at = (2 * j + par) * GROUP
                pool.wait_ge(N["veps4"], upto(g, 1))
                pool.tensor_tensor(rs4[:, :], ve4[:, :], mh[:, 0:GROUP], ALU.pow).then_inc(N["rstd4"], 1)
                pool.wait_ge(N["y_set"], upto(g, 1))
                pool.tensor_tensor(xy_all[:, bass.ds(at, GROUP), :], x2[par][:, :, :], y[:, :, :], ALU.add
                                   ).then_inc(N["xy_set"], 1)

            def e2(g):
                j, par = g
                at = (2 * j + par) * GROUP
                pool.wait_ge(N["z_set"], upto(g, 1))
                pool.tensor_copy(z_all[:, bass.ds(at, GROUP), :], z_g[:, :, :]).then_inc(N["zall_set"], 1)

            schedule({"a0": a0, "a3": a3, "a5": a5, "b4": b4, "b5": b5, "c1": c1, "c2": c2,
                      "e0": e0, "e1": e1, "e2": e2}, pool.Fori)

            pool.wait_ge(N["idx_set"], 2)
            pool.wait_ge(N["zall_set"], GROUPS)
            pool.wait_ge(N["zeroed"], 16)
            for i in range(TILES):
                pool.indirect_dma_start(out=slots_in, out_offset=bass.IndirectOffsetOnAxis(ap=to_slot[:, i:i + 1], axis=0),
                                        in_=z_all[:, i, :], in_offset=None, bounds_check=SLOTS - 1,
                                        oob_is_err=False).then_inc(N["scattered"], 16)
            pool.wait_ge(eo_stored[0], 16 * (EXPERTS // 2))
            pool.wait_ge(eo_stored[1], 16 * (EXPERTS // 2))
            for i in range(TILES):
                pool.indirect_dma_start(out=back[:, i, :], out_offset=None, in_=slots_out,
                                        in_offset=bass.IndirectOffsetOnAxis(ap=from_slot[:, i:i + 1], axis=0)
                                        ).then_inc(N["gathered"], 16)

        @block.tensor
        def _(pe):
            pe.wait_ge(N["early_in"], 16)
            ident = E("ident")

            def a1(g):
                pe.wait_ge(N["silu_set"], before(g, GROUP))
                pe.wait_ge(N["xn1_set"], upto(g, 1))
                for b in range(GROUP):
                    mm = pe.transpose(A[:, b * L:(b + 1) * L], xn1[:, b, :], ident)
                mm.then_inc(N["xt1"], 1)

            def a2(g):
                pe.wait_ge(N["xt1_out"], upto(g, 1))
                pe.matmul(B[0:RANK, 0:T], E("w1"), xn1_t[:, :], start=True, stop=True).then_inc(N["low_done"], 1)

            def a3(g):
                pe.wait_ge(N["low_out"], upto(g, 1))
                pe.matmul(A[:, 0:T], E("w2")[0:RANK, :], low[:, :], start=True, stop=True).then_inc(N["z_done"], 1)
                pe.matmul(B[:, 0:T], E("q"), xn1_t[:, :], start=True, stop=True)
                pe.matmul(B[:, T:2 * T], E("k"), xn1_t[:, :], start=True, stop=True).then_inc(N["qk_done"], 1)

            def a5(g):
                pe.wait_ge(N["abs_set"], upto(g, 1))
                pe.wait_ge(N["min_set"], upto(g, 1))
                pe.matmul(A[:, :], xn1_t[:, 0:L], E("vg"), start=True, stop=True).then_inc(N["vg_done"], 1)
                pe.wait_ge(N["gated"], upto(g, 1))
                pe.matmul(B[:, :], xn1_t[:, L:T], E("vg"), start=True, stop=True).then_inc(N["vg_done"], 1)

            def b_scores(h):
                def piece(g):
                    par = g[1]
                    rows = slice(DK * h, DK * (h + 1))
                    if h == 0:
                        pe.wait_ge(N["og_set"], before(g, 1))
                        pe.wait_ge(N["gated"], upto(g, 1))
                    else:
                        pe.wait_ge(N["att_set"], upto(g, GLA_HEADS, h))
                    for b in range(GROUP):
                        pe.matmul(C[:, b * L:b * L + CHUNK], k_first[par][rows, b, :], qg[par][rows, b, 0:CHUNK],
                                  start=True, stop=True)
                        mm = pe.matmul(C[:, b * L + CHUNK:(b + 1) * L], k_second[par][rows, b, :],
                                       qg[par][rows, b, CHUNK:L], start=True, stop=True)
                    mm.then_inc(N["at_done"], 1)
                return piece

            def b4(g):
                par = g[1]
                pe.wait_ge(N["v_set"], upto(g, GROUP))
                pe.wait_ge(N["att_set"], upto(g, GLA_HEADS))
                for b in range(GROUP):
                    for h in range(GLA_HEADS):
                        at = (b * GLA_HEADS + h) * DV
                        mm = pe.matmul(C[:, at:at + DV], att[h][:, b, :], v_sb[par][:, b, h * DV:(h + 1) * DV],
                                       start=True, stop=True)
                mm.then_inc(N["o_done"], 1)

            def c0(g):
                par = g[1]
                pe.wait_ge(N["qrest_set"], before(g, 1))
                pe.wait_ge(N["og_set"], upto(g, 1))
                for b in range(GROUP):
                    for c in range(2):
                        at = (2 * b + c) * L
                        mm = pe.transpose(K[:, at:at + L], og[par][:, b, c * P:(c + 1) * P], ident)
                mm.then_inc(N["ogt_done"], 1)

            def c1(g):
                if is_first(g):
                    pe.wait_ge(N["late_in"], 16)
                pe.wait_ge(N["ogt_out"], upto(g, 1))
                for b in range(GROUP):
                    for c in range(2):
                        mm = pe.matmul(K[:, b * D:(b + 1) * D], og_t[:, b, c, :],
                                       Lt("wo")[:, c * D:(c + 1) * D], start=(c == 0), stop=(c == 1))
                mm.then_inc(N["wo_done"], 1)

            def c2(g):
                j, par = g
                pe.wait_ge(ctx_in[par], 16 * (j + 1))
                pe.wait_ge(N["x1_set"], upto(g, 1))
                pe.matmul(K[:, 0:GROUP * KEYS], Lt("xk"), ctx_g[par][:, :, :].rearrange("p b k -> p (b k)"),
                          start=True, stop=True)
                for b in range(GROUP):
                    mm = pe.matmul(K[0:KEYS, T + b * D:T + (b + 1) * D], ctx_g[par][:, b, :], Lt("xv"),
                                   start=True, stop=True)
                mm.then_inc(N["kv_done"], 1)

            def c3(g):
                pe.wait_ge(N["vaug_set"], upto(g, 1))
                pe.wait_ge(N["krest_set"], upto(g, 1))
                pe.wait_ge(N["xn2_set"], upto(g, 1))
                for b in range(GROUP):
                    mm = pe.transpose(K[:, b * L:(b + 1) * L], xn2[:, b, :], ident)
                mm.then_inc(N["xt2"], 1)

            def c4(g):
                pe.wait_ge(N["xt2_out"], upto(g, 1))
                pe.matmul(K[:, 0:T], Lt("xq"), xn2_t[:, :], start=True, stop=True).then_inc(N["q_done"], 1)

            def heads(u):
                return u % 2, slice(64 * (u % 2), 64 * (u % 2) + 64), range(4 * (u // 2), 4 * (u // 2) + 4)

            def s(b):
                def piece(g):
                    j, par = g
                    if b == 0:
                        pe.wait_ge(ks_in[par], 128 * (j + 1))
                        pe.wait_ge(qs_in[par], 128 * (j + 1))
                    for u in range(4):
                        two, rows, pairs = heads(u)
                        wait_after(pe, N["max_set"], g, 8, 1 - 4 * b - u)
                        for i, pair in enumerate(pairs):
                            mm = pe.matmul(SB[two][:, i * KEYS:(i + 1) * KEYS],
                                           qs[par][rows, pair, b * L:(b + 1) * L],
                                           ks[par][rows, pair, b * KEYS:(b + 1) * KEYS], start=True, stop=True)
                        mm.then_inc(N["s_done"], 1)
                return piece

            def m(b):
                def piece(g):
                    wait_after(pe, N["exp2_set"], g, 8, -4 * b)
                    pe.wait_ge(N["m2_set"], before(g, GROUP) + b + 1)
                    pe.transpose(TB[:, 0:P // 2].bitcast(BF16), max_part[:, :, :, :].rearrange("p w c a -> p (w c a)"),
                                 S16("ident")).then_inc(N["mt_done"], 1)
                return piece

            def t(b, u):
                def piece(g):
                    par = g[1]
                    two, rows, pairs = heads(u)
                    if u == 0:
                        pe.wait_ge(N["mt_out"], before(g, GROUP) + b + 1)
                    else:
                        pe.wait_ge(N["exp2_set"], before(g, 8) + 4 * b + u)
                    for i, pair in enumerate(pairs):
                        pe.matmul(TB[0:KEYS, i * L:(i + 1) * L], ks[par][rows, pair, b * KEYS:(b + 1) * KEYS],
                                  qs[par][rows, pair, b * L:(b + 1) * L], start=True, stop=False)
                        mm = pe.matmul(TB[0:KEYS, i * L:(i + 1) * L], pick[rows, pair, :], max_t[rows, :],
                                       start=False, stop=True)
                    mm.then_inc(N["t_done"], 1)
                return piece

            def o0(b):
                def piece(g):
                    par = g[1]
                    n = before(g, GROUP) + b
                    if b:
                        pe.wait_ge(N["x2_set"], n)
                    else:
                        pe.wait_ge(N["lg_set"], before(g, 1))
                        pe.wait_ge(N["vaug_set"], upto(g, 1))
                    pe.wait_ge(N["exp2_set"], before(g, 8) + 4 * b + 4)
                    for u in range(4):
                        two, _, pairs = heads(u)
                        for i, pair in enumerate(pairs):
                            mm = pe.matmul(M[TILE * i:TILE * (i + 1), u * L:(u + 1) * L],
                                           v_aug[par][:, b, 2 * pair + two, :], prob[b][:, u, i, :],
                                           start=True, stop=True)
                    mm.then_inc(N["pv_done"], 1)
                return piece

            def o1(b):
                def piece(g):
                    pe.wait_ge(N["pv_out"], before(g, GROUP) + b + 1)
                    for u in range(4):
                        mm = pe.transpose(M[:, u * P:(u + 1) * P], pv[:, u * L:(u + 1) * L], ident)
                    mm.then_inc(N["pvt_done"], 1)
                return piece

            def o2_(b):
                def piece(g):
                    pe.wait_ge(N["o2_set"], before(g, GROUP) + b + 1)
                    pe.transpose(M[:, 0:L], o2[:, :, :].rearrange("p h e -> p (h e)"), ident
                                 ).then_inc(N["o2t_done"], 1)
                return piece

            def o3(b):
                def piece(g):
                    pe.wait_ge(N["o2t_out"], before(g, GROUP) + b + 1)
                    pe.matmul(M[:, 0:D], o2_t[:, :], Lt("xo"), start=True, stop=True).then_inc(N["xo_done"], 1)
                return piece

            def e3(g):
                pe.wait_ge(N["x2_set"], upto(g, GROUP))
                pe.wait_ge(N["z_set"], upto(g, 1))
                for b in range(GROUP):
                    mm = pe.transpose(M[:, b * L:(b + 1) * L], z_g[:, b, :], ident)
                mm.then_inc(N["zt_done"], 1)

            def e4(g):
                pe.wait_ge(N["zt_out"], upto(g, 1))
                for b in range(GROUP):
                    mm = pe.matmul(M[:, b * EXPERTS:(b + 1) * EXPERTS], z_t[:, b * L:(b + 1) * L], Lt("gate"),
                                   start=True, stop=True)
                mm.then_inc(N["lg_done"], 1)

            pe.wait_ge(N["shapes16_set"], 1)
            schedule({"a1": a1, "a2": a2, "a3": a3, "a5": a5, "b0": b_scores(0), "b1": b_scores(1),
                      "b2": b_scores(2), "b3": b_scores(3), "b4": b4, "c0": c0, "c1": c1, "c2": c2, "c3": c3,
                      "c4": c4, "s0": s(0), "s1": s(1), "m0": m(0), "m1": m(1),
                      "t00": t(0, 0), "t01": t(0, 1), "t02": t(0, 2), "t03": t(0, 3),
                      "t10": t(1, 0), "t11": t(1, 1), "t12": t(1, 2), "t13": t(1, 3),
                      "o0": o0(0), "o1": o1(0), "o2": o2_(0), "o3": o3(0),
                      "r0": o0(1), "r1": o1(1), "r2": o2_(1), "r3": o3(1), "e3": e3, "e4": e4}, pe.Fori)

            pe.wait_ge(N["hot_set"], 1)
            pe.wait_ge(N["before_set"], 1)
            flat = EXPERTS * TILES
            pe.matmul(M[:, 0:flat], S16("before"), hot16[:, :, :].rearrange("p e i -> p (e i)"),
                      start=True, stop=False)
            pe.matmul(M[:, 0:flat], S16("ones"), tiles_before[:, :, :].rearrange("p e i -> p (e i)"),
                      start=False, stop=True).then_inc(N["rank_done"], 1)

            def expert(j, par, first=False):
                e = 2 * j + par
                t_bank = (A, B)[par]
                h_banks = ((SB[0], SB[1]), (TB, K))[par]
                o_bank = (C, M)[par]
                pe.wait_ge(tok_in[par], 16 * (j + 1))
                for c in range(2):
                    mm = pe.transpose(t_bank[:, c * P:(c + 1) * P], tok[par][:, c, :], ident)
                mm.then_inc(N["tt_done"], 1)
                pe.wait_ge(N["tok_out"], e + 1)
                pe.wait_ge(we_in[par], 32 * (j + 1))
                pe.wait_ge(N["eo_set"], 2 * j)
                for i in range(HT):
                    mm = pe.matmul(h_banks[i // 2][:, (i % 2) * CAPACITY:(i % 2 + 1) * CAPACITY],
                                   wi_e[par][:, i * P:(i + 1) * P], tok_t[par][:, :], start=True, stop=True)
                    if i % 2:
                        mm.then_inc(N["h_done"], 1)
                for c in range(2):
                    for i in range(HT):
                        if c == 0 and i % 2 == 0:
                            pe.wait_ge(N["gelu_set"], 2 * e + i // 2 + 1)
                        mm = pe.matmul(o_bank[:, c * D:(c + 1) * D], hid[par][:, i, c * P:(c + 1) * P],
                                       wo_e[par][:, i, :], start=(i == 0), stop=(i == HT - 1))
                mm.then_inc(N["eo_done"], 1)

            expert(0, 0)
            expert(0, 1)
            with pe.Fori(1, EXPERTS // 2) as j:
                expert(j, 0)
                expert(j, 1)

        @block.scalar
        def _(act):
            act.wait_ge(N["early_in"], 16)
            act.preload_act_table_set(LN_EXP)

            def a1(g):
                act.wait_ge(N["vg_done"], before(g, GROUP))
                act.wait_ge(N["xt1"], upto(g, 1))
                act.activation(xn1_t[:, :], A[:, 0:T], ACT.Identity).then_inc(N["xt1_out"], 1)

            def a2(g):
                act.wait_ge(N["low_done"], upto(g, 1))
                act.activation(low[:, :], B[0:RANK, 0:T], ACT.Identity).then_inc(N["low_out"], 1)

            def a3(g):
                act.wait_ge(N["z_done"], upto(g, 1))
                act.activation(z_abs[:, :], A[:, 0:T], ACT.Abs, bias=E("b2")).then_inc(N["abs_set"], 1)
                act.wait_ge(N["abs_set"], upto(g, 1))
                act.activation(z_exp[:, :], z_abs[:, :], ACT.Exp, scale=-1.0).then_inc(N["exp_set"], 1)
                act.wait_ge(N["exp_set"], upto(g, 1))
                act.wait_ge(N["gk_set"], before(g, 1))
                act.activation(z_ln[:, :], z_exp[:, :], ACT.Ln, bias=1.0).then_inc(N["ln_set"], 1)

            def a4(g):
                act.wait_ge(N["gated"], before(g, 1))
                act.wait_ge(N["scan_set"], upto(g, 1))
                act.activation(e_pos[:, :], bcum[:, :], ACT.Exp, scale=1.0 / GATE_NORM)
                act.activation(e_neg[:, :], bcum[:, :], ACT.Exp, scale=-1.0 / GATE_NORM).then_inc(N["decay_set"], 1)

            def a5(g):
                par = g[1]
                wait_after(act, N["o_done"], g, 1, 1)
                for b in range(GROUP):
                    act.wait_ge(N["vg_done"], upto(g, GROUP, b + 1))
                    act.activation(v_sb[par][:, b, :], (A, B)[b][:, 0:256], ACT.Identity).then_inc(N["v_set"], 1)
                for b in range(GROUP):
                    act.wait_ge(N["silu_set"], before(g, GROUP) + b)
                    act.activation(th[:, b, :], (A, B)[b][:, 256:512], ACT.Tanh, scale=0.5
                                   ).then_inc(N["tanh_set"], 1)
                act.preload_act_table_set(LN_EXP)

            def b4(g):
                act.wait_ge(N["ss_set"], before(g, 1))
                act.wait_ge(N["o_done"], upto(g, 1))
                act.activation(o_sq[:, :, :].rearrange("p h e -> p (h e)"), C[:, :], ACT.Square
                               ).then_inc(N["sq_set"], 1)

            def c0(g):
                act.wait_ge(N["wo_done"], before(g, 1))
                act.wait_ge(N["ogt_done"], upto(g, 1))
                act.activation(og_t[:, :, :, :].rearrange("p b c t -> p (b c t)"), K[:, :], ACT.Identity
                               ).then_inc(N["ogt_out"], 1)

            def c2(g):
                j, par = g
                landed = 128 * (j + par)
                if not isinstance(landed, int) or landed:
                    act.wait_ge(ks_in[1 - par], landed)
                act.wait_ge(N["kv_done"], upto(g, 1))
                act.activation(k_part[0][:, :], K[:, 0:GROUP * KEYS], ACT.Identity, bias=E("bk")
                               ).then_inc(N["k1_set"], 1)
                wait_after(act, N["pv_done"], g, GROUP, GROUP)
                act.activation(v_aug[par][:, :, :, 0:DEPTH],
                               K[0:KEYS, T:2 * T].rearrange("p (b h e) -> p b h e", b=GROUP, h=HEADS),
                               ACT.Identity).then_inc(N["vaug_set"], 1)
                act.wait_ge(N["krest_set"], upto(g, 1))
                act.activation(k_part[1][:, :], k_rest[:, :], ACT.Identity).then_inc(N["k2_set"], 1)

            def c3(g):
                act.wait_ge(N["q_done"], before(g, 1))
                act.wait_ge(N["xt2"], upto(g, 1))
                act.activation(xn2_t[:, :], K[:, 0:T], ACT.Identity).then_inc(N["xt2_out"], 1)

            def c4(g):
                j, par = g
                landed = 128 * (j + par)
                if not isinstance(landed, int) or landed:
                    act.wait_ge(qs_in[1 - par], landed)
                act.wait_ge(N["q_done"], upto(g, 1))
                act.activation(q_part[0][:, :], K[:, 0:T], ACT.Identity, bias=E("bq")).then_inc(N["q1_set"], 1)

            def m(b):
                def piece(g):
                    wait_after(act, N["t_done"], g, 8, -4 * b)
                    act.wait_ge(N["mt_done"], before(g, GROUP) + b + 1)
                    act.activation(max_t[:, :], TB[:, 0:P // 2].bitcast(BF16), ACT.Identity
                                   ).then_inc(N["mt_out"], 1)
                return piece

            def t(b, u):
                def piece(g):
                    if u == 0:
                        wait_after(act, N["pv_done"], g, GROUP, 1 - b)
                    act.wait_ge(N["t_done"], before(g, 8) + 4 * b + u + 1)
                    act.activation(prob[b][:, u, :, :].rearrange("p a t -> p (a t)"), TB[0:KEYS, :],
                                   ACT.Exp, scale=float(DEPTH) ** -0.5).then_inc(N["exp2_set"], 1)
                return piece

            def o0(b):
                def piece(g):
                    n = before(g, GROUP) + b
                    act.wait_ge(N["pvt_done"], n)
                    act.wait_ge(N["pv_done"], n + 1)
                    act.activation(pv[:, :], M[:, :], ACT.Identity).then_inc(N["pv_out"], 1)
                return piece

            def o2_(b):
                def piece(g):
                    act.wait_ge(N["o2t_done"], before(g, GROUP) + b + 1)
                    act.activation(o2_t[:, :], M[:, 0:L], ACT.Identity, bias=E("bv")).then_inc(N["o2t_out"], 1)
                return piece

            def e3(g):
                act.wait_ge(N["zt_done"], upto(g, 1))
                act.activation(z_t[:, :], M[:, 0:T], ACT.Identity, bias=E("beta"), scale=E("gamma")
                               ).then_inc(N["zt_out"], 1)

            def e4(g):
                j, par = g
                act.wait_ge(N["lg_done"], upto(g, 1))
                act.activation(logits[:, :, bass.ds((2 * j + par) * GROUP, GROUP)],
                               M[:, 0:GROUP * EXPERTS].rearrange("p (b e) -> p e b", b=GROUP),
                               ACT.Identity).then_inc(N["lg_set"], 1)

            schedule({"a1": a1, "a2": a2, "a3": a3, "a4": a4, "a5": a5, "b4": b4, "c0": c0, "c2": c2, "c3": c3,
                      "c4": c4, "m0": m(0), "m1": m(1),
                      "t00": t(0, 0), "t01": t(0, 1), "t02": t(0, 2), "t03": t(0, 3),
                      "t10": t(1, 0), "t11": t(1, 1), "t12": t(1, 2), "t13": t(1, 3),
                      "o0": o0(0), "o2": o2_(0), "r0": o0(1), "r2": o2_(1), "e3": e3, "e4": e4}, act.Fori)

            act.wait_ge(N["r_sub"], 1)
            act.activation(r_exp[:, :, :], r_diff[:, :, :], ACT.Exp).then_inc(N["r_expd"], 1)

            with act.Fori(0, EXPERTS // 2) as j:
                for par in range(2):
                    e = 2 * j + par
                    act.wait_ge(N["tt_done"], e + 1)
                    act.activation(tok_t[par][:, :], (A, B)[par][:, 0:CAPACITY], ACT.Identity, bias=E("beta"),
                                   scale=E("gamma")).then_inc(N["tok_out"], 1)
                    for i in range(2):
                        act.wait_ge(N["h_done"], 2 * e + i + 1)
                        act.activation(hid[par][:, 2 * i:2 * i + 2, :].rearrange("p a t -> p (a t)"),
                                       ((SB[0], SB[1]), (TB, K))[par][i][:, :], ACT.Gelu).then_inc(N["gelu_set"], 1)

        @block.vector
        def _(dve):
            dve.memset(back[:, :, :], 0.0).then_inc(N["cleared"], 1)
            dve.memset(max_part[:, :, :, :], 0.0)
            for i in range(2):
                dve.memset(k_first[i][:, :, :], 0.0)
                dve.memset(v_aug[i][:, :, :, DEPTH:TILE], 0.0).then_inc(N["v_ones"], 1)
                dve.wait_ge(N["v_ones"], i + 1)
                dve.memset(v_aug[i][:, :, :, DEPTH:DEPTH + 1], 1.0)

            def norm_stats(src, st, mv, ve, s_stats, s_aggr, s_veps, g):
                for b in range(GROUP):
                    dve.bn_stats(st[:, b, :], src[:, b, :]).then_inc(s_stats, 1)
                dve.wait_ge(s_stats, upto(g, GROUP))
                dve.memset(pause[:, :], 0.0)
                for b in range(GROUP):
                    dve.bn_aggr(mv[:, b, :], st[:, b, :]).then_inc(s_aggr, 1)
                dve.wait_ge(s_aggr, upto(g, GROUP))
                dve.tensor_scalar(ve[:, :], mv[:, :, 1], EPS, None, ALU.add).then_inc(s_veps, 1)

            def group_of(a, g):
                return a[:, bass.ds((2 * g[0] + g[1]) * GROUP, GROUP), :]

            def tk(a):
                return a.rearrange("p (b t) -> p b t", b=GROUP)

            def a0(g):
                j, par = g
                if isinstance(j, int) and 2 * j + par < 3:
                    dve.wait_ge(x_in[2 * j + par], 16)
                norm_stats(group_of(x_all, g), st1, mv1, ve1, N["stats1"], N["aggr1"], N["veps1"], g)

            def a1(g):
                par = g[1]
                dve.wait_ge(N["rstd1"], upto(g, 1))
                for b in range(GROUP):
                    op = dve.tensor_scalar(xn1[:, b, :], group_of(x_all, g)[:, b, :], mv1[:, b, 0:1], rs1[:, b:b + 1],
                                           ALU.subtract, ALU.mult)
                op.then_inc(N["xn1_set"], 1)

            def a3(g):
                dve.wait_ge(N["abs_set"], upto(g, 1))
                dve.tensor_scalar(z_min[:, :], A[:, 0:T], E("b2"), 0.0, ALU.add, ALU.min).then_inc(N["min_set"], 1)

            def a4(g):
                par = g[1]
                dve.wait_ge(N["gk_set"], upto(g, 1))
                dve.tensor_tensor_scan(bcum[:, :], S("reset"), gk[:, :], 0.0, ALU.mult, ALU.add
                                       ).then_inc(N["scan_set"], 1)

            def a45(g):
                par = g[1]
                dve.wait_ge(N["decay_set"], upto(g, 1))
                dve.wait_ge(N["qk_done"], upto(g, 1))
                dve.scalar_tensor_tensor(qg[par][:, :, :], tk(B[:, 0:T]), float(DK) ** -0.5, tk(e_pos[:, :]),
                                         ALU.mult, ALU.mult)
                dve.tensor_tensor(k_second[par][:, :, CHUNK:L], tk(B[:, T:2 * T])[:, :, CHUNK:L],
                                  tk(e_neg[:, :])[:, :, CHUNK:L], ALU.mult)
                dve.tensor_tensor(k_first[par][:, :, 0:CHUNK], tk(B[:, T:2 * T])[:, :, 0:CHUNK],
                                  tk(e_neg[:, :])[:, :, 0:CHUNK], ALU.mult).then_inc(N["kf_set"], 1)
                dve.wait_ge(N["kf_set"], upto(g, 1))
                dve.tensor_tensor(k_second[par][:, :, 0:CHUNK], k_first[par][:, :, 0:CHUNK],
                                  tk(e_pos[:, :])[:, :, CHUNK - 1:CHUNK].to_broadcast([P, GROUP, CHUNK]),
                                  ALU.mult).then_inc(N["gated"], 1)

            def a5(g):
                for b in range(GROUP):
                    dve.wait_ge(N["silu_n_set"], before(g, GROUP) + b)
                    dve.wait_ge(N["tanh_set"], upto(g, GROUP, b + 1))
                    dve.scalar_tensor_tensor(silu2[:, b, :], th[:, b, :], 1.0, (A, B)[b][:, 256:512],
                                             ALU.add, ALU.mult).then_inc(N["silu_set"], 1)

            def b_mask(h):
                def piece(g):
                    dve.wait_ge(N["at_done"], upto(g, GLA_HEADS, h + 1))
                    dve.tensor_tensor(att[h][:, :, :], tk(C[:, 0:T]),
                                      S("causal").unsqueeze(1).to_broadcast([P, GROUP, L]), ALU.mult
                                      ).then_inc(N["att_set"], 1)
                return piece

            def b4(g):
                dve.wait_ge(N["sq_set"], upto(g, 1))
                dve.tensor_reduce(o_ss[:, :], o_sq[:, :, :], AX.X, ALU.add).then_inc(N["ss_set"], 1)
                dve.wait_ge(N["ss_set"], upto(g, 1))
                dve.tensor_scalar(o_ms[:, :], o_ss[:, :], 1.0 / DV, EPS, ALU.mult, ALU.add).then_inc(N["ms_set"], 1)

            def b5(g):
                par = g[1]
                dve.wait_ge(N["gate_set"], upto(g, 1))
                wait_after(dve, N["ogt_done"], g, 1, 1)
                dve.tensor_tensor(og[par][:, :, :].rearrange("p b c -> p (b c)"), C[:, :],
                                  o_gate[:, :, :].rearrange("p b c -> p (b c)"), ALU.mult).then_inc(N["og_set"], 1)

            def c1(g):
                j, par = g
                dve.wait_ge(N["x1b_set"], before(g, 1))
                dve.wait_ge(N["wo_done"], upto(g, 1))
                dve.tensor_tensor(x1[:, :, :].rearrange("p b d -> p (b d)"), K[:, 0:GROUP * D],
                                  group_of(x_all, g).rearrange("p b d -> p (b d)"), ALU.add
                                  ).then_inc(N["x1_set"], 1)
                dve.wait_ge(N["x1_set"], upto(g, 1))
                norm_stats(x1, st2, mv2, ve2, N["stats2"], N["aggr2"], N["veps2"], g)

            def c2(g):
                dve.wait_ge(N["k3_set"], before(g, 1))
                dve.wait_ge(N["vaug_set"], upto(g, 1))
                dve.wait_ge(N["k1_set"], upto(g, 1))
                dve.scalar_tensor_tensor(k_rest[:, :], K[:, 0:GROUP * KEYS], E("bk"), k_part[0][:, :],
                                         ALU.add, ALU.subtract).then_inc(N["krest_set"], 1)

            def c3(g):
                dve.wait_ge(N["rstd2"], upto(g, 1))
                for b in range(GROUP):
                    op = dve.tensor_scalar(xn2[:, b, :], x1[:, b, :], mv2[:, b, 0:1], rs2[:, b:b + 1],
                                           ALU.subtract, ALU.mult)
                op.then_inc(N["xn2_set"], 1)

            def c4(g):
                dve.wait_ge(N["q1_set"], upto(g, 1))
                dve.scalar_tensor_tensor(q_rest[:, :], K[:, 0:T], E("bq"), q_part[0][:, :],
                                         ALU.add, ALU.subtract).then_inc(N["qrest_set"], 1)
                dve.wait_ge(N["qrest_set"], upto(g, 1))
                dve.tensor_copy(q_part[1][:, :], q_rest[:, :]).then_inc(N["q2_set"], 1)
                dve.wait_ge(N["q2_set"], upto(g, 1))
                dve.tensor_tensor(q_part[2][:, :], q_rest[:, :], q_part[1][:, :], ALU.subtract
                                  ).then_inc(N["q3_set"], 1)

            def s(b):
                def piece(g):
                    for u in range(4):
                        dve.wait_ge(N["s_done"], before(g, 8) + 4 * b + u + 1)
                        dve.tensor_reduce(max_neg[:, u % 2, 4 * (u // 2):4 * (u // 2) + 4],
                                          SB[u % 2][:, 0:4 * KEYS].rearrange("p (a k) -> p a k", a=4),
                                          AX.X, ALU.max, negate=True).then_inc(N["max_set"], 1)
                return piece

            def m(b):
                def piece(g):
                    n = before(g, GROUP) + b
                    wait_after(dve, N["mt_done"], g, GROUP, -b)
                    dve.wait_ge(N["max_set"], before(g, 8) + 4 * b + 4)
                    dve.tensor_copy(max_part[:, :, 0, :], max_neg[:, :, :]).then_inc(N["m1_set"], 1)
                    dve.wait_ge(N["m1_set"], n + 1)
                    dve.tensor_tensor(max_part[:, :, 1, :], max_neg[:, :, :], max_part[:, :, 0, :], ALU.subtract
                                      ).then_inc(N["m2_set"], 1)
                return piece

            def o1(b):
                def piece(g):
                    n = before(g, GROUP) + b
                    sums = M[:, :].rearrange("p (h e) -> p h e", h=HEADS)
                    dve.wait_ge(N["pvt_done"], n + 1)
                    dve.reciprocal(den[:, :], sums[:, :, DEPTH]).then_inc(N["den_set"], 1)
                    dve.wait_ge(N["den_set"], n + 1)
                    dve.tensor_tensor(o2[:, :, :], sums[:, :, 0:DEPTH],
                                      den[:, :].unsqueeze(2).to_broadcast([P, HEADS, DEPTH]), ALU.mult
                                      ).then_inc(N["o2_set"], 1)
                return piece

            def o3(b):
                def piece(g):
                    par = g[1]
                    if b == 0:
                        dve.wait_ge(N["x1b_set"], upto(g, 1))
                    dve.wait_ge(N["xo_done"], before(g, GROUP) + b + 1)
                    dve.tensor_tensor(x2[par][:, b, :], M[:, 0:D], x1b[par][:, b, :], ALU.add
                                      ).then_inc(N["x2_set"], 1)
                return piece

            def e0(g):
                par = g[1]
                dve.wait_ge(N["x2_set"], upto(g, GROUP))
                norm_stats(x2[par], st3, mv3, ve3, N["stats3"], N["aggr3"], N["veps3"], g)

            def e1(g):
                par = g[1]
                dve.wait_ge(N["rstd3"], upto(g, 1))
                dve.tensor_tensor(rr3[:, :], rs3[:, :], rs3[:, :], ALU.mult).then_inc(N["rr3_set"], 1)
                dve.wait_ge(N["rr3_set"], upto(g, 2, 1))
                dve.tensor_tensor(rr3[:, :], rr3[:, :], mv3[:, :, 1], ALU.mult).then_inc(N["rr3_set"], 1)
                dve.wait_ge(N["rr3_set"], upto(g, 2, 2))
                dve.tensor_scalar(ve4[:, :], rr3[:, :], EPS, None, ALU.add).then_inc(N["veps4"], 1)
                for b in range(GROUP):
                    op = dve.tensor_scalar(y[:, b, :], x2[par][:, b, :], mv3[:, b, 0:1], rs3[:, b:b + 1],
                                           ALU.subtract, ALU.mult)
                op.then_inc(N["y_set"], 1)

            def e2(g):
                dve.wait_ge(N["y_set"], upto(g, 1))
                dve.wait_ge(N["rstd4"], upto(g, 1))
                for b in range(GROUP):
                    op = dve.tensor_scalar(z_g[:, b, :], y[:, b, :], rs4[:, b:b + 1], None, ALU.mult)
                op.then_inc(N["z_set"], 1)

            dve.wait_ge(N["early_in"], 16)
            dve.wait_ge(N["shapes_in"], 16)
            dve.wait_ge(N["shapes16_in"], 16)
            dve.tensor_copy(shapes16[:, :], shapes_w[:, :]).then_inc(N["shapes16_set"], 1)
            dve.wait_ge(N["late_in"], 16)
            dve.tensor_scalar(half_gnorm[:, :], Lt("gnorm"), 0.5, None, ALU.mult).then_inc(N["half_gnorm_set"], 1)
            schedule({"a0": a0, "a1": a1, "a3": a3, "a4": a4, "a45": a45, "a5": a5, "b0": b_mask(0), "b1": b_mask(1),
                      "b2": b_mask(2), "b3": b_mask(3), "b4": b4, "b5": b5, "c1": c1, "c2": c2, "c3": c3, "c4": c4,
                      "s0": s(0), "s1": s(1), "m0": m(0), "m1": m(1), "o1": o1(0), "o3": o3(0), "r1": o1(1),
                      "r3": o3(1), "e0": e0, "e1": e1, "e2": e2}, dve.Fori)

            chain = [0]

            def then(op):
                chain[0] += 1
                op.then_inc(N["r_chain"], 1)
                dve.wait_ge(N["r_chain"], chain[0])

            def each(a):
                return a[:, :].unsqueeze(1).to_broadcast([P, EXPERTS, TILES])

            def by_token(a):
                return a[:, :, :].rearrange("p e i -> p i e")

            cst = lambda n: S(n).rearrange("p (e i) -> p e i", e=EXPERTS)
            dve.wait_ge(N["lg_set"], GROUPS)
            then(dve.tensor_reduce(r_max[:, :], by_token(logits), AX.X, ALU.max))
            dve.tensor_tensor(r_diff[:, :, :], logits[:, :, :], each(r_max), ALU.subtract).then_inc(N["r_sub"], 1)
            then(dve.tensor_tensor(r_eq[:, :, :], logits[:, :, :], each(r_max), ALU.is_equal))
            then(dve.tensor_tensor(r_cand[:, :, :], r_eq[:, :, :], cst("order"), ALU.mult))
            then(dve.tensor_reduce(r_val[:, :], by_token(r_cand), AX.X, ALU.max))
            then(dve.tensor_tensor(one_hot[:, :, :], r_cand[:, :, :], each(r_val), ALU.is_equal))
            dve.tensor_copy(hot16[:, :, :], one_hot[:, :, :]).then_inc(N["hot_set"], 1)
            flat = lambda a: a[:, :, :].rearrange("p e i -> p (e i)")
            then(dve.tensor_tensor_scan(flat(r_incl), S("treset"), flat(one_hot), 0.0, ALU.mult, ALU.add))
            dve.tensor_tensor(tiles_before[:, :, :], r_incl[:, :, :], one_hot[:, :, :], ALU.subtract
                              ).then_inc(N["before_set"], 1)
            dve.wait_ge(N["r_expd"], 1)
            then(dve.tensor_reduce(r_sum[:, :], by_token(r_exp), AX.X, ALU.add))
            then(dve.reciprocal(r_inv[:, :], r_sum[:, :]))
            dve.wait_ge(N["rank_done"], 1)
            m_rank = M[:, 0:EXPERTS * TILES].rearrange("p (e i) -> p e i", e=EXPERTS)
            then(dve.tensor_tensor(r_a[:, :, :], m_rank, cst("ebase"), ALU.add))
            then(dve.tensor_tensor(r_b[:, :, :], r_a[:, :, :], one_hot[:, :, :], ALU.mult))
            then(dve.tensor_reduce(r_slot[:, :], by_token(r_b), AX.X, ALU.add))
            then(dve.scalar_tensor_tensor(flat(r_rank), M[:, 0:EXPERTS * TILES], float(CAPACITY), flat(one_hot),
                                          ALU.is_lt, ALU.mult))
            then(dve.tensor_reduce(r_keep[:, :], by_token(r_rank), AX.X, ALU.add))
            then(dve.tensor_tensor(weight[:, :], r_inv[:, :], r_keep[:, :], ALU.mult))
            then(dve.tensor_tensor(r_tmp[:, :], r_slot[:, :], r_keep[:, :], ALU.mult))
            dve.tensor_copy(from_slot[:, :], r_tmp[:, :]).then_inc(N["idx_set"], 1)
            then(dve.tensor_scalar(r_off[:, :], r_keep[:, :], -2.0 * SLOTS, 2.0 * SLOTS, ALU.mult, ALU.add))
            dve.tensor_tensor(to_slot[:, :], r_tmp[:, :], r_off[:, :], ALU.add).then_inc(N["idx_set"], 1)

            def expert_rows(j, par):
                dve.wait_ge(N["eo_done"], 2 * j + par + 1)
                dve.wait_ge(eo_stored[par], 16 * j)
                dve.tensor_copy(e_out[par][:, :, :].rearrange("p c d -> p (c d)"), (C, M)[par][:, 0:2 * D]
                                ).then_inc(N["eo_set"], 1)

            expert_rows(0, 0)
            expert_rows(0, 1)
            with dve.Fori(1, EXPERTS // 2) as j:
                expert_rows(j, 0)
                expert_rows(j, 1)

            dve.wait_ge(N["gathered"], 16 * TILES)
            for i in range(TILES):
                dve.scalar_tensor_tensor(result[:, i, :], back[:, i, :], weight[:, i:i + 1], xy_all[:, i, :],
                                         ALU.mult, ALU.add).then_inc(N["res_set"], 1)


def host_constants():
    s = np.arange(P)
    shape = np.zeros((P, SHAPE_W), np.float32)

    def put(name, value):
        a, b = SHAPE[name]
        shape[:, a:b] = value
    put("reset", (np.arange(T) % CHUNK != 0)[None, :])
    put("causal", s[:, None] <= s[None, :])
    put("mhalf", -0.5)
    e = np.repeat(np.arange(EXPERTS), TILES)
    put("ebase", (e * CAPACITY)[None, :])
    put("order", (EXPERTS - e)[None, :])
    put("treset", (np.arange(EXPERTS * TILES) % TILES != 0)[None, :])
    shape16 = np.zeros((P, SHAPE16_W), np.float32)

    def put16(name, value):
        a, b = SHAPE16[name]
        shape16[:, a:b] = value
    put16("ident", np.eye(P))
    pick = np.zeros((2, 8, PAIRS, PAIRS, KEYS), np.float32)
    for pair in range(PAIRS):
        pick[:, 0:2, pair, pair, :] = 1.0
    put16("pick", pick.reshape(P, PAIRS * KEYS))
    put16("before", s[:, None] < s[None, :])
    put16("ones", 1.0)
    return shape, shape16


def kernel(**inputs):
    import concourse.bacc as bacc
    from concourse.bass_utils import run_bass_kernel_spmd as run

    a = {k: np.asarray(v) for k, v in inputs.items()}
    order = np.arange(D).reshape(PAIRS, 2, DEPTH).transpose(1, 2, 0).reshape(-1)
    by_unit = np.arange(D).reshape(2, 4, 2, DEPTH).transpose(0, 2, 1, 3).reshape(-1)
    col = lambda v: v[:, None]
    early = np.zeros((P, EARLY_W), np.float32)
    late = np.zeros((P, LATE_W), np.float32)

    def put(dst, where, name, value):
        dst[:value.shape[0], where[name][0]:where[name][1]] = value
    put(early, EARLY, "ident", np.eye(P, dtype=np.float32))
    put(early, EARLY, "w1", a["L0_attn_gk_w1"])
    put(early, EARLY, "w2", a["L0_attn_gk_w2"])
    put(early, EARLY, "b2", col(a["L0_attn_gk_b2"]))
    put(early, EARLY, "bq", col(a["L0_xattn_bq"][order]))
    put(early, EARLY, "bk", col(a["L0_xattn_bk"][order]))
    put(early, EARLY, "bv", col(a["L0_xattn_bv"][by_unit]))
    put(early, EARLY, "gamma", col(a["L0_ffn_ln_gamma"]))
    put(early, EARLY, "beta", col(a["L0_ffn_ln_beta"]))
    put(early, EARLY, "vg", np.concatenate([a["L0_attn_Wv"], a["L0_attn_Wg"]], axis=1))
    put(early, EARLY, "q", a["L0_attn_Wq"])
    put(early, EARLY, "k", a["L0_attn_Wk"])
    put(late, LATE, "wo", a["L0_attn_Wo"].reshape(2, P, D).transpose(1, 0, 2).reshape(P, 2 * D))
    put(late, LATE, "xk", a["L0_xattn_wk"].T[:, order])
    put(late, LATE, "xv", a["L0_xattn_wv"].T)
    put(late, LATE, "xq", a["L0_xattn_wq"].T[:, order])
    put(late, LATE, "xo", a["L0_xattn_wo"].T[by_unit])
    put(late, LATE, "gate", a["L0_ffn_gate_weight"].T)
    put(late, LATE, "gnorm", np.tile(a["L0_attn_g_norm_w"], (P, GLA_HEADS)))
    put(late, LATE, "bo", np.tile(a["L0_xattn_bo"], (P, 1)))
    shape, shape16 = host_constants()
    arrays = {
        "x": a["x"].transpose(1, 0, 2),
        "ctx_t": a["ctx_1024"].transpose(2, 0, 1),
        "early": early, "late": late, "shape": shape, "shape16": shape16,
        "wi": a["L0_ffn_wi"].transpose(1, 0, 2),
        "wo": a["L0_ffn_wo"].reshape(EXPERTS * HT, P, D).transpose(1, 0, 2),
    }
    arrays = {k: np.ascontiguousarray(v) for k, v in arrays.items()}
    nc = bacc.Bacc("TRN2", target_bir_lowering=False, num_devices=1)
    ins = {k: nc.dram_tensor(f"in_{k}", v.shape, mybir.dt.from_np(v.dtype), kind="ExternalInput").ap()
           for k, v in arrays.items()}
    out = nc.dram_tensor("out", (P, SEQS, D), F32, kind="ExternalOutput").ap()
    slots_in = nc.dram_tensor("slots_in", (SLOTS, D), F32, kind="Internal").ap()
    slots_out = nc.dram_tensor("slots_out", (SLOTS, D), F32, kind="Internal").ap()
    build(nc, ins["x"], ins["ctx_t"], ins["early"], ins["late"], ins["shape"], ins["shape16"], ins["wi"], ins["wo"],
          out, slots_in, slots_out)
    r = run(nc, [{f"in_{k}": v for k, v in arrays.items()}], core_ids=[0])
    return np.ascontiguousarray(r.results[0]["out"].transpose(1, 0, 2))
```

```python
from contextlib import ExitStack

import numpy as np

import concourse.bass as bass
from concourse import mybir

F32 = mybir.dt.float32
BF16 = mybir.dt.bfloat16
U32 = mybir.dt.uint32
ALU = mybir.AluOpType
ACT = mybir.ActivationFunctionType
AX = mybir.AxisListType

P = 128
SEQS, L, D = 16, 128, 128
KEYS = 120
GROUP = 2
GROUPS = SEQS // GROUP
assert GROUPS == 8
T = GROUP * L
GLA_HEADS, DK, DV, CHUNK = 4, 32, 64, 64
RANK = 16
HEADS, DEPTH = 16, 8
PAIRS = HEADS // 2
TILE = 32
PARTS = 3
Q_PART = (0, 0, 0, 1, 1, 1, 2, 2)
K_PART = (0, 1, 2, 0, 1, 2, 0, 1)
EXPERTS, HIDDEN = 8, 512
CAPACITY = 256
SLOTS = EXPERTS * CAPACITY
ROW = 2 * D + 2
HT = HIDDEN // P
FILL = """r0 r1 t00 s00 b0 t01 s01 a0 c0 s02 e0 s03 r2 b1 s10 s11 a1 s12 c1 x c2 a3 t02 e1 t03 s13 f0 f1 c3 a4
    c4 e2 a45 b4 t10 t11 b5 r3 f2 m0 t12 o0 o1 e3 m1 o2 a5 e4 o3 t13 f3 f4""".split()
DRAIN = """s00 r0 s01 s02 r1 s03 c0 r2 m0 s10 t00 x r3 a0 e0 c1 s11 a1 t01 b0 a3 b1 e1 c2 s12 t02 c3 s13 t03 a4
    m1 e2 c4 e3 t10 a45 o0 t11 f0 e4 b4 t12 f1 o1 f2 a5 f3 b5 o2 f4 t13 o3""".split()
LOOP_PE = """b0 s00 w0 r0 w1 s01 s02 r1 s03 r2 c0 m0 s10 t00 s11 a1 r3 c1 t01 s12 c2 s13 b1 t02 a3 t03 c3 m1 t10
    c4 e3 b4 e4 t11 o0 t12 o1 f2 t13 o2 a5 o3 v0""".split()
LOOP_ACT = """r0 c0 m0 r2 t00 a1 t01 c2 t02 a3 t03 c3 m1 a4 c4 t10 e3 b4 t11 f0 o0 t12 o2 t13 a5""".split()
LOOP_DVE = """s00 b0 s01 a0 s02 r1 s03 a1 m0 s10 s11 r3 e0 c1 s12 c2 e1 b1 s13 c3 m1 a3 a4 e2 a45 c4 b4 f0 f1 f2
    o1 f3 b5 o3 a5""".split()
LOOP_POOL = """a0 e0 c1 c2 e1 a3 b4 b5 a5 f4""".split()
LOOP_SP = """x e1 c2 c4""".split()
AHEAD = {"a": 3, "b": 2, "x": 2, "c": 1, "s": 0, "m": 0, "t": 0, "o": 0, "r": -1, "e": -1, "f": -1, "v": -1, "w": 0}
FILLER = 3
EXPERT_FILLER = 14
EPS = 1e-5
GATE_NORM = 16.0
LN_EXP = "natural_log_exp_and_others"


def layout(parts):
    at, out = 0, {}
    for name, width in parts:
        out[name] = (at, at + width)
        at += width
    return out, at


EARLY, EARLY_W = layout([("ident", P), ("w1_t", D), ("w2", D), ("b2", 1), ("bq", 1), ("bk", 1), ("bv", 1),
                         ("gamma", 1), ("beta", 1), ("vg", 512), ("q", D), ("k", D)])
LATE, LATE_W = layout([("wo", 2 * D), ("xk", D), ("xv", D), ("xq", D), ("xo", D), ("gate", EXPERTS),
                       ("gnorm", GLA_HEADS * DV), ("bo", D)])
SHAPE, SHAPE_W = layout([("reset", T), ("causal", P), ("ecap", GROUP * EXPERTS),
                         ("order", GROUP * EXPERTS), ("ebase", EXPERTS), ("place", SEQS)])
SHAPE16, SHAPE16_W = layout([("ident", P), ("pick", PAIRS * KEYS), ("before", P), ("ones", P)])


def build(nc, x, ctx_t, early_d, late_d, shape_d, shape16_d, wi_d, wo_d, out, slots):
    with ExitStack() as stack:
        def sb(name, shape, dt=F32):
            return stack.enter_context(nc.sbuf_tensor(name, shape, dt))

        def bank(name):
            return stack.enter_context(nc.psum_tensor(name, [P, 512], F32))

        def sem(name):
            return stack.enter_context(nc.semaphore(name))

        early = sb("early", [P, EARLY_W])
        late = sb("late", [P, LATE_W])
        shapes = sb("shapes", [P, SHAPE_W])
        shapes_w = sb("shapes_w", [P, SHAPE16_W])
        shapes16 = sb("shapes16", [P, SHAPE16_W], BF16)

        def E(name):
            return early[:, EARLY[name][0]:EARLY[name][1]]

        def Lt(name):
            return late[:, LATE[name][0]:LATE[name][1]]

        def S(name):
            return shapes[:, SHAPE[name][0]:SHAPE[name][1]]

        def S16(name):
            return shapes16[:, SHAPE16[name][0]:SHAPE16[name][1]]

        pick = S16("pick").rearrange("p (a k) -> p a k", a=PAIRS)
        half_gnorm = sb("half_gnorm", [P, GLA_HEADS * DV])

        x_all = sb("x_all", [P, SEQS, D])

        ctx_g = [sb(f"ctx_g{i}", [P, GROUP, KEYS]) for i in range(2)]
        mh = sb("mh", [P, GROUP * GLA_HEADS])
        st1 = sb("st1", [P, GROUP, 6])
        pause = sb("pause", [P, 1])
        mv1 = sb("mv1", [P, GROUP, 2])
        ve1 = sb("ve1", [P, GROUP])
        rs1 = sb("rs1", [P, GROUP])
        xn1 = sb("xn1", [P, GROUP, D])
        xn1_t = sb("xn1_t", [P, T])
        w12 = sb("w12", [P, D])
        z_abs = sb("z_abs", [P, T])
        z_exp = sb("z_exp", [P, T])
        z_ln = sb("z_ln", [P, T])
        z_min = sb("z_min", [P, T])
        gk = sb("gk", [P, T])
        bcum = sb("bcum", [P, T])
        e_pos = sb("e_pos", [P, T])
        e_neg = sb("e_neg", [P, T])
        qg = [sb(f"qg{i}", [P, GROUP, L]) for i in range(2)]
        k_first = [sb(f"k_first{i}", [P, GROUP, CHUNK]) for i in range(2)]
        k_second = [sb(f"k_second{i}", [P, GROUP, L]) for i in range(2)]
        v_sb = [sb(f"v_sb{i}", [P, GROUP, GLA_HEADS * DV]) for i in range(2)]
        th = sb("th", [P, GROUP, GLA_HEADS * DV])
        silu2 = sb("silu2", [P, GROUP, GLA_HEADS * DV])
        silu_n = [sb(f"silu_n{i}", [P, GROUP, GLA_HEADS * DV]) for i in range(2)]
        att = sb("att", [P, GLA_HEADS, GROUP, L])
        o_sq = sb("o_sq", [P, GROUP * GLA_HEADS, DV])
        o_ss = sb("o_ss", [P, GROUP * GLA_HEADS])
        o_ms = sb("o_ms", [P, GROUP * GLA_HEADS])
        o_rs = sb("o_rs", [P, GROUP * GLA_HEADS])
        o_gate = sb("o_gate", [P, GROUP, GLA_HEADS * DV])
        og = [sb(f"og{i}", [P, GROUP, GLA_HEADS * DV]) for i in range(2)]
        og_t = sb("og_t", [P, GROUP, 2, L])
        x1 = sb("x1", [P, GROUP, D])
        x1b = [sb(f"x1b{i}", [P, GROUP, D]) for i in range(2)]
        st2 = sb("st2", [P, GROUP, 6])
        mv2 = sb("mv2", [P, GROUP, 2])
        ve2 = sb("ve2", [P, GROUP])
        rs2 = sb("rs2", [P, GROUP])
        xn2 = sb("xn2", [P, GROUP, D])
        xn2_t = sb("xn2_t", [P, T])
        k_part = [sb(f"k_part{i}", [P, GROUP * KEYS], BF16) for i in range(PARTS)]
        q_part = [sb(f"q_part{i}", [P, T], BF16) for i in range(PARTS)]
        k_rest = sb("k_rest", [P, GROUP * KEYS])
        q_rest = sb("q_rest", [P, T])
        ks = [sb(f"ks{i}", [P, PAIRS, GROUP * KEYS], BF16) for i in range(2)]
        qs = [sb(f"qs{i}", [P, PAIRS, T], BF16) for i in range(2)]
        v_aug = [sb(f"v_aug{i}", [KEYS, GROUP, HEADS, TILE]) for i in range(2)]

        max_neg = sb("max_neg", [P, 2, PAIRS])
        max_part = sb("max_part", [P, 2, 8, PAIRS], BF16)
        max_t = sb("max_t", [P, P], BF16)
        prob = [sb(f"prob{i}", [KEYS, 4, 4, L]) for i in range(GROUP)]
        pv = sb("pv", [P, 4 * L])
        den = sb("den", [P, HEADS])
        o2 = sb("o2", [P, HEADS, DEPTH])
        o2_t = sb("o2_t", [P, L])
        x2 = [sb(f"x2_{i}", [P, GROUP, D]) for i in range(2)]
        st3 = sb("st3", [P, GROUP, 6])
        mv3 = sb("mv3", [P, GROUP, 2])
        ve3 = sb("ve3", [P, GROUP])
        rs3 = sb("rs3", [P, GROUP])
        rr3 = sb("rr3", [P, GROUP])
        ve4 = sb("ve4", [P, GROUP])
        rs4 = sb("rs4", [P, GROUP])
        y = sb("y", [P, GROUP, D])
        z_t = sb("z_t", [P, T])
        rows = [sb(f"rows{i}", [P, GROUP, ROW]) for i in range(2)]

        r_max, r_val, r_sum, r_slot = [sb(n, [P, GROUP]) for n in ("r_max", "r_val", "r_sum", "r_slot")]
        r_cand, r_diff, r_exp, r_over, r_all, r_own = [
            sb(n, [P, GROUP, EXPERTS]) for n in ("r_cand", "r_diff", "r_exp", "r_over", "r_all", "r_own")]
        hot16 = sb("hot16", [P, GROUP, EXPERTS], BF16)
        tiles_before = [sb(f"tiles_before{i}", [P, GROUP, EXPERTS], BF16) for i in range(2)]
        to_slot = [sb(f"to_slot{i}", [P, GROUP], U32) for i in range(2)]

        wi_e = [sb(f"wi_e{i}", [P, HIDDEN]) for i in range(2)]
        wo_e = [sb(f"wo_e{i}", [P, HT, D]) for i in range(2)]
        tok = [sb(f"tok{i}", [P, 2, D]) for i in range(2)]
        side = [sb(f"side{i}", [P, 2, D + 2]) for i in range(2)]
        tok_t = [sb(f"tok_t{i}", [P, CAPACITY]) for i in range(2)]
        hid = [sb(f"hid{i}", [P, HT, CAPACITY]) for i in range(2)]
        e_out = [sb(f"e_out{i}", [P, 2, D]) for i in range(2)]
        place = [sb(f"place{i}", [P, 2], U32) for i in range(2)]
        empty = sb("empty", [P, ROW])
        pool_pause = sb("pool_pause", [P, 1])

        A, B, C, K, M, R, SB, TB = [bank(f"bank_{n}") for n in "abckmrst"]

        names = """early_in late_in shapes_in shapes16_in shapes16_set empty_set mhalf_set half_gnorm_set v_ones
            stats1 aggr1 veps1 rstd1 xn1_set xt1 xt1_out w12_done w12_set z_done abs_set exp_set ln_set min_set
            gk_set scan_set decay_set vg_done v_set tanh_set silu_set silu_n_set qk_done kf_set gated
            at_done att_set o_done sq_set ss_set ms_set rs_set gate_set og_set ogt_done ogt_out wo_done x1_set
            x1b_set stats2 aggr2 veps2 rstd2 xn2_set xt2 xt2_out q_done kv_done k1_set krest_set k2_set k3_set
            vaug_set q1_set qrest_set q2_set q3_set
            s_done max_set m1_set m2_set mt_done mt_out t_done exp2_set pv_done pv_out pvt_done den_set
            o2_set o2t_done o2t_out xo_done x2_set stats3 aggr3 veps3 rstd3 rr3_set veps4 rstd4 y_set xy_set z_set zt_done
            zt_out lg_done
            carried r_step r_sub r_expd hot_set rank_done idx_set tt_done tok_out h_done gelu_set eo_done eo_set
            """.split()
        N = {n: sem(n) for n in names}
        x_in = [sem(f"x_in{i}") for i in range(3)]
        ctx_in = [sem("ctx_in0"), sem("ctx_in1")]
        ks_in = [sem("ks_in0"), sem("ks_in1")]
        qs_in = [sem("qs_in0"), sem("qs_in1")]
        wi_in = [sem("wi_in0"), sem("wi_in1")]
        wo_in = [sem("wo_in0"), sem("wo_in1")]
        tok_in = [sem("tok_in0"), sem("tok_in1")]
        side_in = [sem("side_in0"), sem("side_in1")]
        sums_out = [sem("sums_out0"), sem("sums_out1")]
        rows_out = [sem("rows_out0"), sem("rows_out1")]
        returned = [sem("returned0"), sem("returned1")]

        def upto(g, n, k=None):
            j, par = g
            return (2 * j + par) * n + (n if k is None else k)

        def before(g, n):
            j, par = g
            return (2 * j + par) * n

        def initialise(eng, quarter, signal):
            n = SLOTS // P // 4
            eng.dma_start(slots.rearrange("(t p) d -> p t d", p=P)[:, quarter * n:(quarter + 1) * n, :],
                          empty[:, :].unsqueeze(1).to_broadcast([P, n, ROW])).then_inc(signal, 16)

        def slots_filled(eng):
            for par in range(2):
                eng.wait_ge(sums_out[par], 16 + 16 * (GROUPS // 2))
                eng.wait_ge(rows_out[par], 16 + 32 * (GROUPS // 2))

        R_STEPS = 10

        def is_first(g):
            return isinstance(g[0], int) and g == (0, 0)

        def wait_after(eng, signal, g, n, less):
            count = before(g, n) - less
            if not isinstance(count, int) or count > 0:
                eng.wait_ge(signal, count)

        def schedule(steps, loop, Fori):
            def stage(order, group_of):
                for name in order:
                    g = group_of(AHEAD[name[0]])
                    if g is not None and name in steps:
                        steps[name](g)

            def fixed(order, n):
                stage(order, lambda ahead: divmod(n + ahead, 2) if 0 <= n + ahead < GROUPS else None)

            for n in range(-max(AHEAD.values()), 0):
                fixed(FILL, n)
            fixed(loop, 0)
            with Fori(0, 2) as j:
                for n in (1, 2):
                    stage(loop, lambda ahead: (j + (n + ahead) // 2, (n + ahead) % 2))
            fixed(loop, 5)
            for n in range(6, GROUPS + 1):
                fixed(DRAIN, n)

        block = stack.enter_context(nc.Block())

        @block.sync
        def _(sp):
            def x_ctx(g):
                j, par = g
                wait_after(sp, N["kv_done"], g, 1, 1)
                sp.dma_start(ctx_g[par][:, :, :], ctx_t[:, bass.ds((2 * j + par) * GROUP, GROUP), :]
                             ).then_inc(ctx_in[par], 16)

            def load_x(i, first, last):
                sp.dma_start(x_all[:, first:last, :], x[:, first:last, :]).then_inc(x_in[i], 16)

            def c2(g):
                par = g[1]
                sp.wait_ge(N["k3_set"], upto(g, 1))
                wait_after(sp, N["t_done"], g, 8, 8)
                for c in range(8):
                    sp.dma_start(ks[par][c::8, :, :], k_part[K_PART[c]][:, :]).then_inc(ks_in[par], 16)

            def c4(g):
                par = g[1]
                sp.wait_ge(N["q3_set"], upto(g, 1))
                for c in range(8):
                    sp.dma_start(qs[par][c::8, :, :], q_part[Q_PART[c]][:, :]).then_inc(qs_in[par], 16)

            load_x(0, 0, GROUP)
            sp.dma_start(early[:, :], early_d).then_inc(N["early_in"], 16)
            load_x(1, GROUP, 2 * GROUP)
            sp.dma_start(shapes[:, :], shape_d).then_inc(N["shapes_in"], 16)
            sp.dma_start(late[:, :], late_d).then_inc(N["late_in"], 16)
            sp.dma_start(shapes_w[:, :], shape16_d).then_inc(N["shapes16_in"], 16)
            load_x(2, 2 * GROUP, SEQS)
            sp.wait_ge(N["empty_set"], 2)
            for i in range(2):
                initialise(sp, i, sums_out[i])

            def e1(g):
                j, par = g
                sp.wait_ge(N["xy_set"], upto(g, 1))
                sp.dma_start(out[:, bass.ds((2 * j + par) * GROUP, GROUP), :], rows[par][:, :, D:2 * D]
                             ).then_inc(sums_out[par], 16)

            def weights_in(j, par):
                sp.dma_start(wi_e[par][:, :], wi_d[:, bass.ds(2 * j + par, 1), :].rearrange("p o n -> p (o n)")
                             ).then_inc(wi_in[par], 16)

            def weights_out(j, par):
                sp.dma_start(wo_e[par][:, :, :], wo_d[:, bass.ds((2 * j + par) * HT, HT), :]
                             ).then_inc(wo_in[par], 16)

            for par in range(2):
                weights_in(0, par)
                weights_out(0, par)
            schedule({"x": x_ctx, "c2": c2, "c4": c4, "e1": e1}, LOOP_SP, sp.Fori)

            def slots_of(e):
                return slots.rearrange("(t p) d -> p t d", p=P)[:, bass.ds(e * 2, 2), :]

            def tokens(j, par):
                sp.dma_start(tok[par][:, :, :], slots_of(2 * j + par)[:, :, 0:D]).then_inc(tok_in[par], 16)

            def sides(j, par):
                sp.dma_start(side[par][:, :, :], slots_of(2 * j + par)[:, :, D:ROW]).then_inc(side_in[par], 16)

            slots_filled(sp)
            for par in range(2):
                tokens(0, par)
            for par in range(2):
                sides(0, par)

            def step(j, par, more_tokens=True, more_in=True):
                e = 2 * j + par
                if more_tokens:
                    sp.wait_ge(N["tt_done"], e + 3)
                    tokens(j + 2, par)
                if more_in:
                    sp.wait_ge(N["h_done"], 2 * e + 4)
                    weights_in(j + 1 + par, 1 - par)
                sp.wait_ge(N["eo_done"], e + 1)
                weights_out(j + 1, par)
                sp.wait_ge(N["eo_set"], e + 1)
                sides(j + 1, par)

            for par in range(2):
                sp.wait_ge(N["tt_done"], par + 1)
                tokens(1, par)
            sp.wait_ge(N["h_done"], 2)
            weights_in(1, 0)
            last = EXPERTS // 2 - 1
            with sp.Fori(0, last - 1) as j:
                step(j, 0)
                step(j, 1)
            step(last - 1, 0, more_tokens=False)
            step(last - 1, 1, more_tokens=False, more_in=False)
            for par in range(2):
                sp.wait_ge(returned[par], 32 * (EXPERTS // 2))

        @block.gpsimd
        def _(pool):
            pool.memset(mh[:, :], -0.5).then_inc(N["mhalf_set"], 1)
            pool.wait_ge(N["mhalf_set"], 1)

            def a0(g):
                pool.wait_ge(N["veps1"], upto(g, 1))
                pool.tensor_tensor(rs1[:, :], ve1[:, :], mh[:, 0:GROUP], ALU.pow).then_inc(N["rstd1"], 1)

            def a3(g):
                if is_first(g):
                    pool.wait_ge(N["empty_set"], 2)
                    for i in range(2):
                        initialise(pool, 2 + i, rows_out[i])
                pool.wait_ge(N["ln_set"], upto(g, 1))
                pool.wait_ge(N["min_set"], upto(g, 1))
                pool.tensor_tensor(gk[:, :], z_min[:, :], z_ln[:, :], ALU.subtract).then_inc(N["gk_set"], 1)

            def a5(g):
                par = g[1]
                if is_first(g):
                    pool.wait_ge(N["half_gnorm_set"], 1)
                for b in range(GROUP):
                    pool.wait_ge(N["silu_set"], upto(g, GROUP, b + 1))
                    pool.tensor_tensor(silu_n[par][:, b, :], silu2[:, b, :], half_gnorm[:, :], ALU.mult
                                       ).then_inc(N["silu_n_set"], 1)

            def b4(g):
                pool.wait_ge(N["ms_set"], upto(g, 1))
                pool.tensor_tensor(o_rs[:, :], o_ms[:, :], mh[:, 0:GROUP * GLA_HEADS], ALU.pow
                                   ).then_inc(N["rs_set"], 1)

            def b5(g):
                par = g[1]
                pool.wait_ge(N["rs_set"], upto(g, 1))
                pool.wait_ge(N["silu_n_set"], upto(g, GROUP))
                pool.tensor_tensor(o_gate[:, :, :].rearrange("p b (h e) -> p (b h) e", h=GLA_HEADS),
                                   silu_n[par][:, :, :].rearrange("p b (h e) -> p (b h) e", h=GLA_HEADS),
                                   o_rs[:, :].unsqueeze(2).to_broadcast([P, GROUP * GLA_HEADS, DV]),
                                   ALU.mult).then_inc(N["gate_set"], 1)

            def c1(g):
                par = g[1]
                pool.wait_ge(N["veps2"], upto(g, 1))
                pool.tensor_tensor(rs2[:, :], ve2[:, :], mh[:, 0:GROUP], ALU.pow).then_inc(N["rstd2"], 1)
                if is_first(g):
                    pool.wait_ge(N["late_in"], 16)
                wait_after(pool, N["x2_set"], g, GROUP, GROUP)
                pool.tensor_tensor(x1b[par][:, :, :], x1[:, :, :],
                                   Lt("bo").unsqueeze(1).to_broadcast([P, GROUP, D]), ALU.add
                                   ).then_inc(N["x1b_set"], 1)

            def c2(g):
                pool.wait_ge(N["k2_set"], upto(g, 1))
                pool.tensor_tensor(k_part[2][:, :], k_rest[:, :], k_part[1][:, :], ALU.subtract
                                   ).then_inc(N["k3_set"], 1)

            def e0(g):
                pool.wait_ge(N["veps3"], upto(g, 1))
                pool.tensor_tensor(rs3[:, :], ve3[:, :], mh[:, 0:GROUP], ALU.pow).then_inc(N["rstd3"], 1)

            def e1(g):
                j, par = g
                pool.wait_ge(sums_out[par], 16 + 16 * j)
                pool.wait_ge(rows_out[par], 16 + 32 * j)
                pool.wait_ge(N["veps4"], upto(g, 1))
                pool.tensor_tensor(rs4[:, :], ve4[:, :], mh[:, 0:GROUP], ALU.pow).then_inc(N["rstd4"], 1)
                pool.wait_ge(N["y_set"], upto(g, 1))
                pool.tensor_tensor(rows[par][:, :, D:2 * D], x2[par][:, :, :], y[:, :, :], ALU.add
                                   ).then_inc(N["xy_set"], 1)

            def carry():
                pool.tensor_tensor(pool_pause[:, :], mh[:, 0:1], mh[:, 0:1], ALU.mult
                                   ).then_inc(N["carried"], 1)

            def f4(g):
                par = g[1]
                pool.wait_ge(sums_out[1 - par], 16)
                pool.wait_ge(rows_out[1 - par], 16)
                pool.wait_ge(N["xy_set"], upto(g, 1))
                pool.wait_ge(N["idx_set"], upto(g, 1))
                carry()
                for b in range(GROUP):
                    pool.indirect_dma_start(
                        out=slots, out_offset=bass.IndirectOffsetOnAxis(ap=to_slot[par][:, b:b + 1], axis=0),
                        in_=rows[par][:, b, :], in_offset=None, bounds_check=SLOTS - 1, oob_is_err=False
                        ).then_inc(rows_out[par], 16)

            schedule({"a0": a0, "a3": a3, "a5": a5, "b4": b4, "b5": b5, "c1": c1, "c2": c2,
                      "e0": e0, "e1": e1, "f4": f4}, LOOP_POOL, pool.Fori)

            slots_filled(pool)
            with pool.Fori(0, EXPERTS // 2) as j:
                for par in range(2):
                    pool.wait_ge(N["carried"], GROUPS + 2 * j + par)
                    pool.wait_ge(N["eo_set"], 2 * j + par + 1)
                    carry()
                    for c in range(2):
                        pool.indirect_dma_start(
                            out=out.rearrange("p i d -> (p i) d"),
                            out_offset=bass.IndirectOffsetOnAxis(ap=place[par][:, c:c + 1], axis=0),
                            in_=e_out[par][:, c, :], in_offset=None, bounds_check=SEQS * L - 1, oob_is_err=False
                            ).then_inc(returned[par], 16)

        @block.tensor
        def _(pe):
            pe.wait_ge(N["early_in"], 16)
            ident = E("ident")

            def a1(g):
                pe.wait_ge(N["silu_set"], before(g, GROUP))
                pe.wait_ge(N["xn1_set"], upto(g, 1))
                for b in range(GROUP):
                    mm = pe.transpose(A[:, b * L:(b + 1) * L], xn1[:, b, :], ident)
                mm.then_inc(N["xt1"], 1)

            def a3(g):
                pe.wait_ge(N["xt1_out"], upto(g, 1))
                pe.matmul(A[:, 0:T], w12[:, :], xn1_t[:, :], start=True, stop=True).then_inc(N["z_done"], 1)
                pe.matmul(B[:, 0:T], E("q"), xn1_t[:, :], start=True, stop=True)
                pe.matmul(B[:, T:2 * T], E("k"), xn1_t[:, :], start=True, stop=True).then_inc(N["qk_done"], 1)

            def a5(g):
                pe.wait_ge(N["abs_set"], upto(g, 1))
                pe.wait_ge(N["min_set"], upto(g, 1))
                pe.matmul(A[:, :], xn1_t[:, 0:L], E("vg"), start=True, stop=True).then_inc(N["vg_done"], 1)
                pe.wait_ge(N["gated"], upto(g, 1))
                pe.matmul(B[:, :], xn1_t[:, L:T], E("vg"), start=True, stop=True).then_inc(N["vg_done"], 1)

            def b_scores(half):
                def piece(g):
                    par = g[1]
                    if half == 0:
                        pe.wait_ge(N["og_set"], before(g, 1))
                        pe.wait_ge(N["gated"], upto(g, 1))
                    else:
                        pe.wait_ge(N["att_set"], upto(g, 2, 1))
                    for i in range(2):
                        if i:
                            pe.wait_ge(N["at_done"], upto(g, 4, 2 * half + 1))
                        rows = slice(DK * (2 * half + i), DK * (2 * half + i + 1))
                        for b in range(GROUP):
                            at = (i * GROUP + b) * L
                            pe.matmul(C[0:CHUNK, at:at + CHUNK], k_first[par][rows, b, :],
                                      qg[par][rows, b, 0:CHUNK], start=True, stop=True)
                            mm = pe.matmul(C[:, at + CHUNK:at + L], k_second[par][rows, b, :],
                                           qg[par][rows, b, CHUNK:L], start=True, stop=True)
                        mm.then_inc(N["at_done"], 1)
                return piece

            def b4(g):
                par = g[1]
                pe.wait_ge(N["v_set"], upto(g, GROUP))
                pe.wait_ge(N["att_set"], upto(g, 2))
                for b in range(GROUP):
                    for h in range(GLA_HEADS):
                        at = (b * GLA_HEADS + h) * DV
                        mm = pe.matmul(C[:, at:at + DV], att[:, h, b, :], v_sb[par][:, b, h * DV:(h + 1) * DV],
                                       start=True, stop=True)
                mm.then_inc(N["o_done"], 1)

            def c0(g):
                par = g[1]
                pe.wait_ge(N["qrest_set"], before(g, 1))
                pe.wait_ge(N["og_set"], upto(g, 1))
                for b in range(GROUP):
                    for c in range(2):
                        at = (2 * b + c) * L
                        mm = pe.transpose(K[:, at:at + L], og[par][:, b, c * P:(c + 1) * P], ident)
                mm.then_inc(N["ogt_done"], 1)

            def c1(g):
                if is_first(g):
                    pe.wait_ge(N["late_in"], 16)
                pe.wait_ge(N["ogt_out"], upto(g, 1))
                for b in range(GROUP):
                    for c in range(2):
                        mm = pe.matmul(K[:, b * D:(b + 1) * D], og_t[:, b, c, :],
                                       Lt("wo")[:, c * D:(c + 1) * D], start=(c == 0), stop=(c == 1))
                mm.then_inc(N["wo_done"], 1)

            def c2(g):
                j, par = g
                pe.wait_ge(ctx_in[par], 16 * (j + 1))
                pe.wait_ge(N["x1_set"], upto(g, 1))
                pe.matmul(K[:, 0:GROUP * KEYS], Lt("xk"), ctx_g[par][:, :, :].rearrange("p b k -> p (b k)"),
                          start=True, stop=True)
                for b in range(GROUP):
                    mm = pe.matmul(K[0:KEYS, T + b * D:T + (b + 1) * D], ctx_g[par][:, b, :], Lt("xv"),
                                   start=True, stop=True)
                mm.then_inc(N["kv_done"], 1)

            def c3(g):
                pe.wait_ge(N["vaug_set"], upto(g, 1))
                pe.wait_ge(N["krest_set"], upto(g, 1))
                pe.wait_ge(N["xn2_set"], upto(g, 1))
                for b in range(GROUP):
                    mm = pe.transpose(K[:, b * L:(b + 1) * L], xn2[:, b, :], ident)
                mm.then_inc(N["xt2"], 1)

            def c4(g):
                pe.wait_ge(N["xt2_out"], upto(g, 1))
                pe.matmul(K[:, 0:T], Lt("xq"), xn2_t[:, :], start=True, stop=True).then_inc(N["q_done"], 1)

            def heads(u):
                return u % 2, slice(64 * (u % 2), 64 * (u % 2) + 64), range(4 * (u // 2), 4 * (u // 2) + 4)

            def s(b, u):
                def piece(g):
                    j, par = g
                    if b == 0 and u == 0:
                        pe.wait_ge(ks_in[par], 128 * (j + 1))
                        pe.wait_ge(qs_in[par], 128 * (j + 1))
                    pe.wait_ge(N["max_set"], before(g, 8) + 4 * b + u)
                    two, rows, pairs = heads(u)
                    for i, pair in enumerate(pairs):
                        mm = pe.matmul(SB[:, i * KEYS:(i + 1) * KEYS], qs[par][rows, pair, b * L:(b + 1) * L],
                                       ks[par][rows, pair, b * KEYS:(b + 1) * KEYS], start=True, stop=True)
                    mm.then_inc(N["s_done"], 1)
                return piece

            def m(b):
                def piece(g):
                    wait_after(pe, N["exp2_set"], g, 8, -4 * b)
                    if b == 0 and is_first(g):
                        pe.wait_ge(N["shapes16_set"], 1)
                    pe.wait_ge(N["m2_set"], before(g, GROUP) + b + 1)
                    pe.transpose(TB[:, 0:P // 2].bitcast(BF16), max_part[:, :, :, :].rearrange("p w c a -> p (w c a)"),
                                 S16("ident")).then_inc(N["mt_done"], 1)
                return piece

            def t(b, u):
                def piece(g):
                    par = g[1]
                    two, rows, pairs = heads(u)
                    if u == 0:
                        pe.wait_ge(N["mt_out"], before(g, GROUP) + b + 1)
                    else:
                        pe.wait_ge(N["exp2_set"], before(g, 8) + 4 * b + u)
                    for i, pair in enumerate(pairs):
                        pe.matmul(TB[0:KEYS, i * L:(i + 1) * L], ks[par][rows, pair, b * KEYS:(b + 1) * KEYS],
                                  qs[par][rows, pair, b * L:(b + 1) * L], start=True, stop=False)
                        mm = pe.matmul(TB[0:KEYS, i * L:(i + 1) * L], pick[rows, pair, :], max_t[rows, :],
                                       start=False, stop=True)
                    mm.then_inc(N["t_done"], 1)
                return piece

            def o0(b):
                def piece(g):
                    par = g[1]
                    n = before(g, GROUP) + b
                    pe.wait_ge(N["x2_set"], n)
                    if b == 0:
                        pe.wait_ge(N["vaug_set"], upto(g, 1))
                    pe.wait_ge(N["exp2_set"], before(g, 8) + 4 * b + 4)
                    for u in range(4):
                        two, _, pairs = heads(u)
                        for i, pair in enumerate(pairs):
                            mm = pe.matmul(M[TILE * i:TILE * (i + 1), u * L:(u + 1) * L],
                                           v_aug[par][:, b, 2 * pair + two, :], prob[b][:, u, i, :],
                                           start=True, stop=True)
                    mm.then_inc(N["pv_done"], 1)
                return piece

            def o1(b):
                def piece(g):
                    pe.wait_ge(N["pv_out"], before(g, GROUP) + b + 1)
                    for u in range(4):
                        mm = pe.transpose(M[:, u * P:(u + 1) * P], pv[:, u * L:(u + 1) * L], ident)
                    mm.then_inc(N["pvt_done"], 1)
                return piece

            def o2_(b):
                def piece(g):
                    pe.wait_ge(N["o2_set"], before(g, GROUP) + b + 1)
                    pe.transpose(M[:, 0:L], o2[:, :, :].rearrange("p h e -> p (h e)"), ident
                                 ).then_inc(N["o2t_done"], 1)
                return piece

            def o3(b):
                def piece(g):
                    pe.wait_ge(N["o2t_out"], before(g, GROUP) + b + 1)
                    pe.matmul(M[:, 0:D], o2_t[:, :], Lt("xo"), start=True, stop=True).then_inc(N["xo_done"], 1)
                return piece

            def e3(g):
                pe.wait_ge(N["z_set"], upto(g, 1))
                for b in range(GROUP):
                    mm = pe.transpose(R[:, b * L:(b + 1) * L], rows[g[1]][:, b, 0:D], ident)
                mm.then_inc(N["zt_done"], 1)

            def e4(g):
                pe.wait_ge(N["zt_out"], upto(g, 1))
                for b in range(GROUP):
                    mm = pe.matmul(R[:, b * EXPERTS:(b + 1) * EXPERTS], z_t[:, b * L:(b + 1) * L], Lt("gate"),
                                   start=True, stop=True)
                mm.then_inc(N["lg_done"], 1)

            def keep_busy(n):
                for _ in range(n):
                    pe.matmul(R[:, :], S16("ident"), shapes16[:, 0:512], start=True, stop=True)

            def busy(first=False):
                def piece(g):
                    pe.wait_ge(N["shapes16_set"], 1)
                    if first:
                        pe.wait_ge(N["idx_set"], upto(g, 1))
                    keep_busy(FILLER)
                return piece

            def f2(g):
                at = GROUP * EXPERTS
                pe.wait_ge(N["hot_set"], upto(g, 1))
                pe.matmul(R[:, 0:at], S16("before"), hot16[:, :, :].rearrange("p b e -> p (b e)"),
                          start=True, stop=False)
                pe.matmul(R[:, 0:at], S16("ones"), tiles_before[g[1]][:, :, :].rearrange("p b e -> p (b e)"),
                          start=False, stop=True).then_inc(N["rank_done"], 1)

            pe.matmul(A[:, 0:D], E("w1_t")[0:RANK, :], E("w2")[0:RANK, :], start=True, stop=True
                      ).then_inc(N["w12_done"], 1)
            pe.wait_ge(N["w12_set"], 1)
            schedule({"a1": a1, "a3": a3, "a5": a5, "b0": b_scores(0), "b1": b_scores(1),
                      "b4": b4, "c0": c0, "c1": c1, "c2": c2, "c3": c3,
                      "c4": c4, "s00": s(0, 0), "s01": s(0, 1), "s02": s(0, 2), "s03": s(0, 3),
                      "s10": s(1, 0), "s11": s(1, 1), "s12": s(1, 2), "s13": s(1, 3),
                      "m0": m(0), "m1": m(1),
                      "t00": t(0, 0), "t01": t(0, 1), "t02": t(0, 2), "t03": t(0, 3),
                      "t10": t(1, 0), "t11": t(1, 1), "t12": t(1, 2), "t13": t(1, 3),
                      "o0": o0(0), "o1": o1(0), "o2": o2_(0), "o3": o3(0),
                      "r0": o0(1), "r1": o1(1), "r2": o2_(1), "r3": o3(1), "e3": e3, "e4": e4, "f2": f2,
                      "v0": busy(first=True), "w0": busy(), "w1": busy(), "w2": busy()}, LOOP_PE, pe.Fori)

            def transposes(j, par):
                t_bank = (A, B)[par]
                pe.wait_ge(tok_in[par], 16 * (j + 1))
                for c in range(2):
                    mm = pe.transpose(t_bank[:, c * P:(c + 1) * P], tok[par][:, c, :], ident)
                mm.then_inc(N["tt_done"], 1)

            def hidden(j, par):
                h_banks = ((SB, R), (TB, K))[par]
                pe.wait_ge(N["tok_out"], 2 * j + par + 1)
                pe.wait_ge(wi_in[par], 16 * (j + 1))
                for i in range(HT):
                    mm = pe.matmul(h_banks[i // 2][:, (i % 2) * CAPACITY:(i % 2 + 1) * CAPACITY],
                                   wi_e[par][:, i * P:(i + 1) * P], tok_t[par][:, :], start=True, stop=True)
                    if i % 2:
                        mm.then_inc(N["h_done"], 1)

            def rows_made(j, par):
                e = 2 * j + par
                o_bank = (C, M)[par]
                pe.wait_ge(wo_in[par], 16 * (j + 1))
                if not isinstance(j, int) or j:
                    pe.wait_ge(N["eo_set"], e - 1)
                for c in range(2):
                    for i in range(HT):
                        if c == 0 and i % 2 == 0:
                            pe.wait_ge(N["gelu_set"], 2 * e + i // 2 + 1)
                        mm = pe.matmul(o_bank[:, c * D:(c + 1) * D], hid[par][:, i, c * P:(c + 1) * P],
                                       wo_e[par][:, i, :], start=(i == 0), stop=(i == HT - 1))
                mm.then_inc(N["eo_done"], 1)

            pe.wait_ge(N["idx_set"], GROUPS)
            keep_busy(EXPERT_FILLER)
            transposes(0, 0)
            transposes(0, 1)
            hidden(0, 0)
            last = EXPERTS // 2 - 1

            def two_experts(j):
                transposes(j + 1, 0)
                hidden(j, 1)
                rows_made(j, 0)
                transposes(j + 1, 1)
                hidden(j + 1, 0)
                rows_made(j, 1)

            two_experts(0)
            with pe.Fori(1, last) as j:
                two_experts(j)
            hidden(last, 1)
            rows_made(last, 0)
            rows_made(last, 1)

        @block.scalar
        def _(act):
            act.preload_act_table_set(LN_EXP)
            act.wait_ge(N["early_in"], 16)
            act.wait_ge(N["w12_done"], 1)
            act.activation(w12[:, :], A[:, 0:D], ACT.Identity).then_inc(N["w12_set"], 1)

            def a1(g):
                act.wait_ge(N["vg_done"], before(g, GROUP))
                act.wait_ge(N["xt1"], upto(g, 1))
                act.activation(xn1_t[:, :], A[:, 0:T], ACT.Identity).then_inc(N["xt1_out"], 1)

            def a3(g):
                act.wait_ge(N["z_done"], upto(g, 1))
                act.activation(z_abs[:, :], A[:, 0:T], ACT.Abs, bias=E("b2")).then_inc(N["abs_set"], 1)
                act.wait_ge(N["abs_set"], upto(g, 1))
                act.activation(z_exp[:, :], z_abs[:, :], ACT.Exp, scale=-1.0).then_inc(N["exp_set"], 1)
                act.wait_ge(N["exp_set"], upto(g, 1))
                act.wait_ge(N["gk_set"], before(g, 1))
                act.activation(z_ln[:, :], z_exp[:, :], ACT.Ln, bias=1.0).then_inc(N["ln_set"], 1)

            def a4(g):
                act.wait_ge(N["gated"], before(g, 1))
                act.wait_ge(N["scan_set"], upto(g, 1))
                act.activation(e_pos[:, :], bcum[:, :], ACT.Exp, scale=1.0 / GATE_NORM)
                act.activation(e_neg[:, :], bcum[:, :], ACT.Exp, scale=-1.0 / GATE_NORM).then_inc(N["decay_set"], 1)

            def a5(g):
                par = g[1]
                wait_after(act, N["o_done"], g, 1, 1)
                for b in range(GROUP):
                    act.wait_ge(N["vg_done"], upto(g, GROUP, b + 1))
                    act.activation(v_sb[par][:, b, :], (A, B)[b][:, 0:256], ACT.Identity).then_inc(N["v_set"], 1)
                for b in range(GROUP):
                    act.wait_ge(N["silu_set"], before(g, GROUP) + b)
                    act.activation(th[:, b, :], (A, B)[b][:, 256:512], ACT.Tanh, scale=0.5
                                   ).then_inc(N["tanh_set"], 1)
                act.preload_act_table_set(LN_EXP)

            def b4(g):
                act.wait_ge(N["ss_set"], before(g, 1))
                act.wait_ge(N["o_done"], upto(g, 1))
                act.activation(o_sq[:, :, :].rearrange("p h e -> p (h e)"), C[:, :], ACT.Square
                               ).then_inc(N["sq_set"], 1)

            def c0(g):
                act.wait_ge(N["wo_done"], before(g, 1))
                act.wait_ge(N["ogt_done"], upto(g, 1))
                act.activation(og_t[:, :, :, :].rearrange("p b c t -> p (b c t)"), K[:, :], ACT.Identity
                               ).then_inc(N["ogt_out"], 1)

            def c2(g):
                j, par = g
                landed = 128 * (j + par)
                if not isinstance(landed, int) or landed:
                    act.wait_ge(ks_in[1 - par], landed)
                act.wait_ge(N["kv_done"], upto(g, 1))
                act.activation(k_part[0][:, :], K[:, 0:GROUP * KEYS], ACT.Identity, bias=E("bk")
                               ).then_inc(N["k1_set"], 1)
                wait_after(act, N["pv_done"], g, GROUP, GROUP)
                act.activation(v_aug[par][:, :, :, 0:DEPTH],
                               K[0:KEYS, T:2 * T].rearrange("p (b h e) -> p b h e", b=GROUP, h=HEADS),
                               ACT.Identity).then_inc(N["vaug_set"], 1)
                act.wait_ge(N["krest_set"], upto(g, 1))
                act.activation(k_part[1][:, :], k_rest[:, :], ACT.Identity).then_inc(N["k2_set"], 1)

            def c3(g):
                act.wait_ge(N["q_done"], before(g, 1))
                act.wait_ge(N["xt2"], upto(g, 1))
                act.activation(xn2_t[:, :], K[:, 0:T], ACT.Identity).then_inc(N["xt2_out"], 1)

            def c4(g):
                j, par = g
                landed = 128 * (j + par)
                if not isinstance(landed, int) or landed:
                    act.wait_ge(qs_in[1 - par], landed)
                act.wait_ge(N["q_done"], upto(g, 1))
                act.activation(q_part[0][:, :], K[:, 0:T], ACT.Identity, bias=E("bq")).then_inc(N["q1_set"], 1)

            def m(b):
                def piece(g):
                    wait_after(act, N["t_done"], g, 8, -4 * b)
                    act.wait_ge(N["mt_done"], before(g, GROUP) + b + 1)
                    act.activation(max_t[:, :], TB[:, 0:P // 2].bitcast(BF16), ACT.Identity
                                   ).then_inc(N["mt_out"], 1)
                return piece

            def t(b, u):
                def piece(g):
                    if u == 0:
                        wait_after(act, N["pv_done"], g, GROUP, 1 - b)
                    act.wait_ge(N["t_done"], before(g, 8) + 4 * b + u + 1)
                    act.activation(prob[b][:, u, :, :].rearrange("p a t -> p (a t)"), TB[0:KEYS, :],
                                   ACT.Exp, scale=float(DEPTH) ** -0.5).then_inc(N["exp2_set"], 1)
                return piece

            def o0(b):
                def piece(g):
                    n = before(g, GROUP) + b
                    act.wait_ge(N["pvt_done"], n)
                    act.wait_ge(N["pv_done"], n + 1)
                    act.activation(pv[:, :], M[:, :], ACT.Identity).then_inc(N["pv_out"], 1)
                return piece

            def o2_(b):
                def piece(g):
                    act.wait_ge(N["o2t_done"], before(g, GROUP) + b + 1)
                    act.activation(o2_t[:, :], M[:, 0:L], ACT.Identity, bias=E("bv")).then_inc(N["o2t_out"], 1)
                return piece

            def e3(g):
                act.wait_ge(N["zt_done"], upto(g, 1))
                act.activation(z_t[:, :], R[:, 0:T], ACT.Identity, bias=E("beta"), scale=E("gamma")
                               ).then_inc(N["zt_out"], 1)

            def f0(g):
                act.wait_ge(N["r_sub"], upto(g, 1))
                act.activation(r_exp[:, :, :], r_diff[:, :, :], ACT.Exp).then_inc(N["r_expd"], 1)

            schedule({"a1": a1, "a3": a3, "a4": a4, "a5": a5, "b4": b4, "c0": c0, "c2": c2, "c3": c3,
                      "c4": c4, "m0": m(0), "m1": m(1),
                      "t00": t(0, 0), "t01": t(0, 1), "t02": t(0, 2), "t03": t(0, 3),
                      "t10": t(1, 0), "t11": t(1, 1), "t12": t(1, 2), "t13": t(1, 3),
                      "o0": o0(0), "o2": o2_(0), "r0": o0(1), "r2": o2_(1), "e3": e3, "f0": f0}, LOOP_ACT, act.Fori)

            def tokens_out(j, par):
                act.wait_ge(N["tt_done"], 2 * j + par + 1)
                act.activation(tok_t[par][:, :], (A, B)[par][:, 0:CAPACITY], ACT.Identity, bias=E("beta"),
                               scale=E("gamma")).then_inc(N["tok_out"], 1)

            def gelus(j, par):
                for i in range(2):
                    act.wait_ge(N["h_done"], 2 * (2 * j + par) + i + 1)
                    act.activation(hid[par][:, 2 * i:2 * i + 2, :].rearrange("p a t -> p (a t)"),
                                   ((SB, R), (TB, K))[par][i][:, :], ACT.Gelu).then_inc(N["gelu_set"], 1)

            tokens_out(0, 0)
            tokens_out(0, 1)
            gelus(0, 0)
            last = EXPERTS // 2 - 1
            with act.Fori(0, last) as j:
                tokens_out(j + 1, 0)
                gelus(j, 1)
                tokens_out(j + 1, 1)
                gelus(j + 1, 0)
            gelus(last, 1)

        @block.vector
        def _(dve):
            dve.memset(empty[:, 0:ROW - 1], 0.0).then_inc(N["empty_set"], 1)
            dve.memset(empty[:, ROW - 1:ROW], float(2 * SEQS * L)).then_inc(N["empty_set"], 1)

            def fill_a0():
                dve.memset(max_part[:, :, :, :], 0.0)

            def fill_a1():
                dve.memset(att[:, :, :, :], 0.0)

            def fill_a3():
                dve.wait_ge(N["shapes_in"], 16)
                dve.tensor_copy(tiles_before[0][:, 0, :], S("ebase"))
                dve.wait_ge(N["late_in"], 16)
                dve.tensor_scalar(half_gnorm[:, :], Lt("gnorm"), 0.5, None, ALU.mult).then_inc(N["half_gnorm_set"], 1)

            def fill_a5():
                dve.wait_ge(N["shapes16_in"], 16)
                dve.tensor_copy(shapes16[:, :], shapes_w[:, :]).then_inc(N["shapes16_set"], 1)
                for i in range(2):
                    dve.memset(v_aug[i][:, :, :, DEPTH:TILE], 0.0).then_inc(N["v_ones"], 1)
                    dve.wait_ge(N["v_ones"], i + 1)
                    dve.memset(v_aug[i][:, :, :, DEPTH:DEPTH + 1], 1.0)

            def norm_stats(src, st, mv, ve, s_stats, s_aggr, s_veps, g):
                for b in range(GROUP):
                    dve.bn_stats(st[:, b, :], src[:, b, :]).then_inc(s_stats, 1)
                dve.wait_ge(s_stats, upto(g, GROUP))
                dve.memset(pause[:, :], 0.0)
                for b in range(GROUP):
                    dve.bn_aggr(mv[:, b, :], st[:, b, :]).then_inc(s_aggr, 1)
                dve.wait_ge(s_aggr, upto(g, GROUP))
                dve.tensor_scalar(ve[:, :], mv[:, :, 1], EPS, None, ALU.add).then_inc(s_veps, 1)

            def group_of(a, g):
                return a[:, bass.ds((2 * g[0] + g[1]) * GROUP, GROUP), :]

            def tk(a):
                return a.rearrange("p (b t) -> p b t", b=GROUP)

            def a0(g):
                j, par = g
                if isinstance(j, int) and 2 * j + par < 3:
                    dve.wait_ge(x_in[2 * j + par], 16)
                norm_stats(group_of(x_all, g), st1, mv1, ve1, N["stats1"], N["aggr1"], N["veps1"], g)
                if is_first(g):
                    fill_a0()

            def a1(g):
                par = g[1]
                dve.wait_ge(N["rstd1"], upto(g, 1))
                for b in range(GROUP):
                    op = dve.tensor_scalar(xn1[:, b, :], group_of(x_all, g)[:, b, :], mv1[:, b, 0:1], rs1[:, b:b + 1],
                                           ALU.subtract, ALU.mult)
                op.then_inc(N["xn1_set"], 1)
                if is_first(g):
                    fill_a1()
                    dve.wait_ge(N["early_in"], 16)

            def a3(g):
                dve.wait_ge(N["abs_set"], upto(g, 1))
                dve.tensor_scalar(z_min[:, :], A[:, 0:T], E("b2"), 0.0, ALU.add, ALU.min).then_inc(N["min_set"], 1)
                if is_first(g):
                    fill_a3()

            def a4(g):
                par = g[1]
                dve.wait_ge(N["gk_set"], upto(g, 1))
                dve.tensor_tensor_scan(bcum[:, :], S("reset"), gk[:, :], 0.0, ALU.mult, ALU.add
                                       ).then_inc(N["scan_set"], 1)

            def a45(g):
                par = g[1]
                dve.wait_ge(N["decay_set"], upto(g, 1))
                dve.wait_ge(N["qk_done"], upto(g, 1))
                dve.scalar_tensor_tensor(qg[par][:, :, :], tk(B[:, 0:T]), float(DK) ** -0.5, tk(e_pos[:, :]),
                                         ALU.mult, ALU.mult)
                dve.tensor_tensor(k_second[par][:, :, CHUNK:L], tk(B[:, T:2 * T])[:, :, CHUNK:L],
                                  tk(e_neg[:, :])[:, :, CHUNK:L], ALU.mult)
                dve.tensor_tensor(k_first[par][:, :, :], tk(B[:, T:2 * T])[:, :, 0:CHUNK],
                                  tk(e_neg[:, :])[:, :, 0:CHUNK], ALU.mult).then_inc(N["kf_set"], 1)
                dve.wait_ge(N["kf_set"], upto(g, 1))
                dve.tensor_tensor(k_second[par][:, :, 0:CHUNK], k_first[par][:, :, :],
                                  tk(e_pos[:, :])[:, :, CHUNK - 1:CHUNK].to_broadcast([P, GROUP, CHUNK]),
                                  ALU.mult).then_inc(N["gated"], 1)

            def a5(g):
                for b in range(GROUP):
                    dve.wait_ge(N["silu_n_set"], before(g, GROUP) + b)
                    dve.wait_ge(N["tanh_set"], upto(g, GROUP, b + 1))
                    dve.scalar_tensor_tensor(silu2[:, b, :], th[:, b, :], 1.0, (A, B)[b][:, 256:512],
                                             ALU.add, ALU.mult).then_inc(N["silu_set"], 1)
                if is_first(g):
                    fill_a5()

            def b_mask(half):
                def piece(g):
                    dve.wait_ge(N["at_done"], upto(g, 4, 2 * half + 2))
                    to = att[:, 2 * half:2 * half + 2, :, :].rearrange("p h b t -> p (h b) t")
                    scores = C[:, :].rearrange("p (c t) -> p c t", t=L)
                    for rows, queries in ((CHUNK, slice(0, CHUNK)), (L, slice(CHUNK, L))):
                        op = dve.tensor_tensor(
                            to[0:rows, :, queries], scores[0:rows, :, queries],
                            S("causal")[0:rows, queries].unsqueeze(1).to_broadcast([rows, 2 * GROUP, CHUNK]),
                            ALU.mult)
                    op.then_inc(N["att_set"], 1)
                return piece

            def b4(g):
                dve.wait_ge(N["sq_set"], upto(g, 1))
                dve.tensor_reduce(o_ss[:, :], o_sq[:, :, :], AX.X, ALU.add).then_inc(N["ss_set"], 1)
                dve.wait_ge(N["ss_set"], upto(g, 1))
                dve.tensor_scalar(o_ms[:, :], o_ss[:, :], 1.0 / DV, EPS, ALU.mult, ALU.add).then_inc(N["ms_set"], 1)

            def b5(g):
                par = g[1]
                dve.wait_ge(N["gate_set"], upto(g, 1))
                wait_after(dve, N["ogt_done"], g, 1, 1)
                dve.tensor_tensor(og[par][:, :, :].rearrange("p b c -> p (b c)"), C[:, :],
                                  o_gate[:, :, :].rearrange("p b c -> p (b c)"), ALU.mult).then_inc(N["og_set"], 1)

            def c1(g):
                j, par = g
                dve.wait_ge(N["x1b_set"], before(g, 1))
                dve.wait_ge(N["wo_done"], upto(g, 1))
                dve.tensor_tensor(x1[:, :, :].rearrange("p b d -> p (b d)"), K[:, 0:GROUP * D],
                                  group_of(x_all, g).rearrange("p b d -> p (b d)"), ALU.add
                                  ).then_inc(N["x1_set"], 1)
                dve.wait_ge(N["x1_set"], upto(g, 1))
                norm_stats(x1, st2, mv2, ve2, N["stats2"], N["aggr2"], N["veps2"], g)

            def c2(g):
                dve.wait_ge(N["k3_set"], before(g, 1))
                dve.wait_ge(N["vaug_set"], upto(g, 1))
                dve.wait_ge(N["k1_set"], upto(g, 1))
                dve.scalar_tensor_tensor(k_rest[:, :], K[:, 0:GROUP * KEYS], E("bk"), k_part[0][:, :],
                                         ALU.add, ALU.subtract).then_inc(N["krest_set"], 1)

            def c3(g):
                dve.wait_ge(N["rstd2"], upto(g, 1))
                for b in range(GROUP):
                    op = dve.tensor_scalar(xn2[:, b, :], x1[:, b, :], mv2[:, b, 0:1], rs2[:, b:b + 1],
                                           ALU.subtract, ALU.mult)
                op.then_inc(N["xn2_set"], 1)

            def c4(g):
                dve.wait_ge(N["q1_set"], upto(g, 1))
                dve.scalar_tensor_tensor(q_rest[:, :], K[:, 0:T], E("bq"), q_part[0][:, :],
                                         ALU.add, ALU.subtract).then_inc(N["qrest_set"], 1)
                dve.wait_ge(N["qrest_set"], upto(g, 1))
                dve.tensor_copy(q_part[1][:, :], q_rest[:, :]).then_inc(N["q2_set"], 1)
                dve.wait_ge(N["q2_set"], upto(g, 1))
                dve.tensor_tensor(q_part[2][:, :], q_rest[:, :], q_part[1][:, :], ALU.subtract
                                  ).then_inc(N["q3_set"], 1)

            def s(b, u):
                def piece(g):
                    dve.wait_ge(N["s_done"], before(g, 8) + 4 * b + u + 1)
                    dve.tensor_reduce(max_neg[:, u % 2, 4 * (u // 2):4 * (u // 2) + 4],
                                      SB[:, 0:4 * KEYS].rearrange("p (a k) -> p a k", a=4),
                                      AX.X, ALU.max, negate=True).then_inc(N["max_set"], 1)
                return piece

            def m(b):
                def piece(g):
                    n = before(g, GROUP) + b
                    wait_after(dve, N["mt_done"], g, GROUP, -b)
                    dve.wait_ge(N["max_set"], before(g, 8) + 4 * b + 4)
                    dve.tensor_copy(max_part[:, :, 0, :], max_neg[:, :, :]).then_inc(N["m1_set"], 1)
                    dve.wait_ge(N["m1_set"], n + 1)
                    dve.tensor_tensor(max_part[:, :, 1, :], max_neg[:, :, :], max_part[:, :, 0, :], ALU.subtract
                                      ).then_inc(N["m2_set"], 1)
                return piece

            def o1(b):
                def piece(g):
                    n = before(g, GROUP) + b
                    sums = M[:, :].rearrange("p (h e) -> p h e", h=HEADS)
                    dve.wait_ge(N["pvt_done"], n + 1)
                    dve.reciprocal(den[:, :], sums[:, :, DEPTH]).then_inc(N["den_set"], 1)
                    dve.wait_ge(N["den_set"], n + 1)
                    dve.tensor_tensor(o2[:, :, :], sums[:, :, 0:DEPTH],
                                      den[:, :].unsqueeze(2).to_broadcast([P, HEADS, DEPTH]), ALU.mult
                                      ).then_inc(N["o2_set"], 1)
                return piece

            def o3(b):
                def piece(g):
                    par = g[1]
                    if b == 0:
                        dve.wait_ge(N["x1b_set"], upto(g, 1))
                    dve.wait_ge(N["xo_done"], before(g, GROUP) + b + 1)
                    dve.tensor_tensor(x2[par][:, b, :], M[:, 0:D], x1b[par][:, b, :], ALU.add
                                      ).then_inc(N["x2_set"], 1)
                return piece

            def e0(g):
                par = g[1]
                dve.wait_ge(N["x2_set"], upto(g, GROUP))
                norm_stats(x2[par], st3, mv3, ve3, N["stats3"], N["aggr3"], N["veps3"], g)

            def e1(g):
                par = g[1]
                dve.wait_ge(N["rstd3"], upto(g, 1))
                dve.tensor_tensor(rr3[:, :], rs3[:, :], rs3[:, :], ALU.mult).then_inc(N["rr3_set"], 1)
                dve.wait_ge(N["rr3_set"], upto(g, 2, 1))
                dve.tensor_tensor(rr3[:, :], rr3[:, :], mv3[:, :, 1], ALU.mult).then_inc(N["rr3_set"], 1)
                dve.wait_ge(N["rr3_set"], upto(g, 2, 2))
                dve.tensor_scalar(ve4[:, :], rr3[:, :], EPS, None, ALU.add).then_inc(N["veps4"], 1)
                for b in range(GROUP):
                    op = dve.tensor_scalar(y[:, b, :], x2[par][:, b, :], mv3[:, b, 0:1], rs3[:, b:b + 1],
                                           ALU.subtract, ALU.mult)
                op.then_inc(N["y_set"], 1)

            def e2(g):
                dve.wait_ge(N["y_set"], upto(g, 1))
                dve.wait_ge(N["rstd4"], upto(g, 1))
                for b in range(GROUP):
                    op = dve.tensor_scalar(rows[g[1]][:, b, 0:D], y[:, b, :], rs4[:, b:b + 1], None, ALU.mult)
                op.then_inc(N["z_set"], 1)

            def then(op, g, step):
                op.then_inc(N["r_step"], 1)
                dve.wait_ge(N["r_step"], upto(g, R_STEPS, step))

            def each(a):
                return a[:, :].unsqueeze(2).to_broadcast([P, GROUP, EXPERTS])

            def by_expert(a):
                return a.rearrange("p (b e) -> p b e", b=GROUP)

            def f0(g):
                logits = by_expert(R[:, 0:GROUP * EXPERTS])
                dve.wait_ge(N["lg_done"], upto(g, 1))
                then(dve.tensor_reduce(r_max[:, :], logits, AX.X, ALU.max), g, 1)
                dve.tensor_tensor(r_diff[:, :, :], logits, each(r_max), ALU.subtract).then_inc(N["r_sub"], 1)

            def f1(g):
                par = g[1]
                dve.wait_ge(N["r_sub"], upto(g, 1))
                then(dve.scalar_tensor_tensor(r_cand[:, :, :], r_diff[:, :, :], 0.0, by_expert(S("order")),
                                              ALU.is_equal, ALU.mult), g, 2)
                then(dve.tensor_reduce(r_val[:, :], r_cand[:, :, :], AX.X, ALU.max), g, 3)
                then(dve.tensor_tensor(hot16[:, :, :], r_cand[:, :, :], each(r_val), ALU.is_equal), g, 4)
                then(dve.tensor_tensor(tiles_before[par][:, 1, :], tiles_before[par][:, 0, :], hot16[:, 0, :],
                                       ALU.add), g, 5)
                dve.tensor_tensor(tiles_before[1 - par][:, 0, :], tiles_before[par][:, 1, :], hot16[:, 1, :],
                                  ALU.add).then_inc(N["hot_set"], 1)

            def f2(g):
                j, par = g
                dve.wait_ge(N["r_expd"], upto(g, 1))
                then(dve.tensor_reduce(r_sum[:, :], r_exp[:, :, :], AX.X, ALU.add), g, 6)
                dve.reciprocal(rows[par][:, :, 2 * D], r_sum[:, :])
                dve.tensor_copy(rows[par][:, :, 2 * D + 1], S("place")[:, bass.ds((2 * j + par) * GROUP, GROUP)])

            def f3(g):
                par = g[1]
                at = GROUP * EXPERTS
                dve.wait_ge(N["rank_done"], upto(g, 1))
                then(dve.tensor_tensor(r_over[:, :, :], by_expert(R[:, 0:at]), by_expert(S("ecap")), ALU.is_ge),
                     g, 7)
                then(dve.scalar_tensor_tensor(r_all[:, :, :], r_over[:, :, :], 2.0 * SLOTS, by_expert(R[:, 0:at]),
                                              ALU.mult, ALU.add), g, 8)
                then(dve.tensor_tensor(r_own[:, :, :], r_all[:, :, :], hot16[:, :, :], ALU.mult), g, 9)
                then(dve.tensor_reduce(r_slot[:, :], r_own[:, :, :], AX.X, ALU.add), g, 10)
                dve.tensor_copy(to_slot[par][:, :], r_slot[:, :]).then_inc(N["idx_set"], 1)

            schedule({"a0": a0, "a1": a1, "a3": a3, "a4": a4, "a45": a45, "a5": a5, "b0": b_mask(0), "b1": b_mask(1),
                      "b4": b4, "b5": b5, "c1": c1, "c2": c2, "c3": c3, "c4": c4,
                      "s00": s(0, 0), "s01": s(0, 1), "s02": s(0, 2), "s03": s(0, 3),
                      "s10": s(1, 0), "s11": s(1, 1), "s12": s(1, 2), "s13": s(1, 3),
                      "m0": m(0), "m1": m(1), "o1": o1(0), "o3": o3(0), "r1": o1(1),
                      "r3": o3(1), "e0": e0, "e1": e1, "e2": e2,
                      "f0": f0, "f1": f1, "f2": f2, "f3": f3}, LOOP_DVE, dve.Fori)

            def expert_rows(j, par):
                if not isinstance(j, int):
                    dve.wait_ge(returned[par], 32 * j)
                dve.wait_ge(side_in[par], 16 * (j + 1))
                dve.tensor_copy(place[par][:, :], side[par][:, :, D + 1])
                dve.wait_ge(N["eo_done"], 2 * j + par + 1)
                for c in range(2):
                    op = dve.scalar_tensor_tensor(e_out[par][:, c, :], (C, M)[par][:, c * D:(c + 1) * D],
                                                  side[par][:, c, D:D + 1], side[par][:, c, 0:D],
                                                  ALU.mult, ALU.add)
                op.then_inc(N["eo_set"], 1)

            expert_rows(0, 0)
            expert_rows(0, 1)
            with dve.Fori(1, EXPERTS // 2) as j:
                expert_rows(j, 0)
                expert_rows(j, 1)


def host_constants():
    s = np.arange(P)
    shape = np.zeros((P, SHAPE_W), np.float32)

    def put(name, value):
        a, b = SHAPE[name]
        shape[:, a:b] = value
    put("reset", (np.arange(T) % CHUNK != 0)[None, :])
    put("causal", s[:, None] <= s[None, :])
    e = np.tile(np.arange(EXPERTS), GROUP)
    put("ecap", (CAPACITY * (e + 1))[None, :])
    put("order", (EXPERTS - e)[None, :])
    put("ebase", (CAPACITY // P * np.arange(EXPERTS))[None, :])
    put("place", s[:, None] * SEQS + np.arange(SEQS)[None, :])
    shape16 = np.zeros((P, SHAPE16_W), np.float32)

    def put16(name, value):
        a, b = SHAPE16[name]
        shape16[:, a:b] = value
    put16("ident", np.eye(P))
    pick = np.zeros((2, 8, PAIRS, PAIRS, KEYS), np.float32)
    for pair in range(PAIRS):
        pick[:, 0:2, pair, pair, :] = 1.0
    put16("pick", pick.reshape(P, PAIRS * KEYS))
    put16("before", s[:, None] < s[None, :])
    put16("ones", 1.0)
    return shape, shape16


def kernel(**inputs):
    import concourse.bacc as bacc
    from concourse.bass_utils import run_bass_kernel_spmd as run

    a = {k: np.asarray(v) for k, v in inputs.items()}
    order = np.arange(D).reshape(PAIRS, 2, DEPTH).transpose(1, 2, 0).reshape(-1)
    by_unit = np.arange(D).reshape(2, 4, 2, DEPTH).transpose(0, 2, 1, 3).reshape(-1)
    col = lambda v: v[:, None]
    early = np.zeros((P, EARLY_W), np.float32)
    late = np.zeros((P, LATE_W), np.float32)

    def put(dst, where, name, value):
        dst[:value.shape[0], where[name][0]:where[name][1]] = value
    put(early, EARLY, "ident", np.eye(P, dtype=np.float32))
    put(early, EARLY, "w1_t", a["L0_attn_gk_w1"].T)
    put(early, EARLY, "w2", a["L0_attn_gk_w2"])
    put(early, EARLY, "b2", col(a["L0_attn_gk_b2"]))
    put(early, EARLY, "bq", col(a["L0_xattn_bq"][order]))
    put(early, EARLY, "bk", col(a["L0_xattn_bk"][order]))
    put(early, EARLY, "bv", col(a["L0_xattn_bv"][by_unit]))
    put(early, EARLY, "gamma", col(a["L0_ffn_ln_gamma"]))
    put(early, EARLY, "beta", col(a["L0_ffn_ln_beta"]))
    put(early, EARLY, "vg", np.concatenate([a["L0_attn_Wv"], a["L0_attn_Wg"]], axis=1))
    put(early, EARLY, "q", a["L0_attn_Wq"])
    put(early, EARLY, "k", a["L0_attn_Wk"])
    put(late, LATE, "wo", a["L0_attn_Wo"].reshape(2, P, D).transpose(1, 0, 2).reshape(P, 2 * D))
    put(late, LATE, "xk", a["L0_xattn_wk"].T[:, order])
    put(late, LATE, "xv", a["L0_xattn_wv"].T)
    put(late, LATE, "xq", a["L0_xattn_wq"].T[:, order])
    put(late, LATE, "xo", a["L0_xattn_wo"].T[by_unit])
    put(late, LATE, "gate", a["L0_ffn_gate_weight"].T)
    put(late, LATE, "gnorm", np.tile(a["L0_attn_g_norm_w"], (P, GLA_HEADS)))
    put(late, LATE, "bo", np.tile(a["L0_xattn_bo"], (P, 1)))
    shape, shape16 = host_constants()
    arrays = {
        "x": a["x"].transpose(1, 0, 2),
        "ctx_t": a["ctx_1024"].transpose(2, 0, 1),
        "early": early, "late": late, "shape": shape, "shape16": shape16,
        "wi": a["L0_ffn_wi"].transpose(1, 0, 2),
        "wo": a["L0_ffn_wo"].reshape(EXPERTS * HT, P, D).transpose(1, 0, 2),
    }
    arrays = {k: np.ascontiguousarray(v) for k, v in arrays.items()}
    nc = bacc.Bacc("TRN2", target_bir_lowering=False, num_devices=1)
    ins = {k: nc.dram_tensor(f"in_{k}", v.shape, mybir.dt.from_np(v.dtype), kind="ExternalInput").ap()
           for k, v in arrays.items()}
    out = nc.dram_tensor("out", (P, SEQS, D), F32, kind="ExternalOutput").ap()
    slots = nc.dram_tensor("slots", (SLOTS, ROW), F32, kind="Internal").ap()
    build(nc, ins["x"], ins["ctx_t"], ins["early"], ins["late"], ins["shape"], ins["shape16"], ins["wi"], ins["wo"],
          out, slots)
    r = run(nc, [{f"in_{k}": v for k, v in arrays.items()}], core_ids=[0])
    return np.ascontiguousarray(r.results[0]["out"].transpose(1, 0, 2))
```
